# Optimizing a Trainium2 kernel written in Bass

```python
import numpy as np
import jax
import jax.numpy as jnp

def _softmax(x, axis=-1):
    return jax.nn.softmax(x, axis=axis)

def _gelu(x):
    return jax.nn.gelu(x, approximate=True)

def _silu(x):
    return jax.nn.silu(x)

def _sigmoid(x):
    return jax.nn.sigmoid(x)

def _layernorm(x, axis=-1, eps=1e-05):
    m = jnp.mean(x, axis=axis, keepdims=True)
    v = jnp.var(x, axis=axis, keepdims=True)
    return (x - m) / jnp.sqrt(v + eps)

def _scatter_add(tgt, idx, src, axis=0):
    return tgt.at[idx].add(src)

def _segment_sum(src, seg, n):
    return jax.ops.segment_sum(src, seg, n)
kernel_name = 'mk_seq_postln_d1_jaxref_r4_95e708'

def setup_inputs(seed: int=0):
    np.random.seed(seed)
    _w = jnp.asarray

    def _L0_attn_setup():
        import jax, jax.numpy as jnp
        import numpy as np
        HIDDEN = 256
        HEADS = 16
        HEAD_DIM = HIDDEN // HEADS
        B, S = (4, 512)
        key = jax.random.key(seed)
        ks = jax.random.split(key, 10)
        scale = 1.0 / np.sqrt(HIDDEN)

        def lin(k):
            return jax.random.uniform(k, (HIDDEN, HIDDEN), jnp.float32, -scale, scale)
        return {'x': jax.random.normal(ks[0], (B, S, HIDDEN), jnp.float32), 'Wq': lin(ks[1]), 'bq': jnp.zeros((HIDDEN,), jnp.float32), 'Wk': lin(ks[2]), 'bk': jnp.zeros((HIDDEN,), jnp.float32), 'Wv': lin(ks[3]), 'bv': jnp.zeros((HIDDEN,), jnp.float32), 'Wo': lin(ks[4]), 'bo': jnp.zeros((HIDDEN,), jnp.float32), 'head_mask': jnp.ones((HEADS,), jnp.float32)}
    _L0_attn_in = _L0_attn_setup()

    def _L0_ffn_setup():
        import jax, jax.numpy as jnp
        import numpy as np
        EMBED = 256
        HEADS = 16
        HEAD_DIM = EMBED // HEADS
        NUM_EXPERTS = 8
        TOP_K = 2
        HIDDEN = (int(2 * (4 * EMBED) / 3) + 63) // 64 * 64
        SEQ = 512
        BATCH = 2
        ROPE_BASE = 10000.0
        EPS = 1e-06

        def _rope_tables(seq_len, dim):
            inv_freq = 1.0 / ROPE_BASE ** (np.arange(0, dim, 2, dtype=np.float32) / dim)
            t = np.arange(seq_len, dtype=np.float32)
            freqs = np.einsum('i,j->ij', t, inv_freq)
            emb = np.concatenate([freqs, freqs], axis=-1)
            return (jnp.asarray(np.cos(emb)), jnp.asarray(np.sin(emb)))

        def _rotate_half(x):
            x1, x2 = jnp.split(x, 2, axis=-1)
            return jnp.concatenate([-x2, x1], axis=-1)

        def _rmsnorm(x, w):
            return x * jax.lax.rsqrt(jnp.mean(x * x, axis=-1, keepdims=True) + EPS) * w

        def _attention(x, wq, wk, wv, wo):
            B, S, _ = x.shape
            q = (x @ wq).reshape(B, S, HEADS, HEAD_DIM).transpose(0, 2, 1, 3)
            k = (x @ wk).reshape(B, S, HEADS, HEAD_DIM).transpose(0, 2, 1, 3)
            v = (x @ wv).reshape(B, S, HEADS, HEAD_DIM).transpose(0, 2, 1, 3)
            cos, sin = _rope_tables(S, HEAD_DIM)
            cos = cos[None, None]
            sin = sin[None, None]
            q = q * cos + _rotate_half(q) * sin
            k = k * cos + _rotate_half(k) * sin
            scale = HEAD_DIM ** (-0.5)
            scores = jnp.einsum('bhqd,bhkd->bhqk', q, k) * scale
            causal = jnp.triu(jnp.ones((S, S), bool), k=1)
            scores = jnp.where(causal, -jnp.inf, scores)
            attn = jax.nn.softmax(scores, axis=-1)
            out = jnp.einsum('bhqk,bhkd->bhqd', attn, v)
            out = out.transpose(0, 2, 1, 3).reshape(B, S, EMBED)
            return out @ wo

        def _moe(x, w_router, wg, wu, wd):
            B, S, E = x.shape
            xf = x.reshape(-1, E)
            logits = xf @ w_router
            probs = jax.nn.softmax(logits, axis=-1)
            topw, topi = jax.lax.top_k(probs, TOP_K)
            topw = topw / jnp.sum(topw, axis=-1, keepdims=True)
            combine = jnp.sum(jax.nn.one_hot(topi, NUM_EXPERTS, dtype=xf.dtype) * topw[..., None], axis=1)
            g = jax.nn.silu(jnp.einsum('td,xdh->txh', xf, wg))
            u = jnp.einsum('td,xdh->txh', xf, wu)
            eo = jnp.einsum('txh,xhd->txd', g * u, wd)
            out = jnp.einsum('txd,tx->td', eo, combine)
            return out.reshape(B, S, E)
        key = jax.random.key(seed)
        ks = jax.random.split(key, 12)
        s = 0.02
        return {'x': jax.random.normal(ks[0], (BATCH, SEQ, EMBED), jnp.float32), 'wq': jax.random.normal(ks[1], (EMBED, EMBED), jnp.float32) * s, 'wk': jax.random.normal(ks[2], (EMBED, EMBED), jnp.float32) * s, 'wv': jax.random.normal(ks[3], (EMBED, EMBED), jnp.float32) * s, 'wo': jax.random.normal(ks[4], (EMBED, EMBED), jnp.float32) * s, 'w_router': jax.random.normal(ks[5], (EMBED, NUM_EXPERTS), jnp.float32) * s, 'wg': jax.random.normal(ks[6], (NUM_EXPERTS, EMBED, HIDDEN), jnp.float32) * s, 'wu': jax.random.normal(ks[7], (NUM_EXPERTS, EMBED, HIDDEN), jnp.float32) * s, 'wd': jax.random.normal(ks[8], (NUM_EXPERTS, HIDDEN, EMBED), jnp.float32) * s, 'g1': jnp.ones((EMBED,), jnp.float32), 'g2': jnp.ones((EMBED,), jnp.float32)}
    _L0_ffn_in = _L0_ffn_setup()
    _d = {'L0_attn_x': _L0_attn_in['x'], 'L0_attn_Wq': _L0_attn_in['Wq'], 'L0_attn_bq': _L0_attn_in['bq'], 'L0_attn_Wk': _L0_attn_in['Wk'], 'L0_attn_bk': _L0_attn_in['bk'], 'L0_attn_Wv': _L0_attn_in['Wv'], 'L0_attn_bv': _L0_attn_in['bv'], 'L0_attn_Wo': _L0_attn_in['Wo'], 'L0_attn_bo': _L0_attn_in['bo'], 'L0_attn_head_mask': _L0_attn_in['head_mask'], 'L0_ffn_wq': _L0_ffn_in['wq'], 'L0_ffn_wk': _L0_ffn_in['wk'], 'L0_ffn_wv': _L0_ffn_in['wv'], 'L0_ffn_wo': _L0_ffn_in['wo'], 'L0_ffn_w_router': _L0_ffn_in['w_router'], 'L0_ffn_wg': _L0_ffn_in['wg'], 'L0_ffn_wu': _L0_ffn_in['wu'], 'L0_ffn_wd': _L0_ffn_in['wd'], 'L0_ffn_g1': _L0_ffn_in['g1'], 'L0_ffn_g2': _L0_ffn_in['g2']}
    _x0 = _d['L0_attn_x']
    _d['L0_attn_x'] = jax.random.normal(jax.random.fold_in(jax.random.key(seed), 1), (8, 512, 256), dtype=_x0.dtype)
    del _x0
    return _d

def reference(L0_attn_x, L0_attn_Wq, L0_attn_bq, L0_attn_Wk, L0_attn_bk, L0_attn_Wv, L0_attn_bv, L0_attn_Wo, L0_attn_bo, L0_attn_head_mask, L0_ffn_wq, L0_ffn_wk, L0_ffn_wv, L0_ffn_wo, L0_ffn_w_router, L0_ffn_wg, L0_ffn_wu, L0_ffn_wd, L0_ffn_g1, L0_ffn_g2):

    def _L0_attn_ref(x, Wq, bq, Wk, bk, Wv, bv, Wo, bo, head_mask):
        import jax, jax.numpy as jnp
        import numpy as np
        HIDDEN = 256
        HEADS = 16
        HEAD_DIM = HIDDEN // HEADS
        B, S = (4, 512)
        b, s, _ = x.shape
        q = (x @ Wq.T + bq).reshape(b, s, HEADS, HEAD_DIM)
        k = (x @ Wk.T + bk).reshape(b, s, HEADS, HEAD_DIM)
        v = (x @ Wv.T + bv).reshape(b, s, HEADS, HEAD_DIM)
        attn = jnp.einsum('bqhd,bkhd->bhqk', q, k) / np.sqrt(HEAD_DIM).astype(np.float32)
        attn = jax.nn.softmax(attn, axis=-1)
        attn = attn * head_mask[None, :, None, None]
        out = jnp.einsum('bhqk,bkhd->bqhd', attn, v).reshape(b, s, HIDDEN)
        return out @ Wo.T + bo

    def _L0_ffn_ref(x, wq, wk, wv, wo, w_router, wg, wu, wd, g1, g2):
        import jax, jax.numpy as jnp
        import numpy as np
        EMBED = 256
        HEADS = 16
        HEAD_DIM = EMBED // HEADS
        NUM_EXPERTS = 8
        TOP_K = 2
        HIDDEN = (int(2 * (4 * EMBED) / 3) + 63) // 64 * 64
        SEQ = 512
        BATCH = 2
        ROPE_BASE = 10000.0
        EPS = 1e-06

        def _rope_tables(seq_len, dim):
            inv_freq = 1.0 / ROPE_BASE ** (np.arange(0, dim, 2, dtype=np.float32) / dim)
            t = np.arange(seq_len, dtype=np.float32)
            freqs = np.einsum('i,j->ij', t, inv_freq)
            emb = np.concatenate([freqs, freqs], axis=-1)
            return (jnp.asarray(np.cos(emb)), jnp.asarray(np.sin(emb)))

        def _rotate_half(x):
            x1, x2 = jnp.split(x, 2, axis=-1)
            return jnp.concatenate([-x2, x1], axis=-1)

        def _rmsnorm(x, w):
            return x * jax.lax.rsqrt(jnp.mean(x * x, axis=-1, keepdims=True) + EPS) * w

        def _attention(x, wq, wk, wv, wo):
            B, S, _ = x.shape
            q = (x @ wq).reshape(B, S, HEADS, HEAD_DIM).transpose(0, 2, 1, 3)
            k = (x @ wk).reshape(B, S, HEADS, HEAD_DIM).transpose(0, 2, 1, 3)
            v = (x @ wv).reshape(B, S, HEADS, HEAD_DIM).transpose(0, 2, 1, 3)
            cos, sin = _rope_tables(S, HEAD_DIM)
            cos = cos[None, None]
            sin = sin[None, None]
            q = q * cos + _rotate_half(q) * sin
            k = k * cos + _rotate_half(k) * sin
            scale = HEAD_DIM ** (-0.5)
            scores = jnp.einsum('bhqd,bhkd->bhqk', q, k) * scale
            causal = jnp.triu(jnp.ones((S, S), bool), k=1)
            scores = jnp.where(causal, -jnp.inf, scores)
            attn = jax.nn.softmax(scores, axis=-1)
            out = jnp.einsum('bhqk,bhkd->bhqd', attn, v)
            out = out.transpose(0, 2, 1, 3).reshape(B, S, EMBED)
            return out @ wo

        def _moe(x, w_router, wg, wu, wd):
            B, S, E = x.shape
            xf = x.reshape(-1, E)
            logits = xf @ w_router
            probs = jax.nn.softmax(logits, axis=-1)
            topw, topi = jax.lax.top_k(probs, TOP_K)
            topw = topw / jnp.sum(topw, axis=-1, keepdims=True)
            combine = jnp.sum(jax.nn.one_hot(topi, NUM_EXPERTS, dtype=xf.dtype) * topw[..., None], axis=1)
            g = jax.nn.silu(jnp.einsum('td,xdh->txh', xf, wg))
            u = jnp.einsum('td,xdh->txh', xf, wu)
            eo = jnp.einsum('txh,xhd->txd', g * u, wd)
            out = jnp.einsum('txd,tx->td', eo, combine)
            return out.reshape(B, S, E)
        h = x + _attention(_rmsnorm(x, g1), wq, wk, wv, wo)
        y = h + _moe(_rmsnorm(h, g2), w_router, wg, wu, wd)
        return y
    x = L0_attn_x
    x = _layernorm(x + _L0_attn_ref(x, L0_attn_Wq, L0_attn_bq, L0_attn_Wk, L0_attn_bk, L0_attn_Wv, L0_attn_bv, L0_attn_Wo, L0_attn_bo, L0_attn_head_mask), axis=-1)
    x = _layernorm(x + _L0_ffn_ref(x, L0_ffn_wq, L0_ffn_wk, L0_ffn_wv, L0_ffn_wo, L0_ffn_w_router, L0_ffn_wg, L0_ffn_wu, L0_ffn_wd, L0_ffn_g1, L0_ffn_g2), axis=-1)
    return x

_drawn_inputs = setup_inputs


def setup_inputs(seed=0):
    import zlib

    import numpy as np

    out = dict(_drawn_inputs(seed))
    spreads = {'L0_attn_bq': (0.0, 0.8),
     'L0_attn_bk': (0.0, 0.8),
     'L0_attn_bv': (0.0, 0.1),
     'L0_attn_bo': (0.0, 0.1),
     'L0_ffn_g1': (1.0, 0.6),
     'L0_ffn_g2': (1.0, 0.6)}
    factors = {'L0_attn_Wq': 6.481,
     'L0_attn_Wk': 6.233,
     'L0_attn_Wv': 3.306,
     'L0_ffn_wq': 8.0,
     'L0_ffn_wk': 8.0,
     'L0_ffn_wv': 6.711,
     'L0_ffn_wo': 6.718,
     'L0_ffn_w_router': 5.882,
     'L0_ffn_wg': 5.284,
     'L0_ffn_wu': 5.218,
     'L0_ffn_wd': 5.212}
    for name, (base, spread) in spreads.items():
        noise = np.random.default_rng([zlib.crc32(name.encode()), seed]).standard_normal(out[name].shape)
        drawn = base * np.exp(spread * noise) if base else spread * noise
        out[name] = jnp.asarray(drawn.astype(out[name].dtype))
    for name, factor in factors.items():
        out[name] = (out[name] * factor).astype(out[name].dtype)
    return out
```

```python
from contextlib import ExitStack, contextmanager

import numpy as np
import concourse.bass as bass
from concourse import mybir

ALU = mybir.AluOpType
ACT = mybir.ActivationFunctionType
AX = mybir.AxisListType
F32 = mybir.dt.float32
F16 = mybir.dt.float16
BF16 = mybir.dt.bfloat16
I32 = mybir.dt.int32
U32 = mybir.dt.uint32
ds = bass.ds

P = 128
B, S, D = 8, 512, 256
H, DH = 16, 16
T = B * S
QT = S // P
NT = T // P
KD = D // P
G, HG = 4, 4
E, F = 8, 704
FT = (F + P - 1) // P
FR = F - (FT - 1) * P
SLOT = 256
MT = 2 * T // SLOT + E
LN_EPS, RMS_EPS = 1e-5, 1e-6
MAXROW = P - 2
NEG = -1.0e30


class Tensors:
    pass


@contextmanager
def stage_semaphores(nc, prefix):
    handles = []

    def sem(name):
        handles.append(nc.alloc_semaphore(name=prefix + name))
        return handles[-1]

    yield sem
    nc.clear_and_free_semaphores(handles)
    nc.all_engine_barrier()


def setup(nc, t, w_in, router_in, vec_in):
    with ExitStack() as ctx:
        sem = ctx.enter_context(stage_semaphores(nc, ""))
        w32 = ctx.enter_context(nc.sbuf_tensor("w32", [P, 8, KD, D], F32))
        r32 = ctx.enter_context(nc.sbuf_tensor("r32", [P, KD, E], F32))
        scale = ctx.enter_context(nc.sbuf_tensor("w_scale", [P, 8, KD], F32))
        loaded, filled, scaled, split_hi, split_lo = (
            sem("setup_loaded"), sem("setup_filled"), sem("weight_scale_ready"), sem("weights_hi"), sem("weights_lo"))
        block = ctx.enter_context(nc.Block())

        @block.sync
        def _(sync):
            n = 0
            for j, w in enumerate(w_in):
                sync.dma_start(w32[:, j], w.rearrange("(k p) n -> p k n", p=P)).then_inc(loaded, 16)
                n += 16
            for dst, src in vec_in:
                sync.dma_start(dst, src).then_inc(loaded, 16)
                n += 16
            sync.dma_start(r32[:], router_in.rearrange("(k p) n -> p k n", p=P)).then_inc(loaded, 16)
            sync.wait_ge(loaded, n + 16)
            sync.wait_ge(split_lo, 9 * KD)

        n_dma = 16 * (len(w_in) + len(vec_in) + 1)

        @block.gpsimd
        def _(pool):
            pool.memset(t.ident32[:], 0.0).then_inc(filled, 1)
            pool.memset(t.mask_kq[:], 0.0).then_inc(filled, 1)
            pool.wait_ge(filled, 2)
            pool.affine_select(out=t.ident32[:], in_=t.ident32[:], pattern=[[-1, P]], compare_op=ALU.not_equal,
                               fill=1.0, base=0, channel_multiplier=1).then_inc(filled, 1)
            pool.affine_select(out=t.mask_qk[:], in_=t.mask_kq[:], pattern=[[-1, P]], compare_op=ALU.is_ge,
                               fill=NEG, base=0, channel_multiplier=1).then_inc(filled, 1)
            pool.wait_ge(filled, 4)
            pool.affine_select(out=t.mask_kq[:], in_=t.mask_kq[:], pattern=[[1, P]], compare_op=ALU.is_ge,
                               fill=NEG, base=0, channel_multiplier=-1).then_inc(filled, 1)
            pool.tensor_copy(t.ident16[:], t.ident32[:]).then_inc(filled, 1)
            pool.tensor_copy(t.ident_bf[:], t.ident32[:]).then_inc(filled, 1)
            pool.wait_ge(filled, 7)

        @block.vector
        def _(vector):
            vector.memset(scale[:], 1.0).then_inc(scaled, 1)
            vector.wait_ge(scaled, 1)
            vector.memset(scale[:, 0], DH ** -0.5).then_inc(scaled, 1)
            vector.wait_ge(loaded, n_dma)
            vector.tensor_scalar(scale[:, 4], t.g1[:], DH ** -0.5, None, ALU.mult).then_inc(scaled, 1)
            for j in (5, 6):
                vector.tensor_copy(scale[:, j], t.g1[:]).then_inc(scaled, 1)
            vector.tensor_scalar(t.bq[:], t.bq[:], DH ** -0.5, None, ALU.mult).then_inc(scaled, 1)
            vector.wait_ge(scaled, 6)
            for j in range(8):
                for k in range(KD):
                    n = j * KD + k + 1
                    vector.wait_ge(split_hi, n)
                    vector.scalar_tensor_tensor(t.w_proj[:, j, 1, k], w32[:, j, k], scale[:, j, k:k + 1],
                                                t.w_proj[:, j, 0, k], ALU.mult, ALU.subtract).then_inc(split_lo, 1)
            for k in range(KD):
                vector.wait_ge(split_hi, 8 * KD + k + 1)
                vector.scalar_tensor_tensor(t.w_router[:, 1, k], r32[:, k], t.g2[:, k:k + 1],
                                            t.w_router[:, 0, k], ALU.mult, ALU.subtract).then_inc(split_lo, 1)

        @block.scalar
        def _(act):
            act.wait_ge(loaded, n_dma)
            act.wait_ge(scaled, 6)
            for j in range(8):
                for k in range(KD):
                    act.activation(t.w_proj[:, j, 0, k], w32[:, j, k], ACT.Copy,
                                   scale=scale[:, j, k:k + 1]).then_inc(split_hi, 1)
            for k in range(KD):
                act.activation(t.w_router[:, 0, k], r32[:, k], ACT.Copy, scale=t.g2[:, k:k + 1]).then_inc(split_hi, 1)


def project_qkv(nc, t, layer, x_dram):
    rope = layer == 1
    with ExitStack() as ctx:
        L = f"l{layer}_"
        sem = ctx.enter_context(stage_semaphores(nc, L))
        pair = lambda n: [sem(f"{n}{i}") for i in range(2)]
        sb = lambda n, s, d: ctx.enter_context(nc.sbuf_tensor(L + n, s, d))
        ps = lambda n, s, d: ctx.enter_context(nc.psum_tensor(L + n, s, d))
        x_in = sb("x_in", [P, 2, QT, 2 * D] if rope else [P, 2, KD, S], F16 if rope else F32)
        xT = sb("xT", [P, 2, 2, KD, S], F16)
        qk = sb("qk", [P, 2, 4, 2, S], F16)
        v = sb("v", [P, 2, QT, D], F32)
        ps_qk = ps("ps_qk", [P, 2, S], F32)
        ps_v = ps("ps_v", [P, 2, 2, D], F32)
        if rope:
            q32 = sb("q32", [P, 2, S], F32)
            q_cos = sb("q_cos", [P, 2, S], F32)
            q_sin = sb("q_sin", [P, 2, S], F32)
            q_rot = sb("q_rot", [P, 2, S], F32)
            ps_rot = ps("ps_rot", [P, 2, S], F32)
            ps_xT = ps("ps_xT", [P, 2, KD, S], F16)
        x_loaded, stored, xT_mm, xT_hi, xT_lo, v_mm, v_out = map(pair, (
            "x_loaded", "stored", "xT_mm", "xT_hi", "xT_lo", "v_mm", "v_out"))
        qk_mm, qk_hi, qk_lo, q32_out, rot_mm, cos_out, sin_out, rot_out = map(pair, (
            "qk_mm", "qk_hi", "qk_lo", "q32_out", "rot_mm", "cos_out", "sin_out", "rot_out"))
        block = ctx.enter_context(nc.Block())
        STORES = 3 * 16

        def done(b, c):
            return b * 2 + (c // 2 + 1)

        def free(b, c):
            return b * 2 + c // 2

        @block.sync
        def _(sync):
            def load(b, s):
                sync.dma_start(x_in[:, s], x_dram(b)).then_inc(x_loaded[s], 16)

            def store(b, s):
                for c in (2, 3):
                    sync.wait_ge(qk_hi[c % 2], done(b, c))
                    sync.wait_ge(qk_lo[c % 2], done(b, c))
                for hl in range(2):
                    sync.dma_start(t.qk_dram[hl][:, :, ds(b * S, S)], qk[:, s, :, hl, :]).then_inc(stored[s], 16)

            def store_v(b, r, s):
                sync.wait_ge(v_out[s], r * 2 + 2)
                sync.dma_start(t.v_dram.rearrange("(k p) n -> p k n", p=P)[:, ds(b * QT, QT), :],
                               v[:, s]).then_inc(stored[s], 16)

            load(0, 0)
            load(1, 1)
            with sync.Fori(0, B // 2 - 1) as r:
                for s in range(2):
                    sync.wait_ge(xT_hi[s], r + 1)
                    sync.wait_ge(xT_lo[s], r + 1)
                    load(r * 2 + (2 + s), s)
                    store(r * 2 + s, s)
                    store_v(r * 2 + s, r, s)
            for s in range(2):
                store(B - 2 + s, s)
                store_v(B - 2 + s, B // 2 - 1, s)
            for s in range(2):
                sync.wait_ge(stored[s], STORES * (B // 2))

        @block.tensor
        def _(pe):
            def transpose_x(r, s):
                pe.wait_ge(x_loaded[s], r * 16 + 16)
                o = 1 - s
                pe.wait_ge(xT_hi[o], r + s)
                pe.wait_ge(xT_lo[o], r + s)
                for hl in range(2):
                    for k in range(KD):
                        for q in range(QT):
                            mm = pe.transpose(ps_xT[:, hl, k, q * P:(q + 1) * P],
                                              x_in[:, s, q, hl * D + k * P:hl * D + (k + 1) * P], t.ident16[:])
                mm.then_inc(xT_mm[s], 1)

            def rotate(b, c):
                pe.wait_ge(q32_out[c % 2], done(b, c))
                pe.wait_ge(sin_out[c % 2], free(b, c))
                pe.matmul(ps_rot[:, c % 2], t.rot[:], q32[:, c % 2], start=True, stop=True).then_inc(rot_mm[c % 2], 1)

            with pe.Fori(0, B // 2) as r:
                for s in range(2):
                    b = r * 2 + s
                    if rope:
                        transpose_x(r, s)
                    pe.wait_ge(xT_hi[s], r + 1)
                    pe.wait_ge(xT_lo[s], r + 1)
                    for c in range(4):
                        w, m = c // 2, c % 2
                        for read in ([q32_out] if rope else [qk_hi, qk_lo]):
                            pe.wait_ge(read[c % 2], free(b, c))
                        n = 0
                        for wh, xh in ((0, 0), (0, 1), (1, 0)):
                            for k in range(KD):
                                mm = pe.matmul(ps_qk[:, c % 2], t.w_proj[:, 4 * layer + w, wh, k, m * P:(m + 1) * P],
                                               xT[:, s, xh, k, :], start=n == 0, stop=n == 5)
                                n += 1
                        mm.then_inc(qk_mm[c % 2], 1)
                        if rope and c >= 1:
                            rotate(b, c - 1)
                    for u in range(2):
                        pe.wait_ge(v_out[1 - s], (r + s) * 2)
                        for j in range(2):
                            n, q = 0, 2 * u + j
                            for wh, xh in ((0, 0), (1, 0), (0, 1)):
                                for k in range(KD):
                                    mm = pe.matmul(ps_v[:, u, j], xT[:, s, xh, k, q * P:(q + 1) * P],
                                                   t.w_proj[:, 4 * layer + 2, wh, k, :], start=n == 0, stop=n == 5)
                                    n += 1
                        mm.then_inc(v_mm[s], 1)
                    if rope:
                        rotate(b, 3)

        @block.scalar
        def _(act):
            def high(b, s, c):
                act.wait_ge(rot_out[c % 2], done(b, c))
                act.activation(qk[:, s, c, 0], q_rot[:, c % 2], ACT.Copy).then_inc(qk_hi[c % 2], 1)

            with act.Fori(0, B // 2) as r:
                for s in range(2):
                    b = r * 2 + s
                    if rope:
                        act.wait_ge(xT_mm[s], r + 1)
                    else:
                        act.wait_ge(x_loaded[s], r * 16 + 16)
                    act.wait_ge(v_mm[s], r * 2)
                    src = ps_xT[:, 0] if rope else x_in[:, s]
                    act.activation(xT[:, s, 0], src, ACT.Copy).then_inc(xT_hi[s], 1)
                    act.wait_ge(stored[s], r * STORES)
                    for c in range(4):
                        act.wait_ge(qk_mm[c % 2], done(b, c))
                        if rope:
                            act.wait_ge(rot_mm[c % 2], free(b, c))
                            act.wait_ge(cos_out[c % 2], free(b, c))
                            act.activation(q32[:, c % 2], ps_qk[:, c % 2], ACT.Copy).then_inc(q32_out[c % 2], 1)
                            if c >= 1:
                                high(b, s, c - 1)
                        else:
                            bias = (t.bq if c < 2 else t.bk)[:, c % 2:c % 2 + 1]
                            act.activation(qk[:, s, c, 0], ps_qk[:, c % 2], ACT.Identity,
                                           bias=bias).then_inc(qk_hi[c % 2], 1)
                    if rope:
                        high(b, s, 3)

        @block.vector
        def _(vector):
            with vector.Fori(0, B // 2) as r:
                for s in range(2):
                    b = r * 2 + s
                    vector.wait_ge(xT_hi[s], r + 1)
                    if rope:
                        vector.tensor_copy(xT[:, s, 1], ps_xT[:, 1]).then_inc(xT_lo[s], 1)
                    else:
                        vector.tensor_tensor(xT[:, s, 1], x_in[:, s], xT[:, s, 0], ALU.subtract).then_inc(xT_lo[s], 1)
                    vector.wait_ge(stored[s], r * STORES)
                    for c in range(4):
                        if rope:
                            vector.wait_ge(rot_mm[c % 2], done(b, c))
                            vector.wait_ge(rot_out[c % 2], free(b, c))
                            vector.tensor_tensor(q_sin[:, c % 2], ps_rot[:, c % 2], t.sin[:],
                                                 ALU.mult).then_inc(sin_out[c % 2], 1)
                        else:
                            bias = (t.bq if c < 2 else t.bk)[:, c % 2:c % 2 + 1]
                            vector.wait_ge(qk_hi[c % 2], done(b, c))
                            vector.scalar_tensor_tensor(qk[:, s, c, 1], ps_qk[:, c % 2], bias, qk[:, s, c, 0],
                                                        ALU.add, ALU.subtract).then_inc(qk_lo[c % 2], 1)
                    for u in range(2):
                        vector.wait_ge(v_mm[s], r * 2 + (u + 1))
                        if rope:
                            vector.tensor_copy(v[:, s, 2 * u:2 * u + 2], ps_v[:, u]).then_inc(v_out[s], 1)
                        else:
                            vector.tensor_tensor(v[:, s, 2 * u:2 * u + 2], ps_v[:, u], t.bv2[:],
                                                 ALU.add).then_inc(v_out[s], 1)

        if rope:
            @block.gpsimd
            def _(pool):
                with pool.Fori(0, B // 2) as r:
                    for s in range(2):
                        b = r * 2 + s
                        pool.wait_ge(stored[s], r * STORES)
                        for c in range(4):
                            i = c % 2
                            pool.wait_ge(q32_out[i], done(b, c))
                            pool.wait_ge(rot_out[i], free(b, c))
                            pool.tensor_tensor(q_cos[:, i], q32[:, i], t.cos[:], ALU.mult).then_inc(cos_out[i], 1)
                            pool.wait_ge(sin_out[i], done(b, c))
                            pool.wait_ge(cos_out[i], done(b, c))
                            pool.wait_ge(qk_hi[i], free(b, c))
                            pool.wait_ge(qk_lo[i], free(b, c))
                            pool.tensor_tensor(q_rot[:, i], q_cos[:, i], q_sin[:, i], ALU.add).then_inc(rot_out[i], 1)
                            pool.wait_ge(qk_hi[i], done(b, c))
                            pool.tensor_tensor(qk[:, s, c, 1], q_rot[:, i], qk[:, s, c, 0],
                                               ALU.subtract).then_inc(qk_lo[i], 1)


def attend(nc, t, layer):
    causal = layer == 1
    width = lambda kt: S - kt * P if causal else S
    keys = lambda q: (q + 1) * P if causal else S
    at = lambda kt: 0 if kt % 2 == 0 else width(kt - 1)
    with ExitStack() as ctx:
        L = f"a{layer}_"
        sem = ctx.enter_context(stage_semaphores(nc, L))
        several = lambda n, k: [sem(f"{n}{i}") for i in range(k)]
        sb = lambda n, s, d: ctx.enter_context(nc.sbuf_tensor(L + n, s, d))
        ps = lambda n, s, d: ctx.enter_context(nc.psum_tensor(L + n, s, d))
        qx = sb("qx", [P, G, HG, S], F16)
        kx = sb("kx", [P, G, HG, S], F16)
        v_in = sb("v_in", [P, G, QT, HG * DH], F32)
        v_one = sb("v_one", [P, G, QT, HG, 32], F32)
        probs = sb("probs", [P, 2, HG, 2 * S], F32)
        neg_max = sb("neg_max", [P, G, QT, HG], F32)
        rows = sb("rows", [HG, 2, 2, S], F16)
        o32 = sb("o32", [P, S], F32)
        inv = sb("inv", [P, 2, QT, HG], F32)
        ps_s = ps("ps_s", [P, 2, 2 * S], F32)
        ps_m = ps("ps_m", [P, 2, S], F32)
        ps_o = ps("ps_o", [P, S], F32)
        ps_x = ps("ps_x", [P, S], F32)
        filled = sem("filled")
        qk_loaded, v_loaded, rows_loaded, v_copied, group_done = (
            several(n, G) for n in ("qk_loaded", "v_loaded", "rows_loaded", "v_copied", "group_done"))
        scores_mm = sem("scores_mm")
        exp_out, max_out = several("exp_out", 2), several("max_out", 2)
        half_done = sem("half_done")
        max_mm, rows_mm, rows_hi, rows_lo = sem("max_mm"), sem("rows_mm"), sem("rows_hi"), sem("rows_lo")
        o_out, back_mm, inv_out, norm_out = sem("o_out"), sem("back_mm"), sem("inv_out"), sem("norm_out")
        block = ctx.enter_context(nc.Block())

        def ahead(b, g, n):
            return b + (g + n) // G, (g + n) % G

        def steps(engine, step):
            for g in range(G):
                step(0, g, first=g == 0)
            with engine.Fori(1, B - 1) as b:
                for g in range(G):
                    step(b, g)
            for g in range(G):
                step(B - 1, g, maxima=g + 2 < G, has_next=g + 1 < G)

        @block.sync
        def _(sync):
            def load(b, g):
                for part, x, c0, terms in ((0, qx, 0, (0, 0, 1)), (1, kx, 2, (0, 1, 0))):
                    for n, hl in enumerate(terms):
                        c, p0 = c0 + g // 2, (g % 2) * HG * DH
                        src = t.qk_dram[hl][p0:p0 + HG * DH, c, ds(b * S, S)].rearrange("(h d) n -> d h n", d=DH)
                        sync.dma_start(x[n * DH:(n + 1) * DH, g], src).then_inc(qk_loaded[g], 16)
                sync.dma_start(v_in[:, g], t.v_dram.rearrange("(k p) n -> p k n", p=P)[
                    :, ds(b * QT, QT), g * HG * DH:(g + 1) * HG * DH]).then_inc(v_loaded[g], 16)

            def load_rows(b, g, n):
                sync.wait_ge(rows_hi, n)
                sync.wait_ge(rows_lo, n)
                for hl in range(2):
                    sync.dma_start(qx[MAXROW + hl:MAXROW + hl + 1, g], rows[0:HG, g % 2, hl]
                                   ).then_inc(rows_loaded[g], 16)

            def step(b, g, first=False, maxima=True, has_next=True):
                if has_next:
                    load_rows(*ahead(b, g, 1), b * G + (g + 2))
                if not (isinstance(b, int) and b == B - 1):
                    scored, copied = counted(sync, b * (8 * G) + 8 * (g + 1)), counted(sync, b + 1)
                    sync.wait_ge(scores_mm, scored)
                    sync.wait_ge(v_copied[g], copied)
                    load(b + 1, g)

            sync.wait_ge(filled, 3)
            for g in range(G):
                load(0, g)
            load_rows(0, 0, 1)
            steps(sync, step)

        @block.gpsimd
        def _(pool):
            pool.memset(qx[:], 0.0).then_inc(filled, 1)
            pool.memset(kx[:], 1.0).then_inc(filled, 1)
            pool.memset(v_one[:], 1.0)
            pool.wait_ge(filled, 2)
            kf = kx[:].rearrange("p g h n -> p (g h n)")
            pool.affine_select(out=kf, in_=kf, pattern=[[0, G * HG * S]], compare_op=ALU.is_ge, fill=0.0,
                               base=-MAXROW, channel_multiplier=1).then_inc(filled, 1)

            def copy_v(b, g):
                loads = counted(pool, b * 16 + 16)
                pool.wait_ge(filled, 3)
                pool.wait_ge(v_loaded[g], loads)
                pool.wait_ge(group_done[g], b)
                pool.tensor_copy(v_one[:, g, :, :, 0:DH],
                                 v_in[:, g].rearrange("p k (h d) -> p k h d", h=HG)).then_inc(v_copied[g], 1)

            with pool.Fori(0, B) as b:
                for g in range(G):
                    copy_v(b, g)

        @block.tensor
        def _(pe):
            def scores(b, g, kp, j):
                c = kp * HG + j
                if c == 0:
                    pe.wait_ge(rows_loaded[g], b * 32 + 32)
                pe.wait_ge(exp_out[c % 2], b * (4 * G) + (4 * g + c // 2))
                for kt in (2 * kp, 2 * kp + 1):
                    out = ps_s[:, c % 2, at(kt):at(kt) + width(kt)]
                    mm = pe.matmul(out, kx[:, g, j, kt * P:(kt + 1) * P], qx[:, g, j, S - width(kt):S],
                                   start=True, stop=not causal)
                    if causal:
                        mm = pe.matmul(ps_s[:, c % 2, at(kt):at(kt) + P], t.ident_bf[:], t.mask_kq[:],
                                       start=False, stop=True)
                mm.then_inc(scores_mm, 1)

            def maxima_of(b, g, c):
                j, q = c // QT, c % QT
                if c == 0:
                    pe.wait_ge(qk_loaded[g], b * 96 + 96)
                pe.wait_ge(max_out[c % 2], b * (8 * G) + (8 * g + c // 2))
                mm = pe.matmul(ps_m[:, c % 2, 0:keys(q)], qx[0:MAXROW, g, j, q * P:(q + 1) * P],
                               kx[0:MAXROW, g, j, 0:keys(q)], start=True, stop=not causal)
                if causal:
                    mm = pe.matmul(ps_m[:, c % 2, q * P:(q + 1) * P], t.ident_bf[:], t.mask_qk[:],
                                   start=False, stop=True)
                mm.then_inc(max_mm, 1)

            def turn_maxima(b, g, n):
                for i in range(2):
                    pe.wait_ge(max_out[i], n * 8 + 8)
                pe.wait_ge(norm_out, max(n - 2, 0) if isinstance(n, int) else n - 2)
                for q in range(QT):
                    mm = pe.transpose(ps_x[0:HG, q * P:(q + 1) * P], neg_max[:, g, q, :], t.ident32[:])
                mm.then_inc(rows_mm, 1)

            def weigh(b, g, kt):
                n = b * G + g
                if kt % 2 == 0:
                    for i in range(2):
                        pe.wait_ge(exp_out[i], n * 4 + (kt + 2))
                if kt == 0:
                    pe.wait_ge(v_copied[g], b + 1)
                    pe.wait_ge(o_out, n)
                for j in range(HG):
                    mm = pe.matmul(ps_o[32 * j:32 * (j + 1), S - width(kt):S], v_one[:, g, kt, j, :],
                                   probs[:, kt // 2, j, at(kt):at(kt) + width(kt)],
                                   start=kt == 0, stop=kt == QT - 1)
                if kt == 1:
                    mm.then_inc(half_done, 1)
                elif kt == QT - 1:
                    mm.then_inc(group_done[g], 1)

            def turn_back(b, g):
                n = b * G + g
                pe.wait_ge(o_out, n + 1)
                turned = min(n + 3, B * G) if isinstance(n, int) else n + 3
                pe.wait_ge(rows_hi, turned)
                pe.wait_ge(rows_lo, turned)
                pe.wait_ge(norm_out, n)
                for q in range(QT):
                    mm = pe.transpose(ps_x[:, q * P:(q + 1) * P], o32[:, q * P:(q + 1) * P], t.ident32[:])
                mm.then_inc(back_mm, 1)

            def step(b, g, first=False, maxima=True, has_next=True):
                def a_maximum(c):
                    if maxima:
                        maxima_of(*ahead(b, g, 2), c)

                for half, kt in enumerate((2, 3, 0, 1)):
                    kp, j = half // 2, half % 2 * 2
                    a_maximum(4 * half)
                    scores(b, g, kp, j)
                    if half == 0 and has_next:
                        turn_maxima(*ahead(b, g, 1), b * G + (g + 1))
                    a_maximum(4 * half + 1)
                    scores(b, g, kp, j + 1)
                    a_maximum(4 * half + 2)
                    if half >= 2:
                        weigh(b, g, kt)
                    elif not first:
                        weigh(*ahead(b, g, -1), kt)
                    a_maximum(4 * half + 3)
                    if half == 2 and not first:
                        turn_back(*ahead(b, g, -1))

            pe.wait_ge(filled, 3)
            for g in range(2):
                for c in range(HG * QT):
                    maxima_of(0, g, c)
                if g == 0:
                    turn_maxima(0, 0, 0)
            steps(pe, step)
            weigh(B - 1, G - 1, 2)
            weigh(B - 1, G - 1, 3)
            turn_back(B - 1, G - 1)

        @block.scalar
        def _(act):
            def exponentials(b, g, kp, j, first):
                n, c = b * G + g, kp * HG + j
                act.wait_ge(scores_mm, n * 8 + (c + 1))
                if j == 0:
                    if kp == 0:
                        act.wait_ge(half_done, n)
                    elif not first:
                        before, of = ahead(b, g, -1)
                        act.wait_ge(group_done[of], before + 1)
                w = width(2 * kp) + width(2 * kp + 1)
                act.activation(probs[:, kp, j, 0:w], ps_s[:, c % 2, 0:w], ACT.Exp).then_inc(exp_out[c % 2], 1)

            def rows_high(b, g, n):
                act.wait_ge(rows_mm, n)
                act.activation(rows[:, g % 2, 0], ps_x[0:HG, :], ACT.Copy).then_inc(rows_hi, 1)

            def empty_o(b, g):
                act.wait_ge(group_done[g], b + 1)
                act.wait_ge(back_mm, b * G + g)
                act.activation(o32[:], ps_o[:], ACT.Copy).then_inc(o_out, 1)

            def step(b, g, first=False, maxima=True, has_next=True):
                for kp in range(2):
                    if kp == 1 and not first:
                        empty_o(*ahead(b, g, -1))
                    for j in range(HG):
                        exponentials(b, g, kp, j, first)
                        if kp == 0 and j == 0 and has_next:
                            rows_high(*ahead(b, g, 1), b * G + (g + 2))

            rows_high(0, 0, 1)
            steps(act, step)
            empty_o(B - 1, G - 1)

        @block.vector
        def _(vector):
            def row_max(b, g, c):
                j, q = c // QT, c % QT
                vector.wait_ge(max_mm, b * (16 * G) + (16 * g + c + 1))
                vector.tensor_reduce(neg_max[:, g, q, j:j + 1], ps_m[:, c % 2, 0:keys(q)], AX.X, ALU.max,
                                     negate=True).then_inc(max_out[c % 2], 1)

            def rows_low(b, g, n):
                vector.wait_ge(rows_hi, n)
                vector.tensor_tensor(rows[:, g % 2, 1], ps_x[0:HG, :], rows[:, g % 2, 0],
                                     ALU.subtract).then_inc(rows_lo, 1)

            def normalise(b, g):
                n = b * G + g
                vector.wait_ge(back_mm, n + 1)
                o = ps_x[:].rearrange("p (q j d) -> p q j d", q=QT, j=HG)
                vector.reciprocal(inv[:, 0], o[:, :, :, DH]).then_inc(inv_out, 1)
                vector.wait_ge(inv_out, n * (1 if causal else 2) + 1)
                scale = inv[:, 0]
                if not causal:
                    mask = t.head_mask[:, g * HG:(g + 1) * HG].rearrange("p (o h) -> p o h", o=1)
                    vector.tensor_tensor(inv[:, 1], inv[:, 0], mask.broadcast_to([P, QT, HG]),
                                         ALU.mult).then_inc(inv_out, 1)
                    vector.wait_ge(inv_out, n * 2 + 2)
                    scale = inv[:, 1]
                out = t.attn[:, ds(b * QT, QT), g * HG * DH:(g + 1) * HG * DH].rearrange(
                    "p q (j d) -> p q j d", j=HG)
                vector.tensor_tensor(out, o[:, :, :, 0:DH],
                                     scale.rearrange("p q (j o) -> p q j o", o=1).broadcast_to([P, QT, HG, DH]),
                                     ALU.mult).then_inc(norm_out, 1)

            def step(b, g, first=False, maxima=True, has_next=True):
                for c in range(16):
                    if c == 4 and has_next:
                        rows_low(*ahead(b, g, 1), b * G + (g + 2))
                    if maxima:
                        row_max(*ahead(b, g, 2), c)
                    if c == 12 and not first:
                        normalise(*ahead(b, g, -1))

            for g in range(2):
                for c in range(16):
                    row_max(0, g, c)
                if g == 0:
                    rows_low(0, 0, 1)
            steps(vector, step)
            normalise(B - 1, G - 1)


def attention_tensors(nc, ctx, t):
    sb = lambda n, s, d: ctx.enter_context(nc.sbuf_tensor(n, s, d))
    t.ident_bf = sb("ident_bf", [P, P], BF16)
    t.mask_kq, t.mask_qk = sb("mask_kq", [P, P], BF16), sb("mask_qk", [P, P], BF16)
    t.rot = sb("rot", [P, P], F32)
    t.cos, t.sin = sb("rope_cos", [P, S], F32), sb("rope_sin", [P, S], F32)
    t.w_proj = sb("w_proj", [P, 8, 2, KD, D], F16)
    t.w_router = sb("w_router_parts", [P, 2, KD, E], F16)
    t.bq, t.bk, t.g1 = sb("bq", [P, KD], F32), sb("bk", [P, KD], F32), sb("g1", [P, KD], F32)
    t.bv2, t.bo = sb("bv2", [P, 2, D], F32), sb("bo", [P, D], F32)
    t.head_mask = sb("head_mask_row", [P, H], F32)
    t.attn = sb("attn", [P, NT, D], F32)


def pipeline(engine, early, late):
    early(0, 0, 0)
    with engine.Fori(0, B // 2 - 1) as r:
        early(r * 2 + 1, 1, r)
        late(r * 2, 0, r)
        early(r * 2 + 2, 0, r + 1)
        late(r * 2 + 1, 1, r)
    early(B - 1, 1, B // 2 - 1)
    late(B - 2, 0, B // 2 - 1)
    late(B - 1, 1, B // 2 - 1)


def counted(engine, value):
    return value if isinstance(value, int) else engine.snap(engine.to_reg(value))


def before_last(b):
    return max(b - 1, 0) if isinstance(b, int) else b - 1


def project_out(nc, t, layer, x_res_dram, x_out_dram, part_dram):
    norm, route = layer == 0, layer == 1
    with ExitStack() as ctx:
        L = f"o{layer}_"
        sem = ctx.enter_context(stage_semaphores(nc, L))
        sb = lambda n, s, d: ctx.enter_context(nc.sbuf_tensor(L + n, s, d))
        ps = lambda n, s, d: ctx.enter_context(nc.psum_tensor(L + n, s, d))
        x_res = sb("x_res", [P, 2, QT, D], F32)
        a_part = sb("a_part", [P, 2, 2, QT, D], F16)
        aT = sb("aT", [P, 2, 2, KD, S], F16)
        x_new = sb("x_new", [P, 2, QT, D], F32)
        x_out = sb("x_out", [P, 2, QT, D], F32) if norm else x_new
        stats, mean_var = sb("stats", [P, 2, QT, 6], F32), sb("mean_var", [P, 2, QT, 2], F32)
        squares = sb("squares", [P, 2, QT, D], F32)
        small = sb("small", [P, 4, QT], F32)
        ms = sb("ms", [P, 2, QT], F32)
        constants = sb("constants", [P, 3, QT], F32)
        part = sb("part", [P, 2, QT, 2, D], F16)
        ps_aT = ps("ps_aT", [P, 2, KD, S], F16)
        ps_y = ps("ps_y", [P, 2, 2, D], F32)
        loaded, stored = [[sem(f"{n}{i}") for i in range(2)] for n in ("loaded", "stored")]
        a_hi, a_lo, aT_mm, aT_hi, aT_lo = map(sem, (
            "a_hi", "a_lo", "aT_mm", "aT_hi", "aT_lo"))
        y_mm, biased, summed, aggregated, var_out, rstd_out, x_done = map(sem, (
            "y_mm", "biased", "summed", "aggregated", "var_out", "rstd_out", "x_done"))
        squared, ms_out, rms_out, part_hi, part_lo, power, stat_out = map(sem, (
            "squared", "ms_out", "rms_out", "part_hi", "part_lo", "power", "stat_out"))
        if route:
            x_sum = sb("x_sum", [P, 2, QT, D], F32)
            nT = sb("nT", [P, 2, KD, S], F16)
            ps_nT = ps("ps_nT", [P, 2, KD, S], F16)
            ps_l = ps("ps_l", [P, QT, E], F32)
            nT_mm, nT_hi, nT_lo, logits_mm, logits_out, added = map(sem, (
                "nT_mm", "nT_hi", "nT_lo", "logits_mm", "logits_out", "added"))
        block = ctx.enter_context(nc.Block())
        tiles = lambda x: x.rearrange("(k p) n -> p k n", p=P)

        def wait_x(engine, b, q):
            if norm:
                engine.wait_ge(x_done, b * QT + (q + 1))
            else:
                engine.wait_ge(summed, b * 2 + (q // 2 + 1))

        @block.sync
        def _(sync):
            def early(b, s, k):
                sync.wait_ge(summed if norm else added, before_last(b) * (2 if norm else 1))
                sync.dma_start(x_res[:, s], tiles(x_res_dram)[:, ds(b * QT, QT), :]).then_inc(loaded[s], 16)

            def late(b, s, k):
                if norm:
                    sync.wait_ge(x_done, b * QT + QT)
                else:
                    sync.wait_ge(added, b + 1)
                sync.dma_start(tiles(x_out_dram)[:, ds(b * QT, QT), :],
                               (x_out if norm else x_sum)[:, s]).then_inc(stored[s], 16)
                sync.wait_ge(part_hi, b * QT + QT)
                sync.wait_ge(part_lo, b * QT + QT)
                sync.dma_start(tiles(part_dram)[:, ds(b * QT, QT), :],
                               part[:, s].rearrange("p q h n -> p q (h n)")).then_inc(stored[s], 16)

            pipeline(sync, early, late)
            for s in range(2):
                sync.wait_ge(stored[s], 32 * (B // 2))

        @block.gpsimd
        def _(pool):
            def early(b, s, k):
                pool.wait_ge(aT_mm, before_last(b))
                pool.wait_ge(a_hi, b + 1)
                pool.tensor_tensor(a_part[:, s, 1], t.attn[:, ds(b * QT, QT), :], a_part[:, s, 0],
                                   ALU.subtract).then_inc(a_lo, 1)
                if norm:
                    pool.wait_ge(loaded[s], k * 16 + 16)
                    pool.tensor_tensor(x_res[:, s], x_res[:, s], t.bo[:].rearrange("p (o n) -> p o n", o=1)
                                       .broadcast_to([P, QT, D]), ALU.add).then_inc(biased, 1)

            def inverse_root(b, src, eps, mid, out, first_done, done):
                pool.tensor_tensor(small[:, mid], src, constants[:, eps], ALU.add).then_inc(first_done, 1)
                pool.wait_ge(first_done, b + 1)
                pool.tensor_tensor(small[:, out], small[:, mid], constants[:, 0], ALU.pow).then_inc(done, 1)

            def late(b, s, k):
                if norm:
                    pool.wait_ge(aggregated, b * QT + QT)
                    inverse_root(b, mean_var[:, s, :, 1], 1, 0, 1, var_out, rstd_out)
                else:
                    pool.wait_ge(summed, b * 2 + 2)
                    pool.wait_ge(stored[s], k * 32)
                    pool.tensor_tensor(x_sum[:, s], x_out[:, s], x_res[:, s], ALU.add).then_inc(added, 1)
                pool.wait_ge(squared, b * QT + QT)
                pool.wait_ge(part_lo, b * QT)
                inverse_root(b, ms[:, s], 2, 2, 3, ms_out, rms_out)

            for i, value in enumerate((-0.5, LN_EPS, RMS_EPS)):
                pool.memset(constants[:, i], value).then_inc(power, 1)
            pool.wait_ge(power, 3)
            pipeline(pool, early, late)

        @block.tensor
        def _(pe):
            def early(b, s, k):
                pe.wait_ge(a_hi, b + 1)
                pe.wait_ge(a_lo, b + 1)
                pe.wait_ge(aT_hi, b)
                pe.wait_ge(aT_lo, b)
                for hl in range(2):
                    for kd in range(KD):
                        for q in range(QT):
                            mm = pe.transpose(ps_aT[:, hl, kd, q * P:(q + 1) * P],
                                              a_part[:, s, hl, q, kd * P:(kd + 1) * P], t.ident16[:])
                mm.then_inc(aT_mm, 1)
                pe.wait_ge(aT_hi, b + 1)
                pe.wait_ge(aT_lo, b + 1)
                for u in range(2):
                    pe.wait_ge(summed, b * 2)
                    for j in range(2):
                        n, q = 0, 2 * u + j
                        for wh, ah in ((0, 0), (1, 0), (0, 1)):
                            for kd in range(KD):
                                mm = pe.matmul(ps_y[:, u, j], aT[:, s, ah, kd, q * P:(q + 1) * P],
                                               t.w_proj[:, 4 * layer + 3, wh, kd, :], start=n == 0, stop=n == 5)
                                n += 1
                    mm.then_inc(y_mm, 1)

            def late(b, s, k):
                if not route:
                    return
                pe.wait_ge(part_hi, b * QT + QT)
                pe.wait_ge(part_lo, b * QT + QT)
                pe.wait_ge(nT_hi, b)
                pe.wait_ge(nT_lo, b)
                for hl in range(2):
                    for kd in range(KD):
                        for q in range(QT):
                            mm = pe.transpose(ps_nT[:, hl, kd, q * P:(q + 1) * P],
                                              part[:, s, q, hl, kd * P:(kd + 1) * P], t.ident16[:])
                mm.then_inc(nT_mm, 1)
                pe.wait_ge(nT_hi, b + 1)
                pe.wait_ge(nT_lo, b + 1)
                pe.wait_ge(logits_out, b)
                for q in range(QT):
                    n = 0
                    for wh, nh in ((0, 0), (1, 0), (0, 1)):
                        for kd in range(KD):
                            mm = pe.matmul(ps_l[:, q], nT[:, nh, kd, q * P:(q + 1) * P], t.w_router[:, wh, kd, :],
                                           start=n == 0, stop=n == 5)
                            n += 1
                mm.then_inc(logits_mm, 1)

            pipeline(pe, early, late)

        @block.scalar
        def _(act):
            def early(b, s, k):
                act.wait_ge(aT_mm, before_last(b))
                act.activation(a_part[:, s, 0], t.attn[:, ds(b * QT, QT), :], ACT.Copy).then_inc(a_hi, 1)
                act.wait_ge(aT_mm, b + 1)
                act.activation(aT[:, s, 0], ps_aT[:, 0], ACT.Copy).then_inc(aT_hi, 1)

            def late(b, s, k):
                for q in range(QT):
                    wait_x(act, b, q)
                    act.activation(squares[:, s, q], x_out[:, s, q], ACT.Square, scale=D ** -0.5,
                                   accum_out=ms[:, s, q:q + 1]).then_inc(squared, 1)
                act.wait_ge(rms_out, b + 1)
                act.wait_ge(stored[s], k * 32)
                for q in range(QT):
                    act.activation(part[:, s, q, 0], x_out[:, s, q], ACT.Copy,
                                   scale=small[:, 3, q:q + 1]).then_inc(part_hi, 1)
                if route:
                    act.wait_ge(nT_mm, b + 1)
                    act.activation(nT[:, 0], ps_nT[:, 0], ACT.Copy).then_inc(nT_hi, 1)

            pipeline(act, early, late)

        @block.vector
        def _(vector):
            def early(b, s, k):
                vector.wait_ge(aT_mm, b + 1)
                vector.tensor_copy(aT[:, s, 1], ps_aT[:, 1]).then_inc(aT_lo, 1)
                vector.wait_ge(biased if norm else loaded[s], b + 1 if norm else k * 16 + 16)
                if norm:
                    vector.wait_ge(stored[s], k * 32)
                else:
                    vector.wait_ge(added, before_last(b))
                    vector.wait_ge(part_hi, before_last(b) * QT)
                for u in range(2):
                    vector.wait_ge(y_mm, b * 2 + u + 1)
                    vector.tensor_tensor(x_new[:, s, 2 * u:2 * u + 2], ps_y[:, u], x_res[:, s, 2 * u:2 * u + 2],
                                         ALU.add).then_inc(summed, 1)
                if not norm:
                    return
                for q in range(QT):
                    vector.wait_ge(summed, b * 2 + q // 2 + 1)
                    vector.bn_stats(stats[:, s, q], x_new[:, s, q]).then_inc(stat_out, 1)
                n = counted(vector, b * QT + QT)
                vector.wait_ge(stat_out, 1)
                vector.wait_ge(stat_out, n)
                for q in range(QT):
                    vector.bn_aggr(mean_var[:, s, q], stats[:, s, q]).then_inc(aggregated, 1)

            def late(b, s, k):
                if norm:
                    vector.wait_ge(rstd_out, b + 1)
                    for q in range(QT):
                        vector.tensor_scalar(x_out[:, s, q], x_new[:, s, q], mean_var[:, s, q, 0:1],
                                             small[:, 1, q:q + 1], ALU.subtract, ALU.mult).then_inc(x_done, 1)
                for q in range(QT):
                    vector.wait_ge(part_hi, b * QT + q + 1)
                    vector.scalar_tensor_tensor(part[:, s, q, 1], x_out[:, s, q], small[:, 3, q:q + 1],
                                                part[:, s, q, 0], ALU.mult, ALU.subtract).then_inc(part_lo, 1)
                if route:
                    vector.wait_ge(nT_mm, b + 1)
                    vector.tensor_copy(nT[:, 1], ps_nT[:, 1]).then_inc(nT_lo, 1)
                    vector.wait_ge(logits_mm, b + 1)
                    vector.tensor_copy(t.logits[:, ds(b * QT, QT), :], ps_l[:]).then_inc(logits_out, 1)

            pipeline(vector, early, late)


def route_tokens(nc, t):
    HI = MT * SLOT // P
    with ExitStack() as ctx:
        sem = ctx.enter_context(stage_semaphores(nc, "r_"))
        sb = lambda n, s, d: ctx.enter_context(nc.sbuf_tensor("r_" + n, s, d))
        ps = lambda n, s, d: ctx.enter_context(nc.psum_tensor("r_" + n, s, d))
        rank = sb("rank", [P, NT, E], F32)
        best = sb("best", [P, 2, NT], F32)
        hit = sb("hit", [P, NT, E], F32)
        pick = sb("pick", [P, NT], F32)
        chosen = sb("chosen", [P, 2, NT, E], F32)
        left = sb("left", [P, NT, E], F32)
        both = sb("both", [P, NT, E], F32)
        gap, e_gap, one_more = sb("gap", [P, NT], F32), sb("e_gap", [P, NT], F32), sb("one_more", [P, NT], F32)
        earlier, ones = sb("earlier", [P, P], F32), sb("ones", [P, P], F32)
        totals = sb("totals", [P, E, NT], F32)
        keep = sb("keep", [P, E, NT], F32)
        run = sb("run", [P, E, NT], F32)
        count_i, padded_i = sb("count_i", [P, E], I32), sb("padded_i", [P, E], I32)
        padded, ends, starts = sb("padded", [P, E], F32), sb("ends", [P, E], F32), sb("starts", [P, E], F32)
        before, row = sb("before", [P, E, NT], F32), sb("row", [P, NT, E], F32)
        mine = sb("mine", [P, NT, E], F32)
        pos, pos_i = sb("pos", [P, 2, NT], F32), t.pos
        tile_start = sb("tile_start", [P, MT, 1], F32)
        passed, expert = sb("passed", [P, MT, E], F32), sb("expert", [P, MT], F32)
        hi_i, lo_i = sb("hi_i", [P, 2 * NT], I32), sb("lo_i", [P, 2 * NT], I32)
        hi, lo = sb("hi", [P, 2 * NT, 1], F32), sb("lo", [P, 2 * NT, 1], F32)
        count_hi, count_lo = sb("count_hi", [P, 1, HI], F32), sb("count_lo", [P, 1, P], F32)
        hot_hi = sb("hot_hi", [P, 2 * NT, HI], BF16)
        hot_lo = sb("hot_lo", [P, 2 * NT, P], BF16)
        by_tile = sb("by_tile", [P, 2 * NT, HI], BF16)
        by_row = sb("by_row", [P, 2 * NT, HI], BF16)
        tile_no, row_no = sb("tile_no", [P, 2, NT, 1], F32), sb("row_no", [P, 1], F32)
        inverse = sb("inverse", [P, P], F32)
        ps_c = ps("ps_c", [P, 2, NT * E], F32)
        ps_i = ps("ps_i", [P, 2, P], F32)
        ps_t = ps("ps_t", [P, P], F32)
        made, did, exp_done, counted, hot_done, by_row_done, inverse_mm, turned = map(sem, (
            "made", "did", "exp_done", "counted", "hot_done", "by_row_done", "inverse_mm", "turned"))
        ready_gap, ready_both, ready_inverse = sem("ready_gap"), sem("ready_both"), sem("ready_inverse")
        block = ctx.enter_context(nc.Block())
        flat = lambda x: x.rearrange("p a b -> p (a b)")
        wide = lambda x, n: x.rearrange("p (a o) -> p a o", o=1).broadcast_to([P, x.shape[1], n])

        @block.gpsimd
        def _(pool):
            iota = lambda out, pattern, base, mult: pool.iota(
                out, pattern, base=base, channel_multiplier=mult,
                allow_small_or_imprecise_dtypes=True).then_inc(made, 1)
            iota(rank[:], [[0, NT], [-1, E]], E, 0)
            iota(tile_start[:], [[SLOT, MT]], 0, 0)
            iota(count_hi[:], [[1, HI]], 0, 0)
            iota(count_lo[:], [[1, P]], 0, 0)
            iota(tile_no[:], [[0, 2], [1, NT]], 0, 0)
            iota(row_no[:], [[0, 1]], 0, 1)
            pool.memset(ones[:], 1.0).then_inc(made, 1)
            pool.memset(keep[:], 1.0).then_inc(made, 1)
            pool.wait_ge(made, 8)
            pool.affine_select(out=earlier[:], in_=ones[:], pattern=[[1, P]], compare_op=ALU.is_gt, fill=0.0,
                               base=0, channel_multiplier=-1).then_inc(made, 1)
            pool.memset(keep[:, :, 0:1], 0.0).then_inc(made, 1)
            pool.wait_ge(made, 10)

        MADE = 10

        @block.scalar
        def _(act):
            act.wait_ge(ready_gap, 1)
            act.activation(e_gap[:], gap[:], ACT.Exp).then_inc(exp_done, 1)

        @block.tensor
        def _(pe):
            pe.wait_ge(made, MADE)
            pe.wait_ge(ready_both, 1)
            pe.matmul(ps_c[:, 0], earlier[:], flat(both[:]), start=True, stop=True)
            pe.matmul(ps_c[:, 1], ones[:], flat(both[:]), start=True, stop=True,
                      skip_group_check=True).then_inc(counted, 1)
            pe.wait_ge(hot_done, 1)
            pe.wait_ge(by_row_done, 1)
            for v, values in enumerate((by_tile, by_row)):
                for n in range(2 * NT):
                    mm = pe.matmul(ps_i[0:HI, v], values[:, n, :], hot_lo[:, n, :], start=n == 0,
                                   stop=n == 2 * NT - 1, skip_group_check=True)
            mm.then_inc(inverse_mm, 1)
            pe.wait_ge(ready_inverse, 1)
            pe.transpose(ps_t[:, 0:HI], inverse[0:HI, :], t.ident32[0:HI, 0:HI]).then_inc(turned, 1)

        @block.vector
        def _(vector):
            done = [0]

            def chained(ins):
                done[0] += 1
                ins.then_inc(did, 1)
                vector.wait_ge(did, done[0])

            vector.wait_ge(made, MADE)
            source = t.logits
            for c in range(2):
                chained(vector.tensor_reduce(best[:, c], source[:], AX.X, ALU.max))
                chained(vector.tensor_tensor(hit[:], source[:], wide(best[:, c], E), ALU.is_equal))
                chained(vector.tensor_tensor(hit[:], hit[:], rank[:], ALU.mult))
                chained(vector.tensor_reduce(pick[:], hit[:], AX.X, ALU.max))
                chained(vector.tensor_tensor(chosen[:, c], rank[:], wide(pick[:], E), ALU.is_equal))
                if c == 0:
                    chained(vector.scalar_tensor_tensor(flat(left[:]), flat(chosen[:, 0]), NEG, flat(source[:]),
                                                        ALU.mult, ALU.add))
                    source = left
            vector.tensor_tensor(gap[:], best[:, 1], best[:, 0], ALU.subtract).then_inc(ready_gap, 1)
            vector.tensor_tensor(both[:], chosen[:, 0], chosen[:, 1], ALU.add).then_inc(ready_both, 1)
            vector.wait_ge(exp_done, 1)
            chained(vector.tensor_scalar(one_more[:], e_gap[:], 1.0, None, ALU.add))
            chained(vector.reciprocal(t.weight[:, 0], one_more[:]))
            chained(vector.tensor_tensor(t.weight[:, 1], t.weight[:, 0], e_gap[:], ALU.mult))
            vector.wait_ge(counted, 1)
            per_expert = ps_c[:, 1].rearrange("p (k e) -> p e k", e=E)
            chained(vector.tensor_copy(totals[:], per_expert))
            chained(vector.tensor_tensor_scan(flat(run[:]), flat(keep[:]), flat(totals[:]), 0.0, ALU.mult, ALU.add))
            chained(vector.tensor_scalar(count_i[:], run[:, :, NT - 1], float(SLOT - 1), None, ALU.add))
            shift = SLOT.bit_length() - 1
            chained(vector.tensor_scalar(padded_i[:], count_i[:], shift, shift, ALU.logical_shift_right,
                                         ALU.logical_shift_left))
            chained(vector.tensor_copy(padded[:], padded_i[:]))
            chained(vector.tensor_tensor_scan(ends[:], ones[:, 0:E], padded[:], 0.0, ALU.mult, ALU.add))
            chained(vector.tensor_tensor(starts[:], ends[:], padded[:], ALU.subtract))
            chained(vector.tensor_tensor(before[:], run[:], totals[:], ALU.subtract))
            chained(vector.tensor_tensor(before[:], before[:], wide(starts[:], NT), ALU.add))
            chained(vector.tensor_tensor(row[:], ps_c[:, 0].rearrange("p (k e) -> p k e", e=E),
                                         before[:].rearrange("p e k -> p k e"), ALU.add))
            for c in range(2):
                chained(vector.tensor_tensor(mine[:], row[:], chosen[:, c], ALU.mult))
                chained(vector.tensor_reduce(pos[:, c], mine[:], AX.X, ALU.add))
            chained(vector.tensor_copy(pos_i[:], pos[:]))
            chained(vector.tensor_tensor(passed[:], ends[:].rearrange("p (o e) -> p o e", o=1)
                                         .broadcast_to([P, MT, E]), tile_start[:].broadcast_to([P, MT, E]), ALU.is_le))
            chained(vector.tensor_reduce(expert[:], passed[:], AX.X, ALU.add))
            chained(vector.tensor_scalar(t.tile_expert[:], expert[:], float(E - 1), None, ALU.min))
            flat_pos = pos_i[:].rearrange("p c k -> p (c k)")
            chained(vector.tensor_scalar(hi_i[:], flat_pos, 7, None, ALU.logical_shift_right))
            chained(vector.tensor_scalar(lo_i[:], flat_pos, P - 1, None, ALU.bitwise_and))
            chained(vector.tensor_copy(hi[:, :, 0], hi_i[:]))
            chained(vector.tensor_copy(lo[:, :, 0], lo_i[:]))
            chained(vector.tensor_tensor(hot_hi[:], hi[:].broadcast_to([P, 2 * NT, HI]),
                                         count_hi[:].broadcast_to([P, 2 * NT, HI]), ALU.is_equal))
            vector.tensor_scalar(flat(by_row[:]), flat(hot_hi[:]), row_no[:, 0:1], None,
                                 ALU.mult).then_inc(by_row_done, 1)
            vector.tensor_tensor(hot_lo[:], lo[:].broadcast_to([P, 2 * NT, P]),
                                 count_lo[:].broadcast_to([P, 2 * NT, P]), ALU.is_equal)
            vector.tensor_tensor(by_tile[:], hot_hi[:], tile_no[:].rearrange("p c k o -> p (c k) o")
                                 .broadcast_to([P, 2 * NT, HI]), ALU.mult).then_inc(hot_done, 1)
            vector.wait_ge(inverse_mm, 1)
            chained(vector.tensor_copy(inverse[0:HI, :], ps_i[0:HI, 1]))
            vector.scalar_tensor_tensor(inverse[0:HI, :], ps_i[0:HI, 0], float(P), inverse[0:HI, :],
                                        ALU.mult, ALU.add).then_inc(ready_inverse, 1)
            vector.wait_ge(turned, 1)
            chained(vector.tensor_copy(t.token_of_row[:], ps_t[:, 0:HI]))


def expert_tiles(nc, t, wg, wu, wd):
    FP = FT * P
    with ExitStack() as ctx:
        sem = ctx.enter_context(stage_semaphores(nc, "e_"))
        pair = lambda n: [sem(f"{n}{i}") for i in range(2)]
        sb = lambda n, s, d: ctx.enter_context(nc.sbuf_tensor("e_" + n, s, d))
        ps = lambda n, s, d: ctx.enter_context(nc.psum_tensor("e_" + n, s, d))
        w_up = sb("w_up", [P, E, 2, KD, 2, FP], F16)
        w_down = sb("w_down", [P, E, 2, FT, D], F16)
        stage = sb("stage", [P, 2, KD, FP], F32)
        x = sb("x", [P, 2, 2, 2 * D], F16)
        index = sb("index", [P, 2, 2], I32)
        xT = sb("xT", [P, 2, 2, KD, SLOT], F16)
        gate = sb("gate", [P, 2, 2, SLOT], F32)
        h32 = sb("h32", [P, 2, 2, SLOT], F32)
        h = sb("h", [P, 2, 2, FT, SLOT], F16)
        y = sb("y", [P, 2, 2, D], F32)
        ps_xT = ps("ps_xT", [P, 2, KD, SLOT], F16)
        ps_gu = ps("ps_gu", [P, 2, 2, 2, SLOT], F32)
        ps_y = ps("ps_y", [P, 2, 2, D], F32)
        staged, split_hi, split_lo, scaled = pair("staged"), sem("split_hi"), sem("split_lo"), sem("zeroed")
        cleared = sem("index_cleared")
        gathered, indexed, stored, xT_mm, xT_out, y_mm, y_out = map(pair, (
            "gathered", "indexed", "stored", "xT_mm", "xT_out", "y_mm", "y_out"))
        gu_mm, gate_out, h_out, h_hi, h_lo = map(pair, ("gu_mm", "gate_out", "h_out", "h_hi", "h_lo"))
        block = ctx.enter_context(nc.Block())
        FG = FT // 2
        jobs = [(e, kind) for e in range(E) for kind in range(3)]

        def target(e, kind, hl):
            if kind == 2:
                return w_down[:, e, hl, 0:FT - 1], w_down[0:FR, e, hl, FT - 1]
            return [w_up[:, e, hl, k, kind, 0:F] for k in range(KD)]

        @block.sync
        def _(sync):
            for n, (e, kind) in enumerate(jobs):
                if n >= 2:
                    sync.wait_ge(split_hi, 2 * (n - 1))
                    sync.wait_ge(split_lo, 2 * (n - 1))
                s = n % 2
                if kind < 2:
                    sync.dma_start(stage[:, s, :, 0:F], (wg, wu)[kind][e].rearrange("(k p) f -> p k f", p=P)
                                   ).then_inc(staged[s], 32)
                else:
                    down = stage[:, s].rearrange("p k f -> p (k f)")
                    sync.dma_start(down[:, 0:(FT - 1) * D].rearrange("p (k n) -> p k n", n=D),
                                   wd[e, 0:(FT - 1) * P].rearrange("(k p) n -> p k n", p=P)).then_inc(staged[s], 16)
                    sync.dma_start(down[0:FR, (FT - 1) * D:FT * D],
                                   wd[e, (FT - 1) * P:F]).then_inc(staged[s], 16)
            with sync.Fori(0, MT // 2) as r:
                for s in range(2):
                    sync.wait_ge(y_out[s], r + 1)
                    sync.dma_start(t.y_dram.rearrange("(k p) n -> p k n", p=P)[:, ds(r * 4 + 2 * s, 2), :],
                                   y[:, s]).then_inc(stored[s], 16)
            for s in range(2):
                sync.wait_ge(stored[s], 16 * (MT // 2))

        @block.gpsimd
        def _(pool):
            pool.memset(index[:], 0).then_inc(cleared, 1)
            with pool.Fori(0, MT // 2) as r:
                for s in range(2):
                    used, copied = counted(pool, r * 32), counted(pool, r + 1)
                    pool.wait_ge(cleared, 1)
                    pool.wait_ge(gathered[s], used)
                    pool.tensor_copy(index[:, s], t.token_of_row[:, ds(r * 4 + 2 * s, 2)]).then_inc(indexed[s], 1)
                    pool.wait_ge(cleared, 1)
                    pool.wait_ge(indexed[s], copied)
                    pool.wait_ge(xT_mm[s], r)
                    for half in range(2):
                        pool.indirect_dma_start(x[:, s, half], None, t.part_dram,
                                                bass.IndirectOffsetOnAxis(ap=index[:, s, half:half + 1], axis=0)
                                                ).then_inc(gathered[s], 16)

        @block.tensor
        def _(pe):
            def turn(r, s):
                pe.wait_ge(gathered[s], r * 32 + 32)
                pe.wait_ge(xT_out[1 - s], r + s)
                for hl in range(2):
                    for k in range(KD):
                        for half in range(2):
                            mm = pe.transpose(ps_xT[:, hl, k, half * P:(half + 1) * P],
                                              x[:, s, half, hl * D + k * P:hl * D + (k + 1) * P], t.ident16[:])
                mm.then_inc(xT_mm[s], 1)

            def tile(r, s, following):
                j = r * 2 + s
                e = pe.value_load(t.tile_expert[0:1, ds(j, 1)], min_val=0, max_val=E - 1)
                pe.wait_ge(xT_out[s], r + 1)
                for i in range(FG):
                    c = s * FG + i
                    bank, turns = c % 2, r * FG + c // 2
                    pe.wait_ge(h_out[bank], turns)
                    for m in range(2):
                        f = 2 * i + m
                        for kind in range(2):
                            n = 0
                            for wh, xh in ((0, 0), (0, 1), (1, 0)):
                                for k in range(KD):
                                    w = w_up[:, :, wh, k, kind, f * P:(f + 1) * P]
                                    mm = pe.matmul(ps_gu[:, bank, kind, m],
                                                   w[:, ds(e, 1)].rearrange("p o f -> p (o f)"),
                                                   xT[:, s, xh, k, :], start=n == 0, stop=n == 5)
                                    n += 1
                    mm.then_inc(gu_mm[bank], 1)
                following()
                pe.wait_ge(y_out[s], r)
                for half in range(2):
                    c = 0
                    for f in range(FT):
                        if half == 0 and f % 2 == 0:
                            g = s * FG + f // 2
                            pe.wait_ge(h_hi[g % 2], r * FG + (g // 2 + 1))
                            pe.wait_ge(h_lo[g % 2], r * FG + (g // 2 + 1))
                        for hh, wh in ((0, 0), (0, 1), (1, 0)):
                            w = w_down[:, :, wh, f, :]
                            mm = pe.matmul(ps_y[:, s, half], h[:, s, hh, f, half * P:(half + 1) * P],
                                           w[:, ds(e, 1)].rearrange("p o f -> p (o f)"),
                                           start=c == 0, stop=c == 3 * FT - 1)
                            c += 1
                mm.then_inc(y_mm[s], 1)

            turn(0, 0)
            pe.wait_ge(split_hi, 2 * len(jobs))
            pe.wait_ge(split_lo, 2 * len(jobs))
            with pe.Fori(0, MT // 2 - 1) as r:
                tile(r, 0, lambda: turn(r, 1))
                tile(r, 1, lambda: turn(r + 1, 0))
            r = MT // 2 - 1
            tile(r, 0, lambda: turn(r, 1))
            tile(r, 1, lambda: None)

        @block.scalar
        def _(act):
            act.wait_ge(scaled, 2)
            for n, (e, kind) in enumerate(jobs):
                act.wait_ge(staged[n % 2], 32 * (n // 2 + 1))
                if kind < 2:
                    for k in range(KD):
                        act.activation(w_up[:, e, 0, k, kind, 0:F], stage[:, n % 2, k, 0:F], ACT.Copy,
                                       scale=t.g2[:, k:k + 1]).then_inc(split_hi, 1)
                else:
                    down = stage[:, n % 2].rearrange("p k f -> p (k f)")
                    act.activation(w_down[:, e, 0, 0:FT - 1].rearrange("p k n -> p (k n)"), down[:, 0:(FT - 1) * D],
                                   ACT.Copy).then_inc(split_hi, 1)
                    act.activation(w_down[0:FR, e, 0, FT - 1], down[0:FR, (FT - 1) * D:FT * D],
                                   ACT.Copy).then_inc(split_hi, 1)

            def move_x(r, s):
                act.wait_ge(xT_mm[s], r + 1)
                act.activation(xT[:, s], ps_xT[:], ACT.Copy).then_inc(xT_out[s], 1)

            move_x(0, 0)

            def tile(r, s, following):
                for i in range(FG):
                    c = s * FG + i
                    bank, turns = c % 2, r * FG + (c // 2 + 1)
                    act.wait_ge(gu_mm[bank], turns)
                    act.activation(gate[:, bank], ps_gu[:, bank, 0], ACT.Silu).then_inc(gate_out[bank], 1)
                    act.wait_ge(h_out[bank], turns)
                    act.activation(h[:, s, 0, 2 * i:2 * i + 2], h32[:, bank], ACT.Copy).then_inc(h_hi[bank], 1)
                    if i == FG - 1:
                        following()

            with act.Fori(0, MT // 2 - 1) as r:
                tile(r, 0, lambda: move_x(r, 1))
                tile(r, 1, lambda: move_x(r + 1, 0))
            r = MT // 2 - 1
            tile(r, 0, lambda: move_x(r, 1))
            tile(r, 1, lambda: None)

        @block.vector
        def _(vector):
            for part in (w_up[:, :, :, :, :, F:FP].rearrange("p e h k g f -> p (e h k g) f"),
                         w_down[FR:P, :, :, FT - 1].rearrange("p e h n -> p (e h) n")):
                vector.memset(part, 0.0).then_inc(scaled, 1)
            for n, (e, kind) in enumerate(jobs):
                vector.wait_ge(split_hi, 2 * n + 2)
                if kind < 2:
                    for k in range(KD):
                        vector.scalar_tensor_tensor(w_up[:, e, 1, k, kind, 0:F], stage[:, n % 2, k, 0:F],
                                                    t.g2[:, k:k + 1], w_up[:, e, 0, k, kind, 0:F],
                                                    ALU.mult, ALU.subtract).then_inc(split_lo, 1)
                else:
                    down = stage[:, n % 2].rearrange("p k f -> p (k f)")
                    flat = lambda hl: w_down[:, e, hl, 0:FT - 1].rearrange("p k n -> p (k n)")
                    vector.tensor_tensor(flat(1), down[:, 0:(FT - 1) * D], flat(0), ALU.subtract).then_inc(split_lo, 1)
                    vector.tensor_tensor(w_down[0:FR, e, 1, FT - 1], down[0:FR, (FT - 1) * D:FT * D],
                                         w_down[0:FR, e, 0, FT - 1], ALU.subtract).then_inc(split_lo, 1)
            with vector.Fori(0, MT // 2) as r:
                for s in range(2):
                    for i in range(FG):
                        c = s * FG + i
                        bank, turns = c % 2, r * FG + c // 2
                        vector.wait_ge(gate_out[bank], turns + 1)
                        vector.wait_ge(h_hi[bank], turns)
                        vector.tensor_tensor(h32[:, bank], gate[:, bank], ps_gu[:, bank, 1],
                                             ALU.mult).then_inc(h_out[bank], 1)
                        vector.wait_ge(h_hi[bank], turns + 1)
                        vector.tensor_tensor(h[:, s, 1, 2 * i:2 * i + 2], h32[:, bank], h[:, s, 0, 2 * i:2 * i + 2],
                                             ALU.subtract).then_inc(h_lo[bank], 1)
                    vector.wait_ge(y_mm[s], r + 1)
                    vector.wait_ge(stored[s], r * 16)
                    vector.tensor_copy(y[:, s], ps_y[:, s]).then_inc(y_out[s], 1)


def combine(nc, t, out):
    with ExitStack() as ctx:
        sem = ctx.enter_context(stage_semaphores(nc, "c_"))
        pair = lambda n: [sem(f"{n}{i}") for i in range(2)]
        sb = lambda n, s, d: ctx.enter_context(nc.sbuf_tensor("c_" + n, s, d))
        h = sb("h", [P, 2, QT, D], F32)
        rows = sb("rows", [P, 2, QT, 2, D], F32)
        index = sb("index", [P, 2, QT, 2], I32)
        z = sb("z", [P, 2, QT, 2, D], F32)
        res = sb("res", [P, 2, QT, D], F32)
        stats, mean_var = sb("stats", [P, 2, QT, 6], F32), sb("mean_var", [P, 2, QT, 2], F32)
        small = sb("small", [P, 2, 2, QT], F32)
        constants = sb("constants", [P, 2, QT], F32)
        loaded, stored, indexed = pair("loaded"), pair("stored"), sem("indexed")
        gathered = [[sem(f"gathered{s}{q}") for q in range(QT)] for s in range(2)]
        first, summed, stat_out, aggregated, power, var_out, rstd_out, done = map(sem, (
            "first", "summed", "stat_out", "aggregated", "power", "var_out", "rstd_out", "done"))
        block = ctx.enter_context(nc.Block())
        tiles = lambda x: x.rearrange("(k p) n -> p k n", p=P)

        @block.sync
        def _(sync):
            def early(b, s, k):
                sync.wait_ge(first, before_last(b) * QT)
                sync.dma_start(h[:, s], tiles(t.h_dram)[:, ds(b * QT, QT), :]).then_inc(loaded[s], 16)

            def late(b, s, k):
                sync.wait_ge(done, b * QT + QT)
                sync.dma_start(tiles(out)[:, ds(b * QT, QT), :], res[:, s]).then_inc(stored[s], 16)

            pipeline(sync, early, late)
            for s in range(2):
                sync.wait_ge(stored[s], 16 * (B // 2))

        @block.gpsimd
        def _(pool):
            for i, value in enumerate((-0.5, LN_EPS)):
                pool.memset(constants[:, i], value).then_inc(power, 1)
            pool.wait_ge(power, 2)

            def early(b, s, k):
                used, copied = counted(pool, before_last(b) * QT), counted(pool, b * 2 + 2)
                pool.wait_ge(power, 2)
                pool.wait_ge(summed, used)
                for c in range(2):
                    pool.tensor_copy(index[:, s, :, c], t.pos[:, c, ds(b * QT, QT)]).then_inc(indexed, 1)
                pool.wait_ge(power, 2)
                pool.wait_ge(indexed, copied)
                for q in range(QT):
                    for c in range(2):
                        pool.indirect_dma_start(rows[:, s, q, c], None, t.y_dram,
                                                bass.IndirectOffsetOnAxis(ap=index[:, s, q, c:c + 1], axis=0)
                                                ).then_inc(gathered[s][q], 16)

            def late(b, s, k):
                pool.wait_ge(aggregated, b * QT + QT)
                pool.tensor_tensor(small[:, s, 0], mean_var[:, s, :, 1], constants[:, 1],
                                   ALU.add).then_inc(var_out, 1)
                pool.wait_ge(var_out, b + 1)
                pool.tensor_tensor(small[:, s, 1], small[:, s, 0], constants[:, 0], ALU.pow).then_inc(rstd_out, 1)

            pipeline(pool, early, late)

        @block.vector
        def _(vector):
            def early(b, s, k):
                for q in range(QT):
                    vector.wait_ge(gathered[s][q], k * 32 + 32)
                    if q == 0:
                        vector.wait_ge(loaded[s], k * 16 + 16)
                    w = t.weight[:, :, ds(b * QT + q, 1)]
                    vector.scalar_tensor_tensor(z[:, s, q, 0], rows[:, s, q, 0], w[:, 0], h[:, s, q],
                                                ALU.mult, ALU.add).then_inc(first, 1)
                for q in range(QT):
                    w = t.weight[:, :, ds(b * QT + q, 1)]
                    vector.wait_ge(first, b * QT + (q + 1))
                    vector.scalar_tensor_tensor(z[:, s, q, 1], rows[:, s, q, 1], w[:, 1], z[:, s, q, 0],
                                                ALU.mult, ALU.add).then_inc(summed, 1)
                for q in range(QT):
                    vector.wait_ge(summed, b * QT + (q + 1))
                    vector.bn_stats(stats[:, s, q], z[:, s, q, 1]).then_inc(stat_out, 1)
                n = counted(vector, b * QT + QT)
                vector.wait_ge(stat_out, 1)
                vector.wait_ge(stat_out, n)
                for q in range(QT):
                    vector.bn_aggr(mean_var[:, s, q], stats[:, s, q]).then_inc(aggregated, 1)

            def late(b, s, k):
                vector.wait_ge(rstd_out, b + 1)
                vector.wait_ge(stored[s], k * 16)
                for q in range(QT):
                    vector.tensor_scalar(res[:, s, q], z[:, s, q, 1], mean_var[:, s, q, 0:1],
                                         small[:, s, 1, q:q + 1], ALU.subtract, ALU.mult).then_inc(done, 1)

            pipeline(vector, early, late)


def feed_forward_kernel(nc, a, out):
    with ExitStack() as top:
        dram = lambda n, s, d: nc.dram_tensor(n, s, d).ap()
        sb = lambda n, s, d: top.enter_context(nc.sbuf_tensor(n, s, d))
        t = Tensors()
        t.qk_dram = [dram(f"qk_{hl}", [P, 4, T], F16) for hl in ("hi", "lo")]
        t.v_dram, x1_dram, t.h_dram = dram("v", [T, D], F32), dram("x1", [T, D], F32), dram("h", [T, D], F32)
        t.part_dram = dram("part", [T, 2 * D], F16)
        t.y_dram = dram("y", [MT * SLOT, D], F32)
        t.ident32, t.ident16 = sb("ident32", [P, P], F32), sb("ident16", [P, P], F16)
        t.g2 = sb("g2", [P, KD], F32)
        t.logits, t.weight = sb("logits", [P, NT, E], F32), sb("weight", [P, 2, NT], F32)
        t.pos, t.token_of_row = sb("pos", [P, 2, NT], I32), sb("token_of_row", [P, MT * SLOT // P], I32)
        t.tile_expert = sb("tile_expert", [P, MT], I32)
        with ExitStack() as ctx:
            attention_tensors(nc, ctx, t)
            row = lambda x: x.rearrange("(o n) -> o n", o=1).broadcast_to([P, x.shape[0]])
            setup(nc, t, [a["A_W" + k] for k in "qkvo"] + [a["F_w" + k] for k in "qkvo"], a["w_router"],
                  [(t.bq[:], a["bq"]), (t.bk[:], a["bk"]), (t.g1[:], a["g1"]), (t.g2[:], a["g2"]),
                   (t.bv2[:, 0], row(a["bv"])), (t.bv2[:, 1], row(a["bv"])), (t.bo[:], row(a["bo"])),
                   (t.head_mask[:], row(a["head_mask"])), (t.cos[:], a["cos"]), (t.sin[:], a["sin"]),
                   (t.rot[:], a["rotation"])])
            project_qkv(nc, t, 0, lambda b: a["xT"].rearrange("(k p) n -> p k n", p=P)[:, :, ds(b * S, S)])
            attend(nc, t, 0)
            project_out(nc, t, 0, a["x"], x1_dram, t.part_dram)
            project_qkv(nc, t, 1, lambda b: t.part_dram.rearrange("(k p) n -> p k n", p=P)[:, ds(b * QT, QT), :])
            attend(nc, t, 1)
            project_out(nc, t, 1, x1_dram, t.h_dram, t.part_dram)
        route_tokens(nc, t)
        expert_tiles(nc, t, a["wg"], a["wu"], a["wd"])
        combine(nc, t, out)


def kernel(**inputs):
    import concourse.bacc as bacc
    from concourse.bass_utils import run_bass_kernel_spmd

    given = {k: np.asarray(v) for k, v in inputs.items()}
    columns = lambda x: np.ascontiguousarray(x.reshape(KD, P).T)
    arrays = {"x": given["L0_attn_x"].reshape(T, D)}
    arrays["xT"] = np.ascontiguousarray(arrays["x"].T)
    for k in "qkvo":
        arrays["A_W" + k] = np.ascontiguousarray(given["L0_attn_W" + k].T)
        arrays["F_w" + k] = given["L0_ffn_w" + k]
    for k in ("bv", "bo", "head_mask"):
        arrays[k] = given["L0_attn_" + k]
    for k in ("w_router", "wg", "wu", "wd"):
        arrays[k] = given["L0_ffn_" + k]
    arrays["bq"], arrays["bk"] = columns(given["L0_attn_bq"]), columns(given["L0_attn_bk"])
    arrays["g1"], arrays["g2"] = columns(given["L0_ffn_g1"]), columns(given["L0_ffn_g2"])
    inv_freq = 1.0 / 10000.0 ** (np.arange(0, DH, 2, dtype=np.float32) / DH)
    angle = np.einsum("i,j->ij", np.arange(S, dtype=np.float32), inv_freq)
    angle = np.tile(np.concatenate([angle, angle], axis=-1), (1, P // DH)).T
    arrays["cos"] = np.ascontiguousarray(np.cos(angle), np.float32)
    arrays["sin"] = np.ascontiguousarray(np.sin(angle), np.float32)
    rotation = np.zeros((P, P), np.float32)
    for head in range(P // DH):
        for d in range(DH // 2):
            rotation[head * DH + d + DH // 2, head * DH + d] = -1.0
            rotation[head * DH + d, head * DH + d + DH // 2] = 1.0
    arrays["rotation"] = rotation

    nc = bacc.Bacc("TRN2", target_bir_lowering=False, num_devices=1)
    a = {n: nc.dram_tensor("in_" + n, v.shape, mybir.dt.from_np(v.dtype), kind="ExternalInput").ap()
         for n, v in arrays.items()}
    out = nc.dram_tensor("out", [T, D], F32, kind="ExternalOutput").ap()
    feed_forward_kernel(nc, a, out)
    r = run_bass_kernel_spmd(nc, [{"in_" + n: v for n, v in arrays.items()}], core_ids=[0])
    return np.asarray(r.results[0]["out"]).reshape(B, S, D)
```

```python
from contextlib import ExitStack, contextmanager

import numpy as np
import concourse.bass as bass
from concourse import mybir

ALU = mybir.AluOpType
ACT = mybir.ActivationFunctionType
AX = mybir.AxisListType
F32 = mybir.dt.float32
F16 = mybir.dt.float16
BF16 = mybir.dt.bfloat16
I32 = mybir.dt.int32
U32 = mybir.dt.uint32
ds = bass.ds

P = 128
B, S, D = 8, 512, 256
H, DH = 16, 16
T = B * S
QT = S // P
NT = T // P
KD = D // P
G, HG = 4, 4
E, F = 8, 704
FT = (F + P - 1) // P
FR = F - (FT - 1) * P
SLOT = 256
MT = 2 * T // SLOT + E - 1
SPARE = MT * SLOT
HI = SPARE // P
WP = E * D * F // P // B
LN_EPS, RMS_EPS = 1e-5, 1e-6
MAXROW = P - 2
NEG = -1.0e30


class Tensors:
    pass


@contextmanager
def stage_semaphores(nc, prefix):
    handles = []

    def sem(name):
        handles.append(nc.alloc_semaphore(name=prefix + name))
        return handles[-1]

    yield sem
    nc.clear_and_free_semaphores(handles)
    nc.all_engine_barrier()


def setup(nc, t, w_in, router_in, vec_in):
    with ExitStack() as ctx:
        sem = ctx.enter_context(stage_semaphores(nc, ""))
        w32 = ctx.enter_context(nc.sbuf_tensor("w32", [P, 8, KD, D], F32))
        r32 = ctx.enter_context(nc.sbuf_tensor("r32", [P, KD, E], F32))
        scale = ctx.enter_context(nc.sbuf_tensor("w_scale", [P, 8, KD], F32))
        loaded, filled, scaled, split_hi, split_lo, rotated = map(sem, (
            "setup_loaded", "setup_filled", "weight_scale_ready", "weights_hi", "weights_lo", "weights_rotated"))
        block = ctx.enter_context(nc.Block())

        @block.sync
        def _(sync):
            n = 0
            for j, w in enumerate(w_in):
                sync.dma_start(w32[:, j], w.rearrange("(k p) n -> p k n", p=P)).then_inc(loaded, 16)
                n += 16
            for dst, src in vec_in:
                sync.dma_start(dst, src).then_inc(loaded, 16)
                n += 16
            sync.dma_start(r32[:], router_in.rearrange("(k p) n -> p k n", p=P)).then_inc(loaded, 16)
            sync.wait_ge(loaded, n + 16)
            sync.wait_ge(split_lo, 9 * KD)

        n_dma = 16 * (len(w_in) + len(vec_in) + 1)

        @block.gpsimd
        def _(pool):
            pool.memset(t.ident32[:], 0.0).then_inc(filled, 1)
            pool.memset(t.mask_kq[:], 0.0).then_inc(filled, 1)
            pool.wait_ge(filled, 2)
            pool.affine_select(out=t.ident32[:], in_=t.ident32[:], pattern=[[-1, P]], compare_op=ALU.not_equal,
                               fill=1.0, base=0, channel_multiplier=1).then_inc(filled, 1)
            pool.affine_select(out=t.mask_qk[:], in_=t.mask_kq[:], pattern=[[-1, P]], compare_op=ALU.is_ge,
                               fill=NEG, base=0, channel_multiplier=1).then_inc(filled, 1)
            pool.wait_ge(filled, 4)
            pool.affine_select(out=t.mask_kq[:], in_=t.mask_kq[:], pattern=[[1, P]], compare_op=ALU.is_ge,
                               fill=NEG, base=0, channel_multiplier=-1).then_inc(filled, 1)
            pool.tensor_copy(t.ident16[:], t.ident32[:]).then_inc(filled, 1)
            pool.tensor_copy(t.ident_bf[:], t.ident32[:]).then_inc(filled, 1)
            pool.wait_ge(filled, 7)

        @block.vector
        def _(vector):
            vector.memset(scale[:], 1.0).then_inc(scaled, 1)
            vector.wait_ge(scaled, 1)
            vector.memset(scale[:, 0], DH ** -0.5).then_inc(scaled, 1)
            vector.wait_ge(loaded, n_dma)
            vector.tensor_scalar(scale[:, 4], t.g1[:], DH ** -0.5, None, ALU.mult).then_inc(scaled, 1)
            for j in (5, 6):
                vector.tensor_copy(scale[:, j], t.g1[:]).then_inc(scaled, 1)
            vector.tensor_scalar(t.bq[:], t.bq[:], DH ** -0.5, None, ALU.mult).then_inc(scaled, 1)
            vector.wait_ge(scaled, 6)
            for j in range(8):
                for k in range(KD):
                    n = j * KD + k + 1
                    vector.wait_ge(split_hi, n)
                    vector.scalar_tensor_tensor(t.w_proj[:, j, 1, k], w32[:, j, k], scale[:, j, k:k + 1],
                                                t.w_proj[:, j, 0, k], ALU.mult, ALU.subtract).then_inc(split_lo, 1)
            for k in range(KD):
                vector.wait_ge(split_hi, 8 * KD + k + 1)
                vector.tensor_tensor(t.w_router[:, 1, k], r32[:, k], t.w_router[:, 0, k],
                                     ALU.subtract).then_inc(split_lo, 1)

        @block.scalar
        def _(act):
            act.wait_ge(loaded, n_dma)
            act.wait_ge(scaled, 6)
            for j in range(8):
                for k in range(KD):
                    act.activation(t.w_proj[:, j, 0, k], w32[:, j, k], ACT.Copy,
                                   scale=scale[:, j, k:k + 1]).then_inc(split_hi, 1)
            for k in range(KD):
                act.activation(t.w_router[:, 0, k], r32[:, k], ACT.Copy).then_inc(split_hi, 1)
            act.wait_ge(split_lo, 6 * KD)
            halves = lambda x: x.rearrange("p w b k (h t d) -> p (w b k h) t d", h=H, t=2)
            src, dst = halves(t.w_proj[:, 4:6]), halves(t.w_rot[:])
            act.activation(dst[:, :, 0], src[:, :, 1], ACT.Copy, scale=-1.0).then_inc(rotated, 1)
            act.activation(dst[:, :, 1], src[:, :, 0], ACT.Copy).then_inc(rotated, 1)
            act.wait_ge(rotated, 2)


def project_qkv(nc, t, layer, x_dram):
    rope = layer == 1
    with ExitStack() as ctx:
        L = f"l{layer}_"
        sem = ctx.enter_context(stage_semaphores(nc, L))
        pair = lambda n: [sem(f"{n}{i}") for i in range(2)]
        sb = lambda n, s, d: ctx.enter_context(nc.sbuf_tensor(L + n, s, d))
        ps = lambda n, s, d: ctx.enter_context(nc.psum_tensor(L + n, s, d))
        x_in = sb("x_in", [P, 2, QT, 2 * D] if rope else [P, 2, KD, S], F16 if rope else F32)
        xT = sb("xT", [P, 2, 2, KD, S], F16)
        qk = sb("qk", [P, 2, 4, 2, S], F16)
        v = sb("v", [P, 2, QT, D], F32)
        ps_qk = ps("ps_qk", [P, 2, S], F32)
        ps_v = ps("ps_v", [P, 2, 2, D], F32)
        if rope:
            q_cos = sb("q_cos", [P, 2, S], F32)
            q_sin = sb("q_sin", [P, 2, S], F32)
            q_rot = sb("q_rot", [P, 2, S], F32)
            ps_rot = ps("ps_rot", [P, 2, S], F32)
            ps_xT = ps("ps_xT", [P, 2, KD, S], F16)
        x_loaded, stored, xT_mm, xT_hi, xT_lo, v_mm, v_out = map(pair, (
            "x_loaded", "stored", "xT_mm", "xT_hi", "xT_lo", "v_mm", "v_out"))
        qk_mm, qk_hi, qk_lo, rot_mm, cos_out, sin_out, rot_out = map(pair, (
            "qk_mm", "qk_hi", "qk_lo", "rot_mm", "cos_out", "sin_out", "rot_out"))
        filled = sem("filled")
        block = ctx.enter_context(nc.Block())
        STORES = 3 * 16

        def done(b, c):
            return b * 2 + (c // 2 + 1)

        def free(b, c):
            return b * 2 + c // 2

        @block.sync
        def _(sync):
            def load(b, s):
                sync.dma_start(x_in[:, s], x_dram(b)).then_inc(x_loaded[s], 16)

            def store(b, s):
                for c in (2, 3):
                    sync.wait_ge(qk_hi[c % 2], done(b, c))
                    sync.wait_ge(qk_lo[c % 2], done(b, c))
                for hl in range(2):
                    sync.dma_start(t.qk_dram[hl][:, :, ds(b * S, S)], qk[:, s, :, hl, :]).then_inc(stored[s], 16)

            def store_v(b, r, s):
                sync.wait_ge(v_out[s], r * 2 + 2)
                sync.dma_start(t.v_dram.rearrange("(k p) n -> p k n", p=P)[:, ds(b * QT, QT), :],
                               v[:, s]).then_inc(stored[s], 16)

            load(0, 0)
            load(1, 1)
            with sync.Fori(0, B // 2 - 1) as r:
                for s in range(2):
                    sync.wait_ge(xT_hi[s], r + 1)
                    sync.wait_ge(xT_lo[s], r + 1)
                    load(r * 2 + (2 + s), s)
                    store(r * 2 + s, s)
                    store_v(r * 2 + s, r, s)
            for s in range(2):
                store(B - 2 + s, s)
                store_v(B - 2 + s, B // 2 - 1, s)
            for s in range(2):
                sync.wait_ge(stored[s], STORES * (B // 2))

        @block.tensor
        def _(pe):
            def transpose_x(r, s):
                pe.wait_ge(x_loaded[s], r * 16 + 16)
                o = 1 - s
                pe.wait_ge(xT_hi[o], r + s)
                pe.wait_ge(xT_lo[o], r + s)
                for hl in range(2):
                    for k in range(KD):
                        for q in range(QT):
                            mm = pe.transpose(ps_xT[:, hl, k, q * P:(q + 1) * P],
                                              x_in[:, s, q, hl * D + k * P:hl * D + (k + 1) * P], t.ident16[:])
                mm.then_inc(xT_mm[s], 1)

            def project(out, w, s, m):
                n = 0
                for wh, xh in ((0, 0), (0, 1), (1, 0)):
                    for k in range(KD):
                        mm = pe.matmul(out, w[:, wh, k, m * P:(m + 1) * P], xT[:, s, xh, k, :],
                                       start=n == 0, stop=n == 5)
                        n += 1
                return mm

            with pe.Fori(0, B // 2) as r:
                for s in range(2):
                    b = r * 2 + s
                    if rope:
                        transpose_x(r, s)
                    pe.wait_ge(xT_hi[s], r + 1)
                    pe.wait_ge(xT_lo[s], r + 1)
                    for c in range(4):
                        w, m = c // 2, c % 2
                        for read in ([cos_out] if rope else [qk_hi, qk_lo]):
                            pe.wait_ge(read[c % 2], free(b, c))
                        project(ps_qk[:, c % 2], t.w_proj[:, 4 * layer + w], s, m).then_inc(qk_mm[c % 2], 1)
                        if rope:
                            pe.wait_ge(sin_out[c % 2], free(b, c))
                            project(ps_rot[:, c % 2], t.w_rot[:, w], s, m).then_inc(rot_mm[c % 2], 1)
                    for u in range(2):
                        pe.wait_ge(v_out[1 - s], (r + s) * 2)
                        for j in range(2):
                            n, q = 0, 2 * u + j
                            for wh, xh in ((0, 0), (1, 0), (0, 1)):
                                for k in range(KD):
                                    mm = pe.matmul(ps_v[:, u, j], xT[:, s, xh, k, q * P:(q + 1) * P],
                                                   t.w_proj[:, 4 * layer + 2, wh, k, :], start=n == 0, stop=n == 5)
                                    n += 1
                        mm.then_inc(v_mm[s], 1)

        @block.scalar
        def _(act):
            with act.Fori(0, B // 2) as r:
                for s in range(2):
                    b = r * 2 + s
                    if rope:
                        act.wait_ge(xT_mm[s], r + 1)
                    else:
                        act.wait_ge(x_loaded[s], r * 16 + 16)
                    act.wait_ge(v_mm[s], r * 2)
                    src = ps_xT[:, 0] if rope else x_in[:, s]
                    act.activation(xT[:, s, 0], src, ACT.Copy).then_inc(xT_hi[s], 1)
                    act.wait_ge(stored[s], r * STORES)
                    for c in range(4):
                        if rope:
                            act.wait_ge(rot_out[c % 2], done(b, c))
                            act.activation(qk[:, s, c, 0], q_rot[:, c % 2], ACT.Copy).then_inc(qk_hi[c % 2], 1)
                        else:
                            act.wait_ge(qk_mm[c % 2], done(b, c))
                            bias = (t.bq if c < 2 else t.bk)[:, c % 2:c % 2 + 1]
                            act.activation(qk[:, s, c, 0], ps_qk[:, c % 2], ACT.Identity,
                                           bias=bias).then_inc(qk_hi[c % 2], 1)

        @block.vector
        def _(vector):
            with vector.Fori(0, B // 2) as r:
                for s in range(2):
                    b = r * 2 + s
                    vector.wait_ge(xT_hi[s], r + 1)
                    if rope:
                        vector.tensor_copy(xT[:, s, 1], ps_xT[:, 1]).then_inc(xT_lo[s], 1)
                    else:
                        vector.tensor_tensor(xT[:, s, 1], x_in[:, s], xT[:, s, 0], ALU.subtract).then_inc(xT_lo[s], 1)
                    vector.wait_ge(stored[s], r * STORES)
                    for c in range(4):
                        if rope:
                            vector.wait_ge(qk_mm[c % 2], done(b, c))
                            vector.wait_ge(rot_out[c % 2], free(b, c))
                            vector.tensor_tensor(q_cos[:, c % 2], ps_qk[:, c % 2], t.cos[:],
                                                 ALU.mult).then_inc(cos_out[c % 2], 1)
                            vector.wait_ge(rot_mm[c % 2], done(b, c))
                            vector.tensor_tensor(q_sin[:, c % 2], ps_rot[:, c % 2], t.sin[:],
                                                 ALU.mult).then_inc(sin_out[c % 2], 1)
                        else:
                            bias = (t.bq if c < 2 else t.bk)[:, c % 2:c % 2 + 1]
                            vector.wait_ge(qk_hi[c % 2], done(b, c))
                            vector.scalar_tensor_tensor(qk[:, s, c, 1], ps_qk[:, c % 2], bias, qk[:, s, c, 0],
                                                        ALU.add, ALU.subtract).then_inc(qk_lo[c % 2], 1)
                    for u in range(2):
                        vector.wait_ge(v_mm[s], r * 2 + (u + 1))
                        if rope:
                            vector.tensor_copy(v[:, s, 2 * u:2 * u + 2], ps_v[:, u]).then_inc(v_out[s], 1)
                        else:
                            vector.tensor_tensor(v[:, s, 2 * u:2 * u + 2], ps_v[:, u], t.bv2[:],
                                                 ALU.add).then_inc(v_out[s], 1)

        if rope:
            @block.gpsimd
            def _(pool):
                with pool.Fori(0, B // 2) as r:
                    for s in range(2):
                        b = r * 2 + s
                        pool.wait_ge(stored[s], r * STORES)
                        for c in range(5):
                            if c < 4:
                                i = c % 2
                                pool.wait_ge(qk_hi[i], free(b, c))
                                pool.wait_ge(qk_lo[i], free(b, c))
                                pool.wait_ge(cos_out[i], done(b, c))
                                pool.wait_ge(sin_out[i], done(b, c))
                                pool.tensor_tensor(q_rot[:, i], q_cos[:, i], q_sin[:, i], ALU.add).then_inc(rot_out[i], 1)
                            if c > 0:
                                i = (c - 1) % 2
                                pool.wait_ge(qk_hi[i], done(b, c - 1))
                                pool.tensor_tensor(qk[:, s, c - 1, 1], q_rot[:, i], qk[:, s, c - 1, 0],
                                                   ALU.subtract).then_inc(qk_lo[i], 1)
        else:
            @block.gpsimd
            def _(pool):
                pool.memset(t.qx[:], 0.0).then_inc(filled, 1)
                pool.memset(t.kx[:], 1.0).then_inc(filled, 1)
                pool.memset(t.v_one[:], 1.0).then_inc(filled, 1)
                pool.wait_ge(filled, 3)
                kf = t.kx[:].rearrange("p g h n -> p (g h n)")
                pool.affine_select(out=kf, in_=kf, pattern=[[0, G * HG * S]], compare_op=ALU.is_ge, fill=0.0,
                                   base=-MAXROW, channel_multiplier=1).then_inc(filled, 1)
                pool.wait_ge(filled, 4)


def attend(nc, t, layer, matrices=()):
    causal = layer == 1
    width = lambda kt: S - kt * P if causal else S
    keys = lambda q: (q + 1) * P if causal else S
    at = lambda kt: 0 if kt % 2 == 0 else width(kt - 1)
    with ExitStack() as ctx:
        L = f"a{layer}_"
        sem = ctx.enter_context(stage_semaphores(nc, L))
        several = lambda n, k: [sem(f"{n}{i}") for i in range(k)]
        sb = lambda n, s, d: ctx.enter_context(nc.sbuf_tensor(L + n, s, d))
        ps = lambda n, s, d: ctx.enter_context(nc.psum_tensor(L + n, s, d))
        qx, kx, v_one = t.qx, t.kx, t.v_one
        v_in = sb("v_in", [P, G, QT, HG * DH], F32)
        probs = sb("probs", [P, 2, HG, 2 * S], F32)
        neg_max = sb("neg_max", [P, G, QT, HG], F32)
        rows = sb("rows", [HG, 2, 2, S], F16)
        o32 = sb("o32", [P, S], F32)
        inv = sb("inv", [P, 2, QT, HG], F32)
        o_norm = sb("o_norm", [P, 2, QT, HG * DH], F32)
        if matrices:
            w_in = sb("w_in", [P, len(matrices), WP], F32)
            w_part = sb("w_part", [P, len(matrices), 2, WP], F16)
            w_loaded, w_hi, w_lo, w_stored = (
                several(n, len(matrices)) for n in ("w_loaded", "w_hi", "w_lo", "w_stored"))
        ps_s = ps("ps_s", [P, 2, 2 * S], F32)
        ps_m = ps("ps_m", [P, 2, S], F32)
        ps_o = ps("ps_o", [P, S], F32)
        ps_x = ps("ps_x", [P, S], F32)
        qk_loaded, v_loaded, rows_loaded, v_copied, group_done = (
            several(n, G) for n in ("qk_loaded", "v_loaded", "rows_loaded", "v_copied", "group_done"))
        scores_mm = sem("scores_mm")
        exp_out, max_out = several("exp_out", 2), several("max_out", 2)
        half_done = sem("half_done")
        max_mm, rows_mm, rows_hi, rows_lo = sem("max_mm"), sem("rows_mm"), sem("rows_hi"), sem("rows_lo")
        o_out, back_mm, inv_out, norm_out = sem("o_out"), sem("back_mm"), sem("inv_out"), sem("norm_out")
        attn_hi, attn_lo = sem("attn_hi"), sem("attn_lo")
        block = ctx.enter_context(nc.Block())

        def ahead(b, g, n):
            return b + (g + n) // G, (g + n) % G

        def steps(engine, step):
            for g in range(G):
                step(0, g, first=g == 0)
            with engine.Fori(1, B - 1) as b:
                for g in range(G):
                    step(b, g)
            for g in range(G):
                step(B - 1, g, maxima=g + 2 < G, has_next=g + 1 < G)

        @block.sync
        def _(sync):
            def load(b, g):
                for part, x, c0, terms in ((0, qx, 0, (0, 0, 1)), (1, kx, 2, (0, 1, 0))):
                    for n, hl in enumerate(terms):
                        c, p0 = c0 + g // 2, (g % 2) * HG * DH
                        src = t.qk_dram[hl][p0:p0 + HG * DH, c, ds(b * S, S)].rearrange("(h d) n -> d h n", d=DH)
                        sync.dma_start(x[n * DH:(n + 1) * DH, g], src).then_inc(qk_loaded[g], 16)
                sync.dma_start(v_in[:, g], t.v_dram.rearrange("(k p) n -> p k n", p=P)[
                    :, ds(b * QT, QT), g * HG * DH:(g + 1) * HG * DH]).then_inc(v_loaded[g], 16)

            def load_piece(b, i):
                src = matrices[i].rearrange("e a b -> (e a b)").rearrange("(p n) -> p n", p=P)
                sync.dma_start(w_in[:, i], src[:, ds(b * WP, WP)]).then_inc(w_loaded[i], 16)

            def store_piece(b, i):
                sync.wait_ge(w_hi[i], b + 1)
                sync.wait_ge(w_lo[i], b + 1)
                for hl in range(2):
                    dst = t.w_dram[i][hl].rearrange("e a b -> (e a b)").rearrange("(p n) -> p n", p=P)
                    sync.dma_start(dst[:, ds(b * WP, WP)], w_part[:, i, hl]).then_inc(w_stored[i], 16)

            def load_rows(b, g, n):
                sync.wait_ge(rows_hi, n)
                sync.wait_ge(rows_lo, n)
                for hl in range(2):
                    sync.dma_start(qx[MAXROW + hl:MAXROW + hl + 1, g], rows[0:HG, g % 2, hl]
                                   ).then_inc(rows_loaded[g], 16)

            def step(b, g, first=False, maxima=True, has_next=True):
                if has_next:
                    load_rows(*ahead(b, g, 1), b * G + (g + 2))
                if not (isinstance(b, int) and b == B - 1):
                    scored, copied = counted(sync, b * (8 * G) + 8 * (g + 1)), counted(sync, b + 1)
                    sync.wait_ge(scores_mm, scored)
                    sync.wait_ge(v_copied[g], copied)
                    load(b + 1, g)
                i = g - 1
                if 0 <= i < len(matrices):
                    store_piece(b, i)
                    if not (isinstance(b, int) and b == B - 1):
                        load_piece(b + 1, i)

            for g in range(G):
                load(0, g)
            for i in range(len(matrices)):
                load_piece(0, i)
            load_rows(0, 0, 1)
            steps(sync, step)
            for i in range(len(matrices)):
                sync.wait_ge(w_stored[i], 32 * B)

        @block.gpsimd
        def _(pool):
            def copy_v(b, g):
                loads = counted(pool, b * 16 + 16)
                pool.wait_ge(v_loaded[g], 16)
                pool.wait_ge(v_loaded[g], loads)
                pool.wait_ge(group_done[g], b)
                pool.tensor_copy(v_one[:, g, :, :, 0:DH],
                                 v_in[:, g].rearrange("p k (h d) -> p k h d", h=HG)).then_inc(v_copied[g], 1)

            def split(b, g):
                n = b * G + g
                hi, lo = (t.attn[:, hl, ds(b * QT, QT), g * HG * DH:(g + 1) * HG * DH] for hl in range(2))
                normed = counted(pool, n + 1)
                pool.wait_ge(norm_out, 1)
                pool.wait_ge(norm_out, normed)
                pool.tensor_copy(hi, o_norm[:, g % 2]).then_inc(attn_hi, 1)
                pool.wait_ge(attn_hi, 1)
                pool.wait_ge(attn_hi, normed)
                pool.tensor_tensor(lo, o_norm[:, g % 2], hi, ALU.subtract).then_inc(attn_lo, 1)

            def split_piece(b, i):
                loads, highs, stores = counted(pool, b * 16 + 16), counted(pool, b + 1), counted(pool, b * 32)
                pool.wait_ge(w_loaded[i], 16)
                pool.wait_ge(w_loaded[i], loads)
                pool.wait_ge(w_stored[i], stores)
                pool.tensor_copy(w_part[:, i, 0], w_in[:, i]).then_inc(w_hi[i], 1)
                pool.wait_ge(w_hi[i], highs)
                pool.tensor_tensor(w_part[:, i, 1], w_in[:, i], w_part[:, i, 0], ALU.subtract).then_inc(w_lo[i], 1)

            def step(b, g, first=False, maxima=True, has_next=True):
                copy_v(b, g)
                if g < len(matrices):
                    split_piece(b, g)
                if not (isinstance(b, int) and b * G + g < 3):
                    split(*ahead(b, g, -3))

            steps(pool, step)
            for g in range(1, G):
                split(B - 1, g)

        @block.tensor
        def _(pe):
            def scores(b, g, kp, j):
                c = kp * HG + j
                if c == 0:
                    pe.wait_ge(rows_loaded[g], b * 32 + 32)
                pe.wait_ge(exp_out[c % 2], b * (4 * G) + (4 * g + c // 2))
                for kt in (2 * kp, 2 * kp + 1):
                    out = ps_s[:, c % 2, at(kt):at(kt) + width(kt)]
                    mm = pe.matmul(out, kx[:, g, j, kt * P:(kt + 1) * P], qx[:, g, j, S - width(kt):S],
                                   start=True, stop=not causal)
                    if causal:
                        mm = pe.matmul(ps_s[:, c % 2, at(kt):at(kt) + P], t.ident_bf[:], t.mask_kq[:],
                                       start=False, stop=True)
                mm.then_inc(scores_mm, 1)

            def maxima_of(b, g, c):
                j, q = c // QT, c % QT
                if c == 0:
                    pe.wait_ge(qk_loaded[g], b * 96 + 96)
                pe.wait_ge(max_out[c % 2], b * (8 * G) + (8 * g + c // 2))
                mm = pe.matmul(ps_m[:, c % 2, 0:keys(q)], qx[0:MAXROW, g, j, q * P:(q + 1) * P],
                               kx[0:MAXROW, g, j, 0:keys(q)], start=True, stop=not causal)
                if causal:
                    mm = pe.matmul(ps_m[:, c % 2, q * P:(q + 1) * P], t.ident_bf[:], t.mask_qk[:],
                                   start=False, stop=True)
                mm.then_inc(max_mm, 1)

            def turn_maxima(b, g, n):
                for i in range(2):
                    pe.wait_ge(max_out[i], n * 8 + 8)
                pe.wait_ge(norm_out, max(n - 2, 0) if isinstance(n, int) else n - 2)
                for q in range(QT):
                    mm = pe.transpose(ps_x[0:HG, q * P:(q + 1) * P], neg_max[:, g, q, :], t.ident32[:])
                mm.then_inc(rows_mm, 1)

            def weigh(b, g, kt):
                n = b * G + g
                if kt % 2 == 0:
                    for i in range(2):
                        pe.wait_ge(exp_out[i], n * 4 + (kt + 2))
                if kt == 0:
                    pe.wait_ge(v_copied[g], b + 1)
                    pe.wait_ge(o_out, n)
                for j in range(HG):
                    mm = pe.matmul(ps_o[32 * j:32 * (j + 1), S - width(kt):S], v_one[:, g, kt, j, :],
                                   probs[:, kt // 2, j, at(kt):at(kt) + width(kt)],
                                   start=kt == 0, stop=kt == QT - 1)
                if kt == 1:
                    mm.then_inc(half_done, 1)
                elif kt == QT - 1:
                    mm.then_inc(group_done[g], 1)

            def turn_back(b, g):
                n = b * G + g
                pe.wait_ge(o_out, n + 1)
                turned = min(n + 3, B * G) if isinstance(n, int) else n + 3
                pe.wait_ge(rows_hi, turned)
                pe.wait_ge(rows_lo, turned)
                pe.wait_ge(norm_out, n)
                for q in range(QT):
                    mm = pe.transpose(ps_x[:, q * P:(q + 1) * P], o32[:, q * P:(q + 1) * P], t.ident32[:])
                mm.then_inc(back_mm, 1)

            def step(b, g, first=False, maxima=True, has_next=True):
                def a_maximum(c):
                    if maxima:
                        maxima_of(*ahead(b, g, 2), c)

                for half, kt in enumerate((2, 3, 0, 1)):
                    kp, j = half // 2, half % 2 * 2
                    a_maximum(4 * half)
                    scores(b, g, kp, j)
                    if half == 0 and has_next:
                        turn_maxima(*ahead(b, g, 1), b * G + (g + 1))
                    a_maximum(4 * half + 1)
                    scores(b, g, kp, j + 1)
                    a_maximum(4 * half + 2)
                    if half >= 2:
                        weigh(b, g, kt)
                    elif not first:
                        weigh(*ahead(b, g, -1), kt)
                    a_maximum(4 * half + 3)
                    if half == 2 and not first:
                        turn_back(*ahead(b, g, -1))

            for g in range(2):
                for c in range(HG * QT):
                    maxima_of(0, g, c)
                if g == 0:
                    turn_maxima(0, 0, 0)
            steps(pe, step)
            weigh(B - 1, G - 1, 2)
            weigh(B - 1, G - 1, 3)
            turn_back(B - 1, G - 1)

        @block.scalar
        def _(act):
            def exponentials(b, g, kp, j, first):
                n, c = b * G + g, kp * HG + j
                act.wait_ge(scores_mm, n * 8 + (c + 1))
                if j == 0:
                    if kp == 0:
                        act.wait_ge(half_done, n)
                    elif not first:
                        before, of = ahead(b, g, -1)
                        act.wait_ge(group_done[of], before + 1)
                w = width(2 * kp) + width(2 * kp + 1)
                act.activation(probs[:, kp, j, 0:w], ps_s[:, c % 2, 0:w], ACT.Exp).then_inc(exp_out[c % 2], 1)

            def rows_high(b, g, n):
                act.wait_ge(rows_mm, n)
                act.activation(rows[:, g % 2, 0], ps_x[0:HG, :], ACT.Copy).then_inc(rows_hi, 1)

            def empty_o(b, g):
                act.wait_ge(group_done[g], b + 1)
                act.wait_ge(back_mm, b * G + g)
                act.activation(o32[:], ps_o[:], ACT.Copy).then_inc(o_out, 1)

            def step(b, g, first=False, maxima=True, has_next=True):
                for kp in range(2):
                    if kp == 1 and not first:
                        empty_o(*ahead(b, g, -1))
                    for j in range(HG):
                        exponentials(b, g, kp, j, first)
                        if kp == 0 and j == 0 and has_next:
                            rows_high(*ahead(b, g, 1), b * G + (g + 2))

            rows_high(0, 0, 1)
            steps(act, step)
            empty_o(B - 1, G - 1)

        @block.vector
        def _(vector):
            def row_max(b, g, c):
                j, q = c // QT, c % QT
                vector.wait_ge(max_mm, b * (16 * G) + (16 * g + c + 1))
                vector.tensor_reduce(neg_max[:, g, q, j:j + 1], ps_m[:, c % 2, 0:keys(q)], AX.X, ALU.max,
                                     negate=True).then_inc(max_out[c % 2], 1)

            def rows_low(b, g, n):
                vector.wait_ge(rows_hi, n)
                vector.tensor_tensor(rows[:, g % 2, 1], ps_x[0:HG, :], rows[:, g % 2, 0],
                                     ALU.subtract).then_inc(rows_lo, 1)

            def normalise(b, g):
                n = b * G + g
                vector.wait_ge(back_mm, n + 1)
                o = ps_x[:].rearrange("p (q j d) -> p q j d", q=QT, j=HG)
                vector.reciprocal(inv[:, 0], o[:, :, :, DH]).then_inc(inv_out, 1)
                vector.wait_ge(inv_out, n * (1 if causal else 2) + 1)
                scale = inv[:, 0]
                if not causal:
                    mask = t.head_mask[:, g * HG:(g + 1) * HG].rearrange("p (o h) -> p o h", o=1)
                    vector.tensor_tensor(inv[:, 1], inv[:, 0], mask.broadcast_to([P, QT, HG]),
                                         ALU.mult).then_inc(inv_out, 1)
                    vector.wait_ge(inv_out, n * 2 + 2)
                    scale = inv[:, 1]
                vector.wait_ge(attn_lo, max(n - 1, 0) if isinstance(n, int) else n - 1)
                out = o_norm[:, g % 2].rearrange("p q (j d) -> p q j d", j=HG)
                vector.tensor_tensor(out, o[:, :, :, 0:DH],
                                     scale.rearrange("p q (j o) -> p q j o", o=1).broadcast_to([P, QT, HG, DH]),
                                     ALU.mult).then_inc(norm_out, 1)

            def step(b, g, first=False, maxima=True, has_next=True):
                for c in range(16):
                    if c == 4 and has_next:
                        rows_low(*ahead(b, g, 1), b * G + (g + 2))
                    if maxima:
                        row_max(*ahead(b, g, 2), c)
                    if c == 12 and not first:
                        normalise(*ahead(b, g, -1))

            for g in range(2):
                for c in range(16):
                    row_max(0, g, c)
                if g == 0:
                    rows_low(0, 0, 1)
            steps(vector, step)
            normalise(B - 1, G - 1)


def attention_tensors(nc, ctx, t):
    sb = lambda n, s, d: ctx.enter_context(nc.sbuf_tensor(n, s, d))
    t.ident_bf = sb("ident_bf", [P, P], BF16)
    t.mask_kq, t.mask_qk = sb("mask_kq", [P, P], BF16), sb("mask_qk", [P, P], BF16)
    t.cos, t.sin = sb("rope_cos", [P, S], F32), sb("rope_sin", [P, S], F32)
    t.w_proj = sb("w_proj", [P, 8, 2, KD, D], F16)
    t.w_rot = sb("w_rot", [P, 2, 2, KD, D], F16)
    t.w_router = sb("w_router_parts", [P, 2, KD, E], F16)
    t.bq, t.bk, t.g1 = sb("bq", [P, KD], F32), sb("bk", [P, KD], F32), sb("g1", [P, KD], F32)
    t.bv2, t.bo = sb("bv2", [P, 2, D], F32), sb("bo", [P, D], F32)
    t.head_mask = sb("head_mask_row", [P, H], F32)
    t.g2 = sb("g2", [P, 1, D], F32)
    t.attn = sb("attn", [P, 2, NT, D], F16)
    t.qx = sb("qx", [P, G, HG, S], F16)
    t.kx = sb("kx", [P, G, HG, S], F16)
    t.v_one = sb("v_one", [P, G, QT, HG, 32], F32)


def pipeline(engine, *stages):
    n = len(stages)

    def step(oldest, pair, parity):
        for ahead in range(n):
            if not isinstance(oldest, int) or 0 <= oldest + ahead < B:
                j = parity + ahead
                stages[n - 1 - ahead](oldest + ahead, j % 2, pair + j // 2)

    full = B - n + 1
    for oldest in range(1 - n, 0):
        step(oldest, oldest // 2, oldest % 2)
    with engine.Fori(0, full // 2) as pair:
        for parity in range(2):
            step(pair * 2 + parity, pair, parity)
    for oldest in range(full // 2 * 2, B):
        step(oldest, oldest // 2, oldest % 2)


def counted(engine, value):
    return value if isinstance(value, int) else engine.snap(engine.to_reg(value))


def before_last(b):
    return max(b - 1, 0) if isinstance(b, int) else b - 1


def project_out(nc, t, layer, x_res_dram, x_out_dram, part_dram):
    norm, route = layer == 0, layer == 1
    with ExitStack() as ctx:
        L = f"o{layer}_"
        sem = ctx.enter_context(stage_semaphores(nc, L))
        sb = lambda n, s, d: ctx.enter_context(nc.sbuf_tensor(L + n, s, d))
        ps = lambda n, s, d: ctx.enter_context(nc.psum_tensor(L + n, s, d))
        x_res = sb("x_res", [P, 2, QT, D], F32)
        aT = sb("aT", [P, 2, 2, KD, S], F16)
        x_new = sb("x_new", [P, 2, QT, D], F32)
        x_out = sb("x_out", [P, 2, QT, D], F32) if norm else x_new
        stats, mean_var = sb("stats", [P, 2, QT, 6], F32), sb("mean_var", [P, 2, QT, 2], F32)
        squares = sb("squares", [P, 2, QT, D], BF16)
        small = sb("small", [P, 2, 4, QT], F32)
        ms = sb("ms", [P, 2, QT], F32)
        constants = sb("constants", [P, 3, QT], F32)
        part = sb("part", [P, 2, QT, 2, D], F16)
        ps_aT = ps("ps_aT", [P, 2, KD, S], F16)
        ps_y = ps("ps_y", [P, 2, 2, D], F32)
        loaded, stored = [[sem(f"{n}{i}") for i in range(2)] for n in ("loaded", "stored")]
        aT_mm, aT_hi, aT_lo = map(sem, ("aT_mm", "aT_hi", "aT_lo"))
        y_mm, biased, summed, aggregated, var_out, rstd_out, x_done = map(sem, (
            "y_mm", "biased", "summed", "aggregated", "var_out", "rstd_out", "x_done"))
        squared, ms_out, rms_out, part_hi, part_lo, power, stat_out = map(sem, (
            "squared", "ms_out", "rms_out", "part_hi", "part_lo", "power", "stat_out"))
        if route:
            x_sum = sb("x_sum", [P, 2, QT, D], F32)
            normed = sb("normed", [P, 2, QT, D], F32)
            nT = sb("nT", [P, 2, KD, S], F16)
            ps_nT = ps("ps_nT", [P, 2, KD, S], F16)
            ps_l = ps("ps_l", [P, QT, E], F32)
            nT_mm, nT_hi, nT_lo, logits_mm, logits_out, added, normed_out = map(sem, (
                "nT_mm", "nT_hi", "nT_lo", "logits_mm", "logits_out", "added", "normed_out"))
        block = ctx.enter_context(nc.Block())
        tiles = lambda x: x.rearrange("(k p) n -> p k n", p=P)
        PQ = QT if norm else 1
        idle = lambda b, s, k: None

        def wait_x(engine, b, q):
            if norm:
                engine.wait_ge(x_done, b * QT + (q + 1))
            else:
                engine.wait_ge(summed, b * 2 + (q // 2 + 1))

        @block.sync
        def _(sync):
            def load(b, s, k):
                sync.wait_ge(summed if norm else added, before_last(b) * (2 if norm else 1))
                sync.dma_start(x_res[:, s], tiles(x_res_dram)[:, ds(b * QT, QT), :]).then_inc(loaded[s], 16)

            def store(b, s, k):
                if norm:
                    sync.wait_ge(x_done, b * QT + QT)
                else:
                    sync.wait_ge(added, b + 1)
                sync.dma_start(tiles(x_out_dram)[:, ds(b * QT, QT), :],
                               (x_out if norm else x_sum)[:, s]).then_inc(stored[s], 16)
                sync.wait_ge(part_hi, b * PQ + PQ)
                sync.wait_ge(part_lo, b * PQ + PQ)
                sync.dma_start(tiles(part_dram)[:, ds(b * QT, QT), :],
                               part[:, s].rearrange("p q h n -> p q (h n)")).then_inc(stored[s], 16)

            pipeline(sync, load, idle, idle, idle, store)
            for s in range(2):
                sync.wait_ge(stored[s], 32 * (B // 2))

        @block.gpsimd
        def _(pool):
            def bias(b, s, k):
                if norm:
                    pool.wait_ge(loaded[s], k * 16 + 16)
                    pool.tensor_tensor(x_res[:, s], x_res[:, s], t.bo[:].rearrange("p (o n) -> p o n", o=1)
                                       .broadcast_to([P, QT, D]), ALU.add).then_inc(biased, 1)

            def inverse_root(b, s, src, eps, mid, out, first_done, done):
                pool.tensor_tensor(small[:, s, mid], src, constants[:, eps], ALU.add).then_inc(first_done, 1)
                pool.wait_ge(first_done, b + 1)
                pool.tensor_tensor(small[:, s, out], small[:, s, mid], constants[:, 0], ALU.pow).then_inc(done, 1)

            def deviation(b, s, k):
                if norm:
                    pool.wait_ge(aggregated, b * QT + QT)
                    inverse_root(b, s, mean_var[:, s, :, 1], 1, 0, 1, var_out, rstd_out)

            def root_mean_square(b, s, k):
                if route:
                    pool.wait_ge(summed, b * 2 + 2)
                    pool.wait_ge(stored[s], k * 32)
                    pool.tensor_tensor(x_sum[:, s], x_out[:, s], x_res[:, s], ALU.add).then_inc(added, 1)
                pool.wait_ge(squared, b * QT + QT)
                pool.wait_ge(part_lo, before_last(b) * PQ)
                inverse_root(b, s, ms[:, s], 2, 2, 3, ms_out, rms_out)

            def low_parts(b, s, k):
                if route:
                    pool.wait_ge(part_hi, b + 1)
                    pool.tensor_tensor(part[:, s, :, 1], normed[:, s], part[:, s, :, 0], ALU.subtract).then_inc(part_lo, 1)

            for i, value in enumerate((-0.5, LN_EPS, RMS_EPS)):
                pool.memset(constants[:, i], value).then_inc(power, 1)
            pool.wait_ge(power, 3)
            pipeline(pool, bias, deviation, root_mean_square, low_parts)

        @block.tensor
        def _(pe):
            def turn(b, s, k):
                pe.wait_ge(aT_hi, b)
                pe.wait_ge(aT_lo, b)
                for hl in range(2):
                    for kd in range(KD):
                        for q in range(QT):
                            a = t.attn[:, hl, ds(b * QT + q, 1), kd * P:(kd + 1) * P]
                            mm = pe.transpose(ps_aT[:, hl, kd, q * P:(q + 1) * P],
                                              a.rearrange("p o n -> p (o n)"), t.ident16[:])
                mm.then_inc(aT_mm, 1)

            def product(b, s, k):
                pe.wait_ge(aT_hi, b + 1)
                pe.wait_ge(aT_lo, b + 1)
                for u in range(2):
                    pe.wait_ge(summed, b * 2)
                    for j in range(2):
                        n, q = 0, 2 * u + j
                        for wh, ah in ((0, 0), (1, 0), (0, 1)):
                            for kd in range(KD):
                                mm = pe.matmul(ps_y[:, u, j], aT[:, s, ah, kd, q * P:(q + 1) * P],
                                               t.w_proj[:, 4 * layer + 3, wh, kd, :], start=n == 0, stop=n == 5)
                                n += 1
                    mm.then_inc(y_mm, 1)

            def logits(b, s, k):
                pe.wait_ge(part_hi, b + 1)
                pe.wait_ge(part_lo, b + 1)
                pe.wait_ge(nT_hi, b)
                pe.wait_ge(nT_lo, b)
                for hl in range(2):
                    for kd in range(KD):
                        for q in range(QT):
                            mm = pe.transpose(ps_nT[:, hl, kd, q * P:(q + 1) * P],
                                              part[:, s, q, hl, kd * P:(kd + 1) * P], t.ident16[:])
                mm.then_inc(nT_mm, 1)
                pe.wait_ge(nT_hi, b + 1)
                pe.wait_ge(nT_lo, b + 1)
                pe.wait_ge(logits_out, b)
                for q in range(QT):
                    n = 0
                    for wh, nh in ((0, 0), (1, 0), (0, 1)):
                        for kd in range(KD):
                            mm = pe.matmul(ps_l[:, q], nT[:, nh, kd, q * P:(q + 1) * P], t.w_router[:, wh, kd, :],
                                           start=n == 0, stop=n == 5)
                            n += 1
                mm.then_inc(logits_mm, 1)

            pipeline(pe, turn, product, *([idle, idle, logits] if route else []))

        @block.scalar
        def _(act):
            def turned_high(b, s, k):
                act.wait_ge(aT_mm, b + 1)
                act.activation(aT[:, s, 0], ps_aT[:, 0], ACT.Copy).then_inc(aT_hi, 1)

            def squared_sums(b, s, k):
                for q in range(QT):
                    wait_x(act, b, q)
                    act.activation(squares[:, s, q], x_out[:, s, q], ACT.Square, scale=D ** -0.5,
                                   accum_out=ms[:, s, q:q + 1]).then_inc(squared, 1)

            def high_parts(b, s, k):
                act.wait_ge(stored[s], k * 32)
                if route:
                    act.wait_ge(nT_mm, before_last(b))
                    act.wait_ge(normed_out, b * QT + QT)
                    act.activation(part[:, s, :, 0], normed[:, s], ACT.Copy).then_inc(part_hi, 1)
                else:
                    act.wait_ge(rms_out, b + 1)
                    for q in range(QT):
                        act.activation(part[:, s, q, 0], x_out[:, s, q], ACT.Copy,
                                       scale=small[:, s, 3, q:q + 1]).then_inc(part_hi, 1)

            def logits(b, s, k):
                act.wait_ge(nT_mm, b + 1)
                act.activation(nT[:, 0], ps_nT[:, 0], ACT.Copy).then_inc(nT_hi, 1)

            pipeline(act, turned_high, idle, squared_sums, high_parts, *([logits] if route else []))

        @block.vector
        def _(vector):
            def turned_low(b, s, k):
                vector.wait_ge(aT_mm, b + 1)
                vector.tensor_copy(aT[:, s, 1], ps_aT[:, 1]).then_inc(aT_lo, 1)

            def residual(b, s, k):
                if norm:
                    vector.wait_ge(biased, b + 1)
                    vector.wait_ge(x_done, before_last(b) * QT)
                else:
                    vector.wait_ge(loaded[s], k * 16 + 16)
                    vector.wait_ge(added, before_last(b))
                    vector.wait_ge(squared, before_last(b) * QT)
                    vector.wait_ge(normed_out, before_last(b) * QT)
                for u in range(2):
                    vector.wait_ge(y_mm, b * 2 + u + 1)
                    vector.tensor_tensor(x_new[:, s, 2 * u:2 * u + 2], ps_y[:, u], x_res[:, s, 2 * u:2 * u + 2],
                                         ALU.add).then_inc(summed, 1)
                if not norm:
                    return
                for q in range(QT):
                    vector.wait_ge(summed, b * 2 + q // 2 + 1)
                    vector.bn_stats(stats[:, s, q], x_new[:, s, q]).then_inc(stat_out, 1)
                n = counted(vector, b * QT + QT)
                vector.wait_ge(stat_out, 1)
                vector.wait_ge(stat_out, n)
                for q in range(QT):
                    vector.bn_aggr(mean_var[:, s, q], stats[:, s, q]).then_inc(aggregated, 1)

            def layer_norm(b, s, k):
                if norm:
                    vector.wait_ge(rstd_out, b + 1)
                    vector.wait_ge(stored[s], k * 32)
                    for q in range(QT):
                        vector.tensor_scalar(x_out[:, s, q], x_new[:, s, q], mean_var[:, s, q, 0:1],
                                             small[:, s, 1, q:q + 1], ALU.subtract, ALU.mult).then_inc(x_done, 1)

            def parts(b, s, k):
                if route:
                    vector.wait_ge(rms_out, b + 1)
                    vector.wait_ge(part_lo, before_last(b))
                    for q in range(QT):
                        vector.scalar_tensor_tensor(normed[:, s, q], x_out[:, s, q], small[:, s, 3, q:q + 1],
                                                    t.g2[:, 0], ALU.mult, ALU.mult).then_inc(normed_out, 1)
                else:
                    for q in range(QT):
                        vector.wait_ge(part_hi, b * QT + q + 1)
                        vector.scalar_tensor_tensor(part[:, s, q, 1], x_out[:, s, q], small[:, s, 3, q:q + 1],
                                                    part[:, s, q, 0], ALU.mult, ALU.subtract).then_inc(part_lo, 1)

            def logits(b, s, k):
                vector.wait_ge(nT_mm, b + 1)
                vector.tensor_copy(nT[:, 1], ps_nT[:, 1]).then_inc(nT_lo, 1)
                vector.wait_ge(logits_mm, b + 1)
                vector.tensor_copy(t.logits[:, ds(b * QT, QT), :], ps_l[:]).then_inc(logits_out, 1)

            pipeline(vector, turned_low, residual, layer_norm, parts, *([logits] if route else []))


def route_tokens(nc, t):
    with ExitStack() as ctx:
        sem = ctx.enter_context(stage_semaphores(nc, "r_"))
        sb = lambda n, s, d: ctx.enter_context(nc.sbuf_tensor("r_" + n, s, d))
        ps = lambda n, s, d: ctx.enter_context(nc.psum_tensor("r_" + n, s, d))
        rank = sb("rank", [P, NT, E], F32)
        best = sb("best", [P, 2, NT], F32)
        hit = sb("hit", [P, NT, E], F32)
        pick = sb("pick", [P, NT], F32)
        chosen = sb("chosen", [P, 2, NT, E], F32)
        left = sb("left", [P, NT, E], F32)
        both = sb("both", [P, NT, E], F32)
        gap, e_gap, one_more = sb("gap", [P, NT], F32), sb("e_gap", [P, NT], F32), sb("one_more", [P, NT], F32)
        earlier, ones = sb("earlier", [P, P], F32), sb("ones", [P, P], F32)
        totals = sb("totals", [P, E, NT], F32)
        keep = sb("keep", [P, E, NT], F32)
        run = sb("run", [P, E, NT], F32)
        count_i, padded_i = sb("count_i", [P, E], I32), sb("padded_i", [P, E], I32)
        padded, ends, starts = sb("padded", [P, E], F32), sb("ends", [P, E], F32), sb("starts", [P, E], F32)
        before, row = sb("before", [P, E, NT], F32), sb("row", [P, NT, E], F32)
        mine = sb("mine", [P, NT, E], F32)
        pos, pos_i = sb("pos", [P, 2, NT], F32), sb("pos_i", [P, 2, NT], I32)
        slot_i = sb("slot_i", [P, HI], I32)
        own = sb("own", [P, HI], F32)
        tile_start = sb("tile_start", [P, MT, 1], F32)
        passed, expert = sb("passed", [P, MT, E], F32), sb("expert", [P, MT], F32)
        hi_i, lo_i = sb("hi_i", [P, 2 * NT], I32), sb("lo_i", [P, 2 * NT], I32)
        hi, lo = sb("hi", [P, 2 * NT, 1], F32), sb("lo", [P, 2 * NT, 1], F32)
        count_hi, count_lo = sb("count_hi", [P, 1, HI], F32), sb("count_lo", [P, 1, P], F32)
        hot_hi = sb("hot_hi", [P, 2 * NT, HI], BF16)
        hot_lo = sb("hot_lo", [P, 2 * NT, P], BF16)
        by_tile = sb("by_tile", [P, 2 * NT, HI], BF16)
        by_row = hot_hi
        tile_no, row_no = sb("tile_no", [P, 2 * NT, 1], F32), sb("row_no", [P, 1], F32)
        inverse = sb("inverse", [P, P], F32)
        ps_c = ps("ps_c", [P, 2, NT * E], F32)
        ps_i = ps("ps_i", [P, 2, P], F32)
        ps_t = ps("ps_t", [P, P], F32)
        made, did, exp_done, totalled, hot_done, by_row_done, inverse_mm, turned = map(sem, (
            "made", "did", "exp_done", "totalled", "hot_done", "by_row_done", "inverse_mm", "turned"))
        hot_hi_done, by_tile_done, w_loaded, padded_out = map(sem, (
            "hot_hi_done", "by_tile_done", "w_loaded", "weights_padded"))
        ready_gap, ready_both, ready_inverse = sem("ready_gap"), sem("ready_both"), sem("ready_inverse")
        block = ctx.enter_context(nc.Block())
        flat = lambda x: x.rearrange("p a b -> p (a b)")
        wide = lambda x, n: x.rearrange("p (a o) -> p a o", o=1).broadcast_to([P, x.shape[1], n])

        @block.gpsimd
        def _(pool):
            iota = lambda out, pattern, base, mult: pool.iota(
                out, pattern, base=base, channel_multiplier=mult,
                allow_small_or_imprecise_dtypes=True).then_inc(made, 1)
            iota(rank[:], [[0, NT], [-1, E]], E, 0)
            iota(tile_start[:], [[SLOT, MT]], 0, 0)
            iota(count_hi[:], [[1, HI]], 0, 0)
            iota(count_lo[:], [[1, P]], 0, 0)
            iota(tile_no[:], [[1, 2 * NT]], 1, 0)
            iota(row_no[:], [[0, 1]], 0, 1)
            iota(own[:], [[P, HI]], P - SPARE, 1)
            pool.memset(ones[:], 1.0).then_inc(made, 1)
            pool.memset(keep[:], 1.0).then_inc(made, 1)
            pool.wait_ge(made, 9)
            pool.affine_select(out=earlier[:], in_=ones[:], pattern=[[1, P]], compare_op=ALU.is_gt, fill=0.0,
                               base=0, channel_multiplier=-1).then_inc(made, 1)
            pool.memset(keep[:, :, 0:1], 0.0).then_inc(made, 1)
            pool.wait_ge(made, 11)
            pool.wait_ge(hot_hi_done, 1)
            pool.tensor_tensor(by_tile[:], hot_hi[:], tile_no[:].broadcast_to([P, 2 * NT, HI]),
                               ALU.mult).then_inc(by_tile_done, 1)

        MADE = 11

        @block.sync
        def _(sync):
            n = 0
            for e in range(E):
                for hl in range(2):
                    for kind in range(2):
                        sync.dma_start(t.w_up[:, e, hl, :, kind, 0:F],
                                       t.w_dram[kind][hl][e].rearrange("(k p) f -> p k f", p=P)).then_inc(w_loaded, 16)
                    down = t.w_dram[2][hl][e]
                    sync.dma_start(t.w_down[:, e, hl, 0:FT - 1],
                                   down[0:(FT - 1) * P].rearrange("(k p) n -> p k n", p=P)).then_inc(w_loaded, 16)
                    sync.dma_start(t.w_down[0:FR, e, hl, FT - 1], down[(FT - 1) * P:F]).then_inc(w_loaded, 16)
                    n += 4 * 16
            sync.wait_ge(w_loaded, n)

        @block.scalar
        def _(act):
            act.wait_ge(ready_gap, 1)
            act.activation(e_gap[:], gap[:], ACT.Exp).then_inc(exp_done, 1)
            act.wait_ge(by_tile_done, 1)
            act.activation(flat(by_row[:]), flat(hot_hi[:]), ACT.Copy, scale=row_no[:, 0:1]).then_inc(by_row_done, 1)

        @block.tensor
        def _(pe):
            pe.wait_ge(made, MADE)
            pe.wait_ge(ready_both, 1)
            pe.matmul(ps_c[:, 0], earlier[:], flat(both[:]), start=True, stop=True)
            pe.matmul(ps_c[:, 1], ones[:], flat(both[:]), start=True, stop=True,
                      skip_group_check=True).then_inc(totalled, 1)
            pe.wait_ge(hot_done, 1)
            pe.wait_ge(by_tile_done, 1)
            for v, values in enumerate((by_tile, by_row)):
                if v == 1:
                    pe.wait_ge(by_row_done, 1)
                for n in range(2 * NT):
                    mm = pe.matmul(ps_i[0:HI, v], values[:, n, :], hot_lo[:, n, :], start=n == 0,
                                   stop=n == 2 * NT - 1, skip_group_check=True)
            mm.then_inc(inverse_mm, 1)
            pe.wait_ge(ready_inverse, 1)
            pe.transpose(ps_t[:, 0:HI], inverse[0:HI, :], t.ident32[0:HI, 0:HI]).then_inc(turned, 1)

        @block.vector
        def _(vector):
            done = [0]

            def chained(ins):
                done[0] += 1
                ins.then_inc(did, 1)
                vector.wait_ge(did, done[0])

            for part in (t.w_up[:, :, :, :, :, F:].rearrange("p e h k g f -> p (e h k g) f"),
                         t.w_down[FR:P, :, :, FT - 1].rearrange("p e h n -> p (e h) n")):
                vector.memset(part, 0.0).then_inc(padded_out, 1)
            vector.wait_ge(made, MADE)
            vector.wait_ge(padded_out, 2)
            source = t.logits
            for c in range(2):
                chained(vector.tensor_reduce(best[:, c], source[:], AX.X, ALU.max))
                chained(vector.tensor_tensor(hit[:], source[:], wide(best[:, c], E), ALU.is_equal))
                chained(vector.tensor_tensor(hit[:], hit[:], rank[:], ALU.mult))
                chained(vector.tensor_reduce(pick[:], hit[:], AX.X, ALU.max))
                chained(vector.tensor_tensor(chosen[:, c], rank[:], wide(pick[:], E), ALU.is_equal))
                if c == 0:
                    chained(vector.scalar_tensor_tensor(flat(left[:]), flat(chosen[:, 0]), NEG, flat(source[:]),
                                                        ALU.mult, ALU.add))
                    source = left
            vector.tensor_tensor(gap[:], best[:, 1], best[:, 0], ALU.subtract).then_inc(ready_gap, 1)
            vector.tensor_tensor(both[:], chosen[:, 0], chosen[:, 1], ALU.add).then_inc(ready_both, 1)
            vector.wait_ge(exp_done, 1)
            chained(vector.tensor_scalar(one_more[:], e_gap[:], 1.0, None, ALU.add))
            chained(vector.reciprocal(t.weight[:, 0], one_more[:]))
            chained(vector.tensor_tensor(t.weight[:, 1], t.weight[:, 0], e_gap[:], ALU.mult))
            vector.wait_ge(totalled, 1)
            per_expert = ps_c[:, 1].rearrange("p (k e) -> p e k", e=E)
            chained(vector.tensor_copy(totals[:], per_expert))
            chained(vector.tensor_tensor_scan(flat(run[:]), flat(keep[:]), flat(totals[:]), 0.0, ALU.mult, ALU.add))
            chained(vector.tensor_scalar(count_i[:], run[:, :, NT - 1], float(SLOT - 1), None, ALU.add))
            shift = SLOT.bit_length() - 1
            chained(vector.tensor_scalar(padded_i[:], count_i[:], shift, shift, ALU.logical_shift_right,
                                         ALU.logical_shift_left))
            chained(vector.tensor_copy(padded[:], padded_i[:]))
            chained(vector.tensor_tensor_scan(ends[:], ones[:, 0:E], padded[:], 0.0, ALU.mult, ALU.add))
            chained(vector.tensor_tensor(starts[:], ends[:], padded[:], ALU.subtract))
            chained(vector.tensor_tensor(before[:], run[:], totals[:], ALU.subtract))
            chained(vector.tensor_tensor(before[:], before[:], wide(starts[:], NT), ALU.add))
            chained(vector.tensor_tensor(row[:], ps_c[:, 0].rearrange("p (k e) -> p k e", e=E),
                                         before[:].rearrange("p e k -> p k e"), ALU.add))
            for c in range(2):
                chained(vector.tensor_tensor(mine[:], row[:], chosen[:, c], ALU.mult))
                chained(vector.tensor_reduce(pos[:, c], mine[:], AX.X, ALU.add))
            chained(vector.tensor_copy(pos_i[:], pos[:]))
            flat_pos = pos_i[:].rearrange("p c k -> p (c k)")
            chained(vector.tensor_scalar(lo_i[:], flat_pos, P - 1, None, ALU.bitwise_and))
            chained(vector.tensor_scalar(hi_i[:], flat_pos, 7, None, ALU.logical_shift_right))
            chained(vector.tensor_copy(hi[:, :, 0], hi_i[:]))
            vector.tensor_tensor(hot_hi[:], hi[:].broadcast_to([P, 2 * NT, HI]),
                                 count_hi[:].broadcast_to([P, 2 * NT, HI]), ALU.is_equal).then_inc(hot_hi_done, 1)
            chained(vector.tensor_copy(lo[:, :, 0], lo_i[:]))
            vector.tensor_tensor(hot_lo[:], lo[:].broadcast_to([P, 2 * NT, P]),
                                 count_lo[:].broadcast_to([P, 2 * NT, P]), ALU.is_equal).then_inc(hot_done, 1)
            chained(vector.tensor_tensor(passed[:], ends[:].rearrange("p (o e) -> p o e", o=1)
                                         .broadcast_to([P, MT, E]), tile_start[:].broadcast_to([P, MT, E]), ALU.is_le))
            chained(vector.tensor_reduce(expert[:], passed[:], AX.X, ALU.add))
            chained(vector.tensor_scalar(t.tile_expert[:], expert[:], float(E - 1), None, ALU.min))
            vector.wait_ge(inverse_mm, 1)
            chained(vector.tensor_copy(inverse[0:HI, :], ps_i[0:HI, 1]))
            vector.scalar_tensor_tensor(inverse[0:HI, :], ps_i[0:HI, 0], float(P), inverse[0:HI, :],
                                        ALU.mult, ALU.add).then_inc(ready_inverse, 1)
            vector.wait_ge(turned, 1)
            chained(vector.scalar_tensor_tensor(own[:], ps_t[:, 0:HI], 1.0, own[:], ALU.is_lt, ALU.mult))
            chained(vector.scalar_tensor_tensor(t.slot_of_row[:], ps_t[:, 0:HI], float(SPARE - P), own[:],
                                                ALU.add, ALU.add))
            chained(vector.tensor_scalar(slot_i[:], ps_t[:, 0:HI], float(2 * T - P), None, ALU.add))
            chained(vector.tensor_scalar(t.token_of_row[:], slot_i[:], T - 1, None, ALU.bitwise_and))


def expert_tiles(nc, t):
    with ExitStack() as ctx:
        sem = ctx.enter_context(stage_semaphores(nc, "e_"))
        pair = lambda n: [sem(f"{n}{i}") for i in range(2)]
        sb = lambda n, s, d: ctx.enter_context(nc.sbuf_tensor("e_" + n, s, d))
        ps = lambda n, s, d: ctx.enter_context(nc.psum_tensor("e_" + n, s, d))
        w_up, w_down = t.w_up, t.w_down
        x = sb("x", [P, 2, 2, 2 * D], F16)
        take, put = sb("take", [P, 2, 2], I32), sb("put", [P, 2, 2], I32)
        xT = sb("xT", [P, 2, 2, KD, SLOT], F16)
        gate = sb("gate", [P, 2, 2, SLOT], F32)
        h32 = sb("h32", [P, 2, 2, SLOT], F32)
        h = sb("h", [P, 2, 2, FT, SLOT], F16)
        y = sb("y", [P, 2, 2, D], F32)
        ps_xT = ps("ps_xT", [P, 2, KD, SLOT], F16)
        ps_gu = ps("ps_gu", [P, 2, 2, 2, SLOT], F32)
        ps_y = ps("ps_y", [P, 2, 2, D], F32)
        cleared = sem("indices_cleared")
        gathered, taken, placed, stored, xT_mm, xT_out, y_mm, y_out = map(pair, (
            "gathered", "taken", "placed", "stored", "xT_mm", "xT_out", "y_mm", "y_out"))
        gu_mm, gate_out, h_out, h_hi, h_lo = map(pair, ("gu_mm", "gate_out", "h_out", "h_hi", "h_lo"))
        block = ctx.enter_context(nc.Block())
        FG = FT // 2
        LAST = MT // 2 - 1

        @block.gpsimd
        def _(pool):
            pool.memset(take[:], 0).then_inc(cleared, 1)
            pool.memset(put[:], 0).then_inc(cleared, 1)

            def gather(r, s):
                used, copied = counted(pool, r * 32), counted(pool, r + 1)
                pool.wait_ge(cleared, 2)
                pool.wait_ge(gathered[s], used)
                pool.tensor_copy(take[:, s], t.token_of_row[:, ds(r * 4 + 2 * s, 2)]).then_inc(taken[s], 1)
                pool.wait_ge(cleared, 2)
                pool.wait_ge(taken[s], copied)
                pool.wait_ge(xT_mm[s], r)
                for half in range(2):
                    pool.indirect_dma_start(x[:, s, half], None, t.part_dram,
                                            bass.IndirectOffsetOnAxis(ap=take[:, s, half:half + 1], axis=0)
                                            ).then_inc(gathered[s], 16)

            def scatter(r, s):
                used, copied = counted(pool, r * 32), counted(pool, r + 1)
                pool.wait_ge(cleared, 2)
                pool.wait_ge(stored[s], used)
                pool.tensor_copy(put[:, s], t.slot_of_row[:, ds(r * 4 + 2 * s, 2)]).then_inc(placed[s], 1)
                pool.wait_ge(cleared, 2)
                pool.wait_ge(placed[s], copied)
                pool.wait_ge(y_out[s], copied)
                for half in range(2):
                    pool.indirect_dma_start(t.y_dram, bass.IndirectOffsetOnAxis(ap=put[:, s, half:half + 1], axis=0),
                                            y[:, s, half], None).then_inc(stored[s], 16)

            for s in range(2):
                gather(0, s)
            with pool.Fori(0, LAST) as r:
                for s in range(2):
                    gather(r + 1, s)
                    scatter(r, s)
            gather(LAST + 1, 0)
            for r, s in ((LAST, 0), (LAST, 1), (LAST + 1, 0)):
                scatter(r, s)
            for s in range(2):
                pool.wait_ge(stored[s], 32 * (LAST + 2 - s))

        @block.tensor
        def _(pe):
            def turn(r, s):
                pe.wait_ge(gathered[s], r * 32 + 32)
                pe.wait_ge(xT_out[1 - s], r + s)
                for hl in range(2):
                    for k in range(KD):
                        for half in range(2):
                            mm = pe.transpose(ps_xT[:, hl, k, half * P:(half + 1) * P],
                                              x[:, s, half, hl * D + k * P:hl * D + (k + 1) * P], t.ident16[:])
                mm.then_inc(xT_mm[s], 1)

            def tile(r, s, following):
                j = r * 2 + s
                e = pe.value_load(t.tile_expert[0:1, ds(j, 1)], min_val=0, max_val=E - 1)
                pe.wait_ge(xT_out[s], r + 1)
                for i in range(FG):
                    c = s * FG + i
                    bank, turns = c % 2, r * FG + c // 2
                    pe.wait_ge(h_out[bank], turns)
                    for m in range(2):
                        f = 2 * i + m
                        for kind in range(2):
                            n = 0
                            for wh, xh in ((0, 0), (0, 1), (1, 0)):
                                for k in range(KD):
                                    w = w_up[:, :, wh, k, kind, f * P:(f + 1) * P]
                                    mm = pe.matmul(ps_gu[:, bank, kind, m],
                                                   w[:, ds(e, 1)].rearrange("p o f -> p (o f)"),
                                                   xT[:, s, xh, k, :], start=n == 0, stop=n == 5)
                                    n += 1
                    mm.then_inc(gu_mm[bank], 1)
                following()
                pe.wait_ge(y_out[s], r)
                for half in range(2):
                    c = 0
                    for f in range(FT):
                        if half == 0 and f % 2 == 0:
                            g = s * FG + f // 2
                            pe.wait_ge(h_hi[g % 2], r * FG + (g // 2 + 1))
                            pe.wait_ge(h_lo[g % 2], r * FG + (g // 2 + 1))
                        for hh, wh in ((0, 0), (0, 1), (1, 0)):
                            w = w_down[:, :, wh, f, :]
                            mm = pe.matmul(ps_y[:, s, half], h[:, s, hh, f, half * P:(half + 1) * P],
                                           w[:, ds(e, 1)].rearrange("p o f -> p (o f)"),
                                           start=c == 0, stop=c == 3 * FT - 1)
                            c += 1
                mm.then_inc(y_mm[s], 1)

            turn(0, 0)
            with pe.Fori(0, LAST) as r:
                tile(r, 0, lambda: turn(r, 1))
                tile(r, 1, lambda: turn(r + 1, 0))
            tile(LAST, 0, lambda: turn(LAST, 1))
            tile(LAST, 1, lambda: turn(LAST + 1, 0))
            tile(LAST + 1, 0, lambda: None)

        @block.scalar
        def _(act):
            def move_x(r, s):
                act.wait_ge(xT_mm[s], r + 1)
                act.activation(xT[:, s], ps_xT[:], ACT.Copy).then_inc(xT_out[s], 1)

            move_x(0, 0)

            def tile(r, s, following):
                for i in range(FG):
                    c = s * FG + i
                    bank, turns = c % 2, r * FG + (c // 2 + 1)
                    act.wait_ge(gu_mm[bank], turns)
                    act.activation(gate[:, bank], ps_gu[:, bank, 0], ACT.Silu).then_inc(gate_out[bank], 1)
                    act.wait_ge(h_out[bank], turns)
                    act.activation(h[:, s, 0, 2 * i:2 * i + 2], h32[:, bank], ACT.Copy).then_inc(h_hi[bank], 1)
                    if i == FG - 1:
                        following()

            with act.Fori(0, LAST) as r:
                tile(r, 0, lambda: move_x(r, 1))
                tile(r, 1, lambda: move_x(r + 1, 0))
            tile(LAST, 0, lambda: move_x(LAST, 1))
            tile(LAST, 1, lambda: move_x(LAST + 1, 0))
            tile(LAST + 1, 0, lambda: None)

        @block.vector
        def _(vector):
            def tile(r, s):
                for i in range(FG):
                    c = s * FG + i
                    bank, turns = c % 2, r * FG + c // 2
                    vector.wait_ge(gate_out[bank], turns + 1)
                    vector.wait_ge(h_hi[bank], turns)
                    vector.tensor_tensor(h32[:, bank], gate[:, bank], ps_gu[:, bank, 1],
                                         ALU.mult).then_inc(h_out[bank], 1)
                    vector.wait_ge(h_hi[bank], turns + 1)
                    vector.tensor_tensor(h[:, s, 1, 2 * i:2 * i + 2], h32[:, bank], h[:, s, 0, 2 * i:2 * i + 2],
                                         ALU.subtract).then_inc(h_lo[bank], 1)
                vector.wait_ge(y_mm[s], r + 1)
                vector.wait_ge(stored[s], r * 32)
                vector.tensor_copy(y[:, s], ps_y[:, s]).then_inc(y_out[s], 1)

            with vector.Fori(0, MT // 2) as r:
                for s in range(2):
                    tile(r, s)
            tile(MT // 2, 0)


def combine(nc, t, out):
    with ExitStack() as ctx:
        sem = ctx.enter_context(stage_semaphores(nc, "c_"))
        pair = lambda n: [sem(f"{n}{i}") for i in range(2)]
        sb = lambda n, s, d: ctx.enter_context(nc.sbuf_tensor("c_" + n, s, d))
        h = sb("h", [P, 2, QT, D], F32)
        rows = sb("rows", [P, 2, 2, QT, D], F32)
        z = sb("z", [P, 2, QT, 2, D], F32)
        res = sb("res", [P, 2, QT, D], F32)
        stats, mean_var = sb("stats", [P, 2, QT, 6], F32), sb("mean_var", [P, 2, QT, 2], F32)
        small = sb("small", [P, 2, 4, QT], F32)
        constants = sb("constants", [P, 3, QT], F32)
        loaded, stored = pair("loaded"), pair("stored")
        first, summed, stat_out, aggregated, power, mid_out, rstd_out, shift_out, done = map(sem, (
            "first", "summed", "stat_out", "aggregated", "power", "mid_out", "rstd_out", "shift_out", "done"))
        block = ctx.enter_context(nc.Block())
        tiles = lambda x: x.rearrange("(k p) n -> p k n", p=P)
        idle = lambda b, s, k: None

        @block.sync
        def _(sync):
            def load(b, s, k):
                sync.wait_ge(summed, before_last(b) * QT)
                sync.dma_start(h[:, s], tiles(t.h_dram)[:, ds(b * QT, QT), :]).then_inc(loaded[s], 16)
                for c in range(2):
                    sync.dma_start(rows[:, s, c], tiles(t.y_dram)[:, ds(b * QT + (HI + c * NT), QT), :]
                                   ).then_inc(loaded[s], 16)

            def store(b, s, k):
                sync.wait_ge(done, b * QT + QT)
                sync.dma_start(tiles(out)[:, ds(b * QT, QT), :], res[:, s]).then_inc(stored[s], 16)

            pipeline(sync, load, idle, store)
            for s in range(2):
                sync.wait_ge(stored[s], 16 * (B // 2))

        @block.gpsimd
        def _(pool):
            for i, value in enumerate((-0.5, LN_EPS, -1.0)):
                pool.memset(constants[:, i], value).then_inc(power, 1)
            pool.wait_ge(power, 3)

            def deviation(b, s, k):
                pool.wait_ge(aggregated, b * QT + QT)
                pool.wait_ge(done, before_last(b) * QT)
                mean, var = mean_var[:, s, :, 0], mean_var[:, s, :, 1]
                pool.tensor_tensor(small[:, s, 0], var, constants[:, 1], ALU.add).then_inc(mid_out, 1)
                pool.tensor_tensor(small[:, s, 2], mean, constants[:, 2], ALU.mult).then_inc(mid_out, 1)
                pool.wait_ge(mid_out, b * 2 + 2)
                pool.tensor_tensor(small[:, s, 1], small[:, s, 0], constants[:, 0], ALU.pow).then_inc(rstd_out, 1)
                pool.wait_ge(rstd_out, b + 1)
                pool.tensor_tensor(small[:, s, 3], small[:, s, 2], small[:, s, 1], ALU.mult).then_inc(shift_out, 1)

            pipeline(pool, deviation, idle)

        @block.vector
        def _(vector):
            def weigh(b, s, k):
                vector.wait_ge(loaded[s], k * 48 + 48)
                vector.wait_ge(done, before_last(b) * QT)
                for c, ready in enumerate((first, summed)):
                    for q in range(QT):
                        w = t.weight[:, :, ds(b * QT + q, 1)]
                        if c == 1:
                            vector.wait_ge(first, b * QT + (q + 1))
                        vector.scalar_tensor_tensor(z[:, s, q, c], rows[:, s, c, q], w[:, c],
                                                    z[:, s, q, 0] if c else h[:, s, q],
                                                    ALU.mult, ALU.add).then_inc(ready, 1)
                for q in range(QT):
                    vector.wait_ge(summed, b * QT + (q + 1))
                    vector.bn_stats(stats[:, s, q], z[:, s, q, 1]).then_inc(stat_out, 1)
                n = counted(vector, b * QT + QT)
                vector.wait_ge(stat_out, 1)
                vector.wait_ge(stat_out, n)
                for q in range(QT):
                    vector.bn_aggr(mean_var[:, s, q], stats[:, s, q]).then_inc(aggregated, 1)

            pipeline(vector, weigh, idle)

        @block.scalar
        def _(act):
            def normalise(b, s, k):
                act.wait_ge(rstd_out, b + 1)
                act.wait_ge(shift_out, b + 1)
                act.wait_ge(stored[s], k * 16)
                for q in range(QT):
                    act.activation(res[:, s, q], z[:, s, q, 1], ACT.Identity, bias=small[:, s, 3, q:q + 1],
                                   scale=small[:, s, 1, q:q + 1]).then_inc(done, 1)

            pipeline(act, idle, normalise)


def feed_forward_kernel(nc, a, out):
    with ExitStack() as top:
        dram = lambda n, s, d: nc.dram_tensor(n, s, d).ap()
        sb = lambda n, s, d: top.enter_context(nc.sbuf_tensor(n, s, d))
        t = Tensors()
        t.qk_dram = [dram(f"qk_{hl}", [P, 4, T], F16) for hl in ("hi", "lo")]
        t.v_dram, x1_dram, t.h_dram = dram("v", [T, D], F32), dram("x1", [T, D], F32), dram("h", [T, D], F32)
        t.part_dram = dram("part", [T, 2 * D], F16)
        t.y_dram = dram("y", [SPARE + 2 * T, D], F32)
        t.w_dram = [[dram(f"w_{name}_{hl}", [E, *shape], F16) for hl in ("hi", "lo")]
                    for name, shape in (("gate", (D, F)), ("up", (D, F)), ("down", (F, D)))]
        t.ident32, t.ident16 = sb("ident32", [P, P], F32), sb("ident16", [P, P], F16)
        t.logits, t.weight = sb("logits", [P, NT, E], F32), sb("weight", [P, 2, NT], F32)
        t.token_of_row, t.slot_of_row = sb("token_of_row", [P, HI], I32), sb("slot_of_row", [P, HI], I32)
        t.tile_expert = sb("tile_expert", [P, MT], I32)
        with ExitStack() as ctx:
            attention_tensors(nc, ctx, t)
            row = lambda x: x.rearrange("(o n) -> o n", o=1).broadcast_to([P, x.shape[0]])
            setup(nc, t, [a["A_W" + k] for k in "qkvo"] + [a["F_w" + k] for k in "qkvo"], a["w_router"],
                  [(t.bq[:], a["bq"]), (t.bk[:], a["bk"]), (t.g1[:], a["g1"]), (t.g2[:, 0], row(a["g2"])),
                   (t.bv2[:, 0], row(a["bv"])), (t.bv2[:, 1], row(a["bv"])), (t.bo[:], row(a["bo"])),
                   (t.head_mask[:], row(a["head_mask"])), (t.cos[:], a["cos"]), (t.sin[:], a["sin"])])
            project_qkv(nc, t, 0, lambda b: a["xT"].rearrange("(k p) n -> p k n", p=P)[:, :, ds(b * S, S)])
            attend(nc, t, 0, (a["wg"], a["wu"], a["wd"]))
            project_out(nc, t, 0, a["x"], x1_dram, t.part_dram)
            project_qkv(nc, t, 1, lambda b: t.part_dram.rearrange("(k p) n -> p k n", p=P)[:, ds(b * QT, QT), :])
            attend(nc, t, 1)
            project_out(nc, t, 1, x1_dram, t.h_dram, t.part_dram)
        with ExitStack() as ctx:
            t.w_up = ctx.enter_context(nc.sbuf_tensor("w_up", [P, E, 2, KD, 2, FT * P], F16))
            t.w_down = ctx.enter_context(nc.sbuf_tensor("w_down", [P, E, 2, FT, D], F16))
            route_tokens(nc, t)
            expert_tiles(nc, t)
        combine(nc, t, out)


def kernel(**inputs):
    import concourse.bacc as bacc
    from concourse.bass_utils import run_bass_kernel_spmd

    given = {k: np.asarray(v) for k, v in inputs.items()}
    columns = lambda x: np.ascontiguousarray(x.reshape(KD, P).T)
    arrays = {"x": given["L0_attn_x"].reshape(T, D)}
    arrays["xT"] = np.ascontiguousarray(arrays["x"].T)
    for k in "qkvo":
        arrays["A_W" + k] = np.ascontiguousarray(given["L0_attn_W" + k].T)
        arrays["F_w" + k] = given["L0_ffn_w" + k]
    for k in ("bv", "bo", "head_mask"):
        arrays[k] = given["L0_attn_" + k]
    for k in ("w_router", "wg", "wu", "wd"):
        arrays[k] = given["L0_ffn_" + k]
    arrays["bq"], arrays["bk"] = columns(given["L0_attn_bq"]), columns(given["L0_attn_bk"])
    arrays["g1"], arrays["g2"] = columns(given["L0_ffn_g1"]), given["L0_ffn_g2"]
    inv_freq = 1.0 / 10000.0 ** (np.arange(0, DH, 2, dtype=np.float32) / DH)
    angle = np.einsum("i,j->ij", np.arange(S, dtype=np.float32), inv_freq)
    angle = np.tile(np.concatenate([angle, angle], axis=-1), (1, P // DH)).T
    arrays["cos"] = np.ascontiguousarray(np.cos(angle), np.float32)
    arrays["sin"] = np.ascontiguousarray(np.sin(angle), np.float32)
    nc = bacc.Bacc("TRN2", target_bir_lowering=False, num_devices=1)
    a = {n: nc.dram_tensor("in_" + n, v.shape, mybir.dt.from_np(v.dtype), kind="ExternalInput").ap()
         for n, v in arrays.items()}
    out = nc.dram_tensor("out", [T, D], F32, kind="ExternalOutput").ap()
    feed_forward_kernel(nc, a, out)
    r = run_bass_kernel_spmd(nc, [{"in_" + n: v for n, v in arrays.items()}], core_ids=[0])
    return np.asarray(r.results[0]["out"]).reshape(B, S, D)
```

```python
from contextlib import ExitStack, contextmanager

import numpy as np
import concourse.bass as bass
from concourse import mybir

ALU = mybir.AluOpType
ACT = mybir.ActivationFunctionType
AX = mybir.AxisListType
F32 = mybir.dt.float32
F16 = mybir.dt.float16
BF16 = mybir.dt.bfloat16
I32 = mybir.dt.int32
ds = bass.ds

P = 128
B, S, D = 8, 512, 256
H, DH = 16, 16
T = B * S
QT = S // P
NT = T // P
KD = D // P
G, HG = 4, 4
E, F = 8, 704
FT = (F + P - 1) // P
FR = F - (FT - 1) * P
SLOT = 256
MT = 2 * T // SLOT + E - 1
SPARE = MT * SLOT
HI = SPARE // P
WP = E * D * F // P // B
LN_EPS, RMS_EPS = 1e-5, 1e-6
MAXROW = P - 2
NEG = -1.0e30


ORDER = "SMSMMMSSW"


class Tensors:
    pass


@contextmanager
def stage_semaphores(nc, prefix):
    handles = []

    def sem(name):
        handles.append(nc.alloc_semaphore(name=prefix + name))
        return handles[-1]

    yield sem
    nc.clear_and_free_semaphores(handles)
    nc.all_engine_barrier()


def setup(nc, t, w_in, router_in, vec_in):
    with ExitStack() as ctx:
        sem = ctx.enter_context(stage_semaphores(nc, ""))
        w32 = ctx.enter_context(nc.sbuf_tensor("w32", [P, 8, KD, D], F32))
        r32 = ctx.enter_context(nc.sbuf_tensor("r32", [P, KD, E], F32))
        scale = ctx.enter_context(nc.sbuf_tensor("w_scale", [P, 8, KD], F32))
        loaded, filled, scaled, split_hi, split_lo, rotated = map(sem, (
            "setup_loaded", "setup_filled", "weight_scale_ready", "weights_hi", "weights_lo", "weights_rotated"))
        w_loaded = [sem(f"weight_loaded{j}") for j in range(9)]
        others_loaded = sem("others_loaded")
        block = ctx.enter_context(nc.Block())
        n_first = 2

        @block.sync
        def _(sync):
            for dst, src in vec_in[:n_first]:
                sync.dma_start(dst, src).then_inc(loaded, 16)
            for j, w in enumerate(w_in):
                sync.dma_start(w32[:, j], w.rearrange("(k p) n -> p k n", p=P)).then_inc(w_loaded[j], 16)
            sync.dma_start(r32[:], router_in.rearrange("(k p) n -> p k n", p=P)).then_inc(w_loaded[8], 16)
            for dst, src in vec_in[n_first:]:
                sync.dma_start(dst, src).then_inc(others_loaded, 16)
            sync.wait_ge(others_loaded, 16 * len(vec_in[n_first:]))
            sync.wait_ge(split_lo, 9 * KD)

        @block.gpsimd
        def _(pool):
            pool.memset(t.ident32[:], 0.0).then_inc(filled, 1)
            pool.memset(t.mask_kq[:], 0.0).then_inc(filled, 1)
            pool.wait_ge(filled, 2)
            pool.affine_select(out=t.ident32[:], in_=t.ident32[:], pattern=[[-1, P]], compare_op=ALU.not_equal,
                               fill=1.0, base=0, channel_multiplier=1).then_inc(filled, 1)
            pool.affine_select(out=t.mask_qk[:], in_=t.mask_kq[:], pattern=[[-1, P]], compare_op=ALU.is_ge,
                               fill=NEG, base=0, channel_multiplier=1).then_inc(filled, 1)
            pool.wait_ge(filled, 4)
            pool.affine_select(out=t.mask_kq[:], in_=t.mask_kq[:], pattern=[[1, P]], compare_op=ALU.is_ge,
                               fill=NEG, base=0, channel_multiplier=-1).then_inc(filled, 1)
            pool.tensor_copy(t.ident16[:], t.ident32[:]).then_inc(filled, 1)
            pool.tensor_copy(t.ident_bf[:], t.ident32[:]).then_inc(filled, 1)
            pool.wait_ge(filled, 7)

        @block.vector
        def _(vector):
            vector.memset(scale[:], 1.0).then_inc(scaled, 1)
            vector.wait_ge(scaled, 1)
            vector.memset(scale[:, 0], DH ** -0.5).then_inc(scaled, 1)
            vector.wait_ge(loaded, 16 * n_first)
            vector.tensor_scalar(scale[:, 4], t.g1[:], DH ** -0.5, None, ALU.mult).then_inc(scaled, 1)
            for j in (5, 6):
                vector.tensor_copy(scale[:, j], t.g1[:]).then_inc(scaled, 1)
            vector.tensor_scalar(t.bq[:], t.bq[:], DH ** -0.5, None, ALU.mult).then_inc(scaled, 1)
            vector.wait_ge(scaled, 6)
            for j in range(8):
                for k in range(KD):
                    n = j * KD + k + 1
                    vector.wait_ge(split_hi, n)
                    vector.scalar_tensor_tensor(t.w_proj[:, j, 1, k], w32[:, j, k], scale[:, j, k:k + 1],
                                                t.w_proj[:, j, 0, k], ALU.mult, ALU.subtract).then_inc(split_lo, 1)
            for k in range(KD):
                vector.wait_ge(split_hi, 8 * KD + k + 1)
                vector.tensor_tensor(t.w_router[:, 1, k], r32[:, k], t.w_router[:, 0, k],
                                     ALU.subtract).then_inc(split_lo, 1)

        @block.scalar
        def _(act):
            act.wait_ge(scaled, 6)
            for j in range(8):
                act.wait_ge(w_loaded[j], 16)
                for k in range(KD):
                    act.activation(t.w_proj[:, j, 0, k], w32[:, j, k], ACT.Copy,
                                   scale=scale[:, j, k:k + 1]).then_inc(split_hi, 1)
            act.wait_ge(w_loaded[8], 16)
            for k in range(KD):
                act.activation(t.w_router[:, 0, k], r32[:, k], ACT.Copy).then_inc(split_hi, 1)
            act.wait_ge(split_lo, 6 * KD)
            halves = lambda x: x.rearrange("p w b k (h t d) -> p (w b k h) t d", h=H, t=2)
            src, dst = halves(t.w_proj[:, 4:6]), halves(t.w_rot[:])
            act.activation(dst[:, :, 0], src[:, :, 1], ACT.Copy, scale=-1.0).then_inc(rotated, 1)
            act.activation(dst[:, :, 1], src[:, :, 0], ACT.Copy).then_inc(rotated, 1)
            act.wait_ge(rotated, 2)


def load_unit(sync, t, b, g, qk_loaded, v_loaded):
    for x, c0, terms in ((t.qx, 0, (0, 0, 1)), (t.kx, 2, (0, 1, 0))):
        for n, hl in enumerate(terms):
            c, p0 = c0 + g // 2, (g % 2) * HG * DH
            src = t.qk_dram[hl][p0:p0 + HG * DH, c, ds(b * S, S)].rearrange("(h d) n -> d h n", d=DH)
            sync.dma_start(x[n * DH:(n + 1) * DH, g], src).then_inc(qk_loaded, 16)
    sync.dma_start(t.v_in[:, g], t.v_dram.rearrange("(k p) n -> p k n", p=P)[
        :, ds(b * QT, QT), g * HG * DH:(g + 1) * HG * DH]).then_inc(v_loaded, 16)


def project_qkv(nc, t, layer, x_dram):
    rope = layer == 1
    with ExitStack() as ctx:
        L = f"l{layer}_"
        sem = ctx.enter_context(stage_semaphores(nc, L))
        pair = lambda n: [sem(f"{n}{i}") for i in range(2)]
        sb = lambda n, s, d: ctx.enter_context(nc.sbuf_tensor(L + n, s, d))
        ps = lambda n, s, d: ctx.enter_context(nc.psum_tensor(L + n, s, d))
        x_in = t.x_parts if rope else sb("x_in", [P, 2, KD, S], F32)
        first = 0 if rope else 16
        xT = sb("xT", [P, 2, 2, KD, S], F16)
        qk = sb("qk", [P, 2, 4, 2, S], F16)
        v = sb("v", [P, 2, QT, D], F32)
        NB = 2 if rope else 4
        ps_qk = ps("ps_qk", [P, NB, S], F32)
        ps_v = ps("ps_v", [P, 2, 2, D], F32)
        if rope:
            q_cos = sb("q_cos", [P, 2, S], F32)
            q_sin = sb("q_sin", [P, 2, S], F32)
            q_rot = sb("q_rot", [P, 2, S], F32)
            ps_rot = ps("ps_rot", [P, 2, S], F32)
            ps_xT = ps("ps_xT", [P, 2, KD, S], F16)
        x_loaded, stored, xT_mm, xT_hi, xT_lo, v_mm, v_out = map(pair, (
            "x_loaded", "stored", "xT_mm", "xT_hi", "xT_lo", "v_mm", "v_out"))
        qk_mm, qk_hi, qk_lo = ([sem(f"{n}{i}") for i in range(NB)] for n in ("qk_mm", "qk_hi", "qk_lo"))
        rot_mm, cos_out, sin_out, rot_out = map(pair, ("rot_mm", "cos_out", "sin_out", "rot_out"))
        filled, unit_loaded = sem("filled"), sem("unit_loaded")
        block = ctx.enter_context(nc.Block())
        STORES = 3 * 16

        def done(b, c):
            return b * (4 // NB) + (c // NB + 1)

        def free(b, c):
            return b * (4 // NB) + c // NB

        def batches(engine, batch):
            with engine.Fori(0, B // 2 - 1) as r:
                batch(r, 0, (r, 1))
                batch(r, 1, (r + 1, 0))
            last = B // 2 - 1
            batch(last, 0, (last, 1))
            batch(last, 1, None)

        @block.sync
        def _(sync):
            def load(b, s):
                sync.dma_start(x_in[:, s], x_dram(b)).then_inc(x_loaded[s], 16)

            def store(b, s):
                for c in range(4 - NB, 4):
                    sync.wait_ge(qk_hi[c % NB], done(b, c))
                    sync.wait_ge(qk_lo[c % NB], done(b, c))
                for hl in range(2):
                    sync.dma_start(t.qk_dram[hl][:, :, ds(b * S, S)], qk[:, s, :, hl, :]).then_inc(stored[s], 16)

            def store_v(b, r, s):
                sync.wait_ge(v_out[s], r * 2 + 2)
                sync.dma_start(t.v_dram.rearrange("(k p) n -> p k n", p=P)[:, ds(b * QT, QT), :],
                               v[:, s]).then_inc(stored[s], 16)

            if not rope:
                load(0, 0)
                load(1, 1)
            with sync.Fori(0, B // 2 - 1) as r:
                for s in range(2):
                    sync.wait_ge(xT_hi[s], r + 1)
                    sync.wait_ge(xT_lo[s], r + 1)
                    load(r * 2 + (2 + s), s)
                    store(r * 2 + s, s)
                    store_v(r * 2 + s, r, s)
            sync.wait_ge(stored[0], STORES)
            if not rope:
                sync.wait_ge(filled, 4)
            for s in range(2):
                for g in (2 * s, 2 * s + 1):
                    load_unit(sync, t, 0, g, unit_loaded, unit_loaded)
                store(B - 2 + s, s)
                store_v(B - 2 + s, B // 2 - 1, s)
            sync.wait_ge(unit_loaded, 7 * 16 * G)
            for s in range(2):
                sync.wait_ge(stored[s], STORES * (B // 2))

        @block.tensor
        def _(pe):
            def transpose_x(r, s):
                pe.wait_ge(x_loaded[s], r * 16 + first)
                o = 1 - s
                pe.wait_ge(xT_hi[o], r + s)
                pe.wait_ge(xT_lo[o], r + s)
                for hl in range(2):
                    for k in range(KD):
                        for q in range(QT):
                            mm = pe.transpose(ps_xT[:, hl, k, q * P:(q + 1) * P],
                                              x_in[:, s, q, hl * D + k * P:hl * D + (k + 1) * P], t.ident16[:])
                mm.then_inc(xT_mm[s], 1)

            def project(out, w, s, m):
                n = 0
                for wh, xh in ((0, 0), (0, 1), (1, 0)):
                    for k in range(KD):
                        mm = pe.matmul(out, w[:, wh, k, m * P:(m + 1) * P], xT[:, s, xh, k, :],
                                       start=n == 0, stop=n == 5)
                        n += 1
                return mm

            def batch(r, s, following):
                b = r * 2 + s
                pe.wait_ge(xT_hi[s], r + 1)
                pe.wait_ge(xT_lo[s], r + 1)
                for c in range(4):
                    w, m = c // 2, c % 2
                    for read in ([cos_out] if rope else [qk_hi, qk_lo]):
                        pe.wait_ge(read[c % NB], free(b, c))
                    project(ps_qk[:, c % NB], t.w_proj[:, 4 * layer + w], s, m).then_inc(qk_mm[c % NB], 1)
                    if rope:
                        pe.wait_ge(sin_out[c % 2], free(b, c))
                        project(ps_rot[:, c % 2], t.w_rot[:, w], s, m).then_inc(rot_mm[c % 2], 1)
                        if c == 1 and following is not None:
                            transpose_x(*following)
                for u in range(2):
                    pe.wait_ge(v_out[1 - s], (r + s) * 2)
                    for j in range(2):
                        n, q = 0, 2 * u + j
                        for wh, xh in ((0, 0), (1, 0), (0, 1)):
                            for k in range(KD):
                                mm = pe.matmul(ps_v[:, u, j], xT[:, s, xh, k, q * P:(q + 1) * P],
                                               t.w_proj[:, 4 * layer + 2, wh, k, :], start=n == 0, stop=n == 5)
                                n += 1
                    mm.then_inc(v_mm[s], 1)

            if rope:
                transpose_x(0, 0)
            batches(pe, batch)

        @block.scalar
        def _(act):
            def split_x(r, s):
                if rope:
                    act.wait_ge(xT_mm[s], r + 1)
                else:
                    act.wait_ge(x_loaded[s], r * 16 + first)
                act.wait_ge(v_mm[s], r * 2)
                src = ps_xT[:, 0] if rope else x_in[:, s]
                act.activation(xT[:, s, 0], src, ACT.Copy).then_inc(xT_hi[s], 1)

            def batch(r, s, following):
                b = r * 2 + s
                act.wait_ge(stored[s], r * STORES)
                for c in range(4):
                    if rope:
                        act.wait_ge(rot_out[c % 2], done(b, c))
                        act.activation(qk[:, s, c, 0], q_rot[:, c % 2], ACT.Copy).then_inc(qk_hi[c % NB], 1)
                    else:
                        act.wait_ge(qk_mm[c % NB], done(b, c))
                        bias = (t.bq if c < 2 else t.bk)[:, c % 2:c % 2 + 1]
                        act.activation(qk[:, s, c, 0], ps_qk[:, c % NB], ACT.Identity,
                                       bias=bias).then_inc(qk_hi[c % NB], 1)
                    if c == 1 and following is not None:
                        split_x(*following)

            split_x(0, 0)
            batches(act, batch)

        @block.vector
        def _(vector):
            def split_x(r, s):
                vector.wait_ge(xT_hi[s], r + 1)
                if rope:
                    vector.tensor_copy(xT[:, s, 1], ps_xT[:, 1]).then_inc(xT_lo[s], 1)
                else:
                    vector.tensor_tensor(xT[:, s, 1], x_in[:, s], xT[:, s, 0], ALU.subtract).then_inc(xT_lo[s], 1)

            def batch(r, s, following):
                b = r * 2 + s
                vector.wait_ge(stored[s], r * STORES)
                for c in range(4):
                    if rope:
                        vector.wait_ge(qk_mm[c % NB], done(b, c))
                        vector.wait_ge(rot_out[c % 2], free(b, c))
                        vector.tensor_tensor(q_cos[:, c % 2], ps_qk[:, c % NB], t.cos[:],
                                             ALU.mult).then_inc(cos_out[c % 2], 1)
                        vector.wait_ge(rot_mm[c % 2], done(b, c))
                        vector.tensor_tensor(q_sin[:, c % 2], ps_rot[:, c % 2], t.sin[:],
                                             ALU.mult).then_inc(sin_out[c % 2], 1)
                    else:
                        bias = (t.bq if c < 2 else t.bk)[:, c % 2:c % 2 + 1]
                        vector.wait_ge(qk_hi[c % NB], done(b, c))
                        vector.scalar_tensor_tensor(qk[:, s, c, 1], ps_qk[:, c % NB], bias, qk[:, s, c, 0],
                                                    ALU.add, ALU.subtract).then_inc(qk_lo[c % NB], 1)
                    if c == 1 and following is not None:
                        split_x(*following)
                for u in range(2):
                    vector.wait_ge(v_mm[s], r * 2 + (u + 1))
                    if rope:
                        vector.tensor_copy(v[:, s, 2 * u:2 * u + 2], ps_v[:, u]).then_inc(v_out[s], 1)
                    else:
                        vector.tensor_tensor(v[:, s, 2 * u:2 * u + 2], ps_v[:, u], t.bv2[:],
                                             ALU.add).then_inc(v_out[s], 1)

            split_x(0, 0)
            batches(vector, batch)

        if rope:
            @block.gpsimd
            def _(pool):
                with pool.Fori(0, B // 2) as r:
                    for s in range(2):
                        b = r * 2 + s
                        pool.wait_ge(stored[s], r * STORES)
                        for c in range(5):
                            if c < 4:
                                i = c % 2
                                pool.wait_ge(qk_hi[i], free(b, c))
                                pool.wait_ge(qk_lo[i], free(b, c))
                                pool.wait_ge(cos_out[i], done(b, c))
                                pool.wait_ge(sin_out[i], done(b, c))
                                pool.tensor_tensor(q_rot[:, i], q_cos[:, i], q_sin[:, i], ALU.add).then_inc(rot_out[i], 1)
                            if c > 0:
                                i = (c - 1) % 2
                                pool.wait_ge(qk_hi[i], done(b, c - 1))
                                pool.tensor_tensor(qk[:, s, c - 1, 1], q_rot[:, i], qk[:, s, c - 1, 0],
                                                   ALU.subtract).then_inc(qk_lo[i], 1)
        else:
            @block.gpsimd
            def _(pool):
                pool.memset(t.qx[:], 0.0).then_inc(filled, 1)
                pool.memset(t.kx[:], 1.0).then_inc(filled, 1)
                pool.memset(t.v_one[:], 1.0).then_inc(filled, 1)
                pool.wait_ge(filled, 3)
                kf = t.kx[:].rearrange("p g h n -> p (g h n)")
                pool.affine_select(out=kf, in_=kf, pattern=[[0, G * HG * S]], compare_op=ALU.is_ge, fill=0.0,
                                   base=-MAXROW, channel_multiplier=1).then_inc(filled, 1)
                pool.wait_ge(filled, 4)


def attend(nc, t, layer, matrices=()):
    causal = layer == 1
    width = lambda kt: S - kt * P if causal else S
    keys = lambda q: (q + 1) * P if causal else S
    at = lambda kt: 0 if kt % 2 == 0 else width(kt - 1)
    with ExitStack() as ctx:
        L = f"a{layer}_"
        sem = ctx.enter_context(stage_semaphores(nc, L))
        several = lambda n, k: [sem(f"{n}{i}") for i in range(k)]
        sb = lambda n, s, d: ctx.enter_context(nc.sbuf_tensor(L + n, s, d))
        ps = lambda n, s, d: ctx.enter_context(nc.psum_tensor(L + n, s, d))
        qx, kx, v_in, v_one = t.qx, t.kx, t.v_in, t.v_one
        probs = sb("probs", [P, 2, HG, 2 * S], F32)
        neg_max = sb("neg_max", [P, G, QT, HG], F32)
        max_parts = sb("max_parts", [P, G, QT, 2, HG], F16)
        rows = sb("rows", [2 * HG, 2, S], F16)
        o32 = sb("o32", [P, S], F32)
        inv = sb("inv", [P, 2, QT, HG], F32)
        o_norm = sb("o_norm", [P, 2, QT, HG * DH], F32)
        if matrices:
            w_in = sb("w_in", [P, len(matrices), WP], F32)
            w_part = sb("w_part", [P, len(matrices), 2, WP], F16)
            w_loaded, w_hi, w_lo, w_stored = (
                several(n, len(matrices)) for n in ("w_loaded", "w_hi", "w_lo", "w_stored"))
        ps_s = ps("ps_s", [P, 2, S], F32)
        ps_m = ps("ps_m", [P, 4, S], F32)
        ps_o = ps("ps_o", [P, S], F32)
        ps_x = ps("ps_x", [P, S], F32)
        qk_loaded, v_loaded, rows_loaded, v_copied, group_done = (
            several(n, G) for n in ("qk_loaded", "v_loaded", "rows_loaded", "v_copied", "group_done"))
        scores_mm = sem("scores_mm")
        exp_out, max_out = several("exp_out", 2), several("max_out", 4)
        half_done = sem("half_done")
        max_mm, max_hi, max_lo, rows_mm, rows_out = map(sem, ("max_mm", "max_hi", "max_lo", "rows_mm", "rows_out"))
        ps_rows = ps_x[:].bitcast(F16)
        o_out, back_mm, inv_out, norm_out = sem("o_out"), sem("back_mm"), sem("inv_out"), sem("norm_out")
        attn_hi, attn_lo = sem("attn_hi"), sem("attn_lo")
        block = ctx.enter_context(nc.Block())

        def ahead(b, g, n):
            return b + (g + n) // G, (g + n) % G

        def steps(engine, step):
            for g in range(G):
                step(0, g, first=g == 0)
            with engine.Fori(1, B - 1) as b:
                for g in range(G):
                    step(b, g)
            for g in range(G):
                step(B - 1, g, maxima=g + 2 < G, has_next=g + 1 < G)

        @block.sync
        def _(sync):
            def load_piece(b, i):
                src = matrices[i].rearrange("e a b -> (e a b)").rearrange("(p n) -> p n", p=P)
                sync.dma_start(w_in[:, i], src[:, ds(b * WP, WP)]).then_inc(w_loaded[i], 16)

            def store_piece(b, i):
                sync.wait_ge(w_hi[i], b + 1)
                sync.wait_ge(w_lo[i], b + 1)
                for hl in range(2):
                    dst = t.w_dram[i][hl].rearrange("e a b -> (e a b)").rearrange("(p n) -> p n", p=P)
                    sync.dma_start(dst[:, ds(b * WP, WP)], w_part[:, i, hl]).then_inc(w_stored[i], 16)

            def load_rows(b, g, n):
                sync.wait_ge(rows_out, n)
                sync.dma_start(qx[MAXROW:MAXROW + 2, g], rows[:, g % 2]).then_inc(rows_loaded[g], 16)

            def step(b, g, first=False, maxima=True, has_next=True):
                if has_next:
                    load_rows(*ahead(b, g, 1), b * G + (g + 2))
                if not (isinstance(b, int) and b == B - 1):
                    scored, copied = counted(sync, b * (16 * G) + 16 * (g + 1)), counted(sync, b + 1)
                    sync.wait_ge(scores_mm, scored)
                    sync.wait_ge(v_copied[g], copied)
                    load_unit(sync, t, b + 1, g, qk_loaded[g], v_loaded[g])
                i = g - 1
                if 0 <= i < len(matrices):
                    store_piece(b, i)
                    if not (isinstance(b, int) and b == B - 1):
                        load_piece(b + 1, i)

            for i in range(len(matrices)):
                load_piece(0, i)
            load_rows(0, 0, 1)
            steps(sync, step)
            for i in range(len(matrices)):
                sync.wait_ge(w_stored[i], 32 * B)

        @block.gpsimd
        def _(pool):
            def copy_v(b, g):
                if not (isinstance(b, int) and b == 0):
                    loads = counted(pool, b * 16)
                    pool.wait_ge(v_loaded[g], 16)
                    pool.wait_ge(v_loaded[g], loads)
                    pool.wait_ge(group_done[g], b)
                pool.tensor_copy(v_one[:, g, :, :, 0:DH],
                                 v_in[:, g].rearrange("p k (h d) -> p k h d", h=HG)).then_inc(v_copied[g], 1)

            def split(b, g):
                n = b * G + g
                hi, lo = (t.attn[:, hl, ds(b * QT, QT), g * HG * DH:(g + 1) * HG * DH] for hl in range(2))
                normed = counted(pool, n + 1)
                pool.wait_ge(norm_out, 1)
                pool.wait_ge(norm_out, normed)
                pool.tensor_copy(hi, o_norm[:, g % 2]).then_inc(attn_hi, 1)
                pool.wait_ge(attn_hi, 1)
                pool.wait_ge(attn_hi, normed)
                pool.tensor_tensor(lo, o_norm[:, g % 2], hi, ALU.subtract).then_inc(attn_lo, 1)

            def split_piece(b, i):
                loads, highs, stores = counted(pool, b * 16 + 16), counted(pool, b + 1), counted(pool, b * 32)
                pool.wait_ge(w_loaded[i], 16)
                pool.wait_ge(w_loaded[i], loads)
                pool.wait_ge(w_stored[i], stores)
                pool.tensor_copy(w_part[:, i, 0], w_in[:, i]).then_inc(w_hi[i], 1)
                pool.wait_ge(w_hi[i], highs)
                pool.tensor_tensor(w_part[:, i, 1], w_in[:, i], w_part[:, i, 0], ALU.subtract).then_inc(w_lo[i], 1)

            def step(b, g, first=False, maxima=True, has_next=True):
                copy_v(b, g)
                if g < len(matrices):
                    split_piece(b, g)
                if not (isinstance(b, int) and b * G + g < 3):
                    split(*ahead(b, g, -3))

            steps(pool, step)
            for g in range(1, G):
                split(B - 1, g)

        @block.tensor
        def _(pe):
            def scores(b, g, j, kt):
                kp, i = kt // 2, kt % 2
                if kt == 0 and j == 0:
                    pe.wait_ge(rows_loaded[g], b * 16 + 16)
                pe.wait_ge(exp_out[i], b * (8 * G) + (8 * g + kp * HG + j))
                mm = pe.matmul(ps_s[:, i, 0:width(kt)], kx[:, g, j, kt * P:(kt + 1) * P],
                               qx[:, g, j, S - width(kt):S], start=True, stop=not causal)
                if causal:
                    mm = pe.matmul(ps_s[:, i, 0:P], t.ident_bf[:], t.mask_kq[:], start=False, stop=True)
                mm.then_inc(scores_mm, 1)

            def maxima_of(b, g, c):
                j, q = c // QT, c % QT
                if c == 0:
                    pe.wait_ge(qk_loaded[g], b * 96)
                pe.wait_ge(max_out[c % 4], b * (4 * G) + (4 * g + c // 4))
                mm = pe.matmul(ps_m[:, c % 4, 0:keys(q)], qx[0:MAXROW, g, j, q * P:(q + 1) * P],
                               kx[0:MAXROW, g, j, 0:keys(q)], start=True, stop=not causal)
                if causal:
                    mm = pe.matmul(ps_m[:, c % 4, q * P:(q + 1) * P], t.ident_bf[:], t.mask_qk[:],
                                   start=False, stop=True)
                mm.then_inc(max_mm, 1)

            def turn_maxima(b, g, n):
                pe.wait_ge(max_hi, n + 1)
                pe.wait_ge(max_lo, n + 1)
                pe.wait_ge(norm_out, max(n - 2, 0) if isinstance(n, int) else n - 2)
                for q in range(QT):
                    mm = pe.transpose(ps_rows[0:2 * HG, q * P:(q + 1) * P],
                                      max_parts[:, g, q].rearrange("p l h -> p (l h)"), t.ident16[:])
                mm.then_inc(rows_mm, 1)

            def weigh(b, g, kt):
                n = b * G + g
                pe.wait_ge(exp_out[kt % 2], n * 8 + (kt // 2 + 1) * HG)
                if kt == 0:
                    pe.wait_ge(v_copied[g], b + 1)
                    pe.wait_ge(o_out, n)
                for j in range(HG):
                    mm = pe.matmul(ps_o[32 * j:32 * (j + 1), S - width(kt):S], v_one[:, g, kt, j, :],
                                   probs[:, kt // 2, j, at(kt):at(kt) + width(kt)],
                                   start=kt == 0, stop=kt == QT - 1)
                if kt == 1:
                    mm.then_inc(half_done, 1)
                elif kt == QT - 1:
                    mm.then_inc(group_done[g], 1)

            def turn_back(b, g):
                n = b * G + g
                pe.wait_ge(o_out, n + 1)
                turned = min(n + 3, B * G) if isinstance(n, int) else n + 3
                pe.wait_ge(rows_out, turned)
                pe.wait_ge(norm_out, n)
                for q in range(QT):
                    mm = pe.transpose(ps_x[:, q * P:(q + 1) * P], o32[:, q * P:(q + 1) * P], t.ident32[:])
                mm.then_inc(back_mm, 1)

            def step(b, g, first=False, maxima=True, has_next=True):
                def a_maximum(c):
                    if maxima:
                        maxima_of(*ahead(b, g, 2), c)

                for half, kt in enumerate((2, 3, 0, 1)):
                    c, done = 4 * half, 0
                    for work in ORDER:
                        if work == "M":
                            a_maximum(c)
                            c += 1
                        elif work == "S":
                            scores(b, g, half % 2 * 2 + done // 2, half // 2 * 2 + done % 2)
                            done += 1
                            if half == 0 and done == 3 and has_next:
                                turn_maxima(*ahead(b, g, 1), b * G + (g + 1))
                        elif half >= 2:
                            weigh(b, g, kt)
                        elif not first:
                            weigh(*ahead(b, g, -1), kt)
                    if half == 2 and not first:
                        turn_back(*ahead(b, g, -1))

            for g in range(2):
                for c in range(HG * QT):
                    maxima_of(0, g, c)
                if g == 0:
                    turn_maxima(0, 0, 0)
            steps(pe, step)
            weigh(B - 1, G - 1, 2)
            weigh(B - 1, G - 1, 3)
            turn_back(B - 1, G - 1)

        @block.scalar
        def _(act):
            def exponentials(b, g, kp, j, first):
                n = b * G + g
                for i in range(2):
                    act.wait_ge(scores_mm, n * 16 + (kp * 8 + j * 2 + i + 1))
                    if j == 0 and i == 0:
                        if kp == 0:
                            act.wait_ge(half_done, n)
                        elif not first:
                            before, of = ahead(b, g, -1)
                            act.wait_ge(group_done[of], before + 1)
                    kt = 2 * kp + i
                    w = width(kt)
                    act.activation(probs[:, kp, j, at(kt):at(kt) + w], ps_s[:, i, 0:w], ACT.Exp).then_inc(exp_out[i], 1)

            def copy_rows(b, g, n):
                act.wait_ge(rows_mm, n)
                act.activation(rows[:, g % 2], ps_rows[0:2 * HG, 0:S], ACT.Copy).then_inc(rows_out, 1)

            def empty_o(b, g):
                act.wait_ge(group_done[g], b + 1)
                act.wait_ge(back_mm, b * G + g)
                act.activation(o32[:], ps_o[:], ACT.Copy).then_inc(o_out, 1)

            def step(b, g, first=False, maxima=True, has_next=True):
                for kp in range(2):
                    if kp == 1 and not first:
                        empty_o(*ahead(b, g, -1))
                    for j in range(HG):
                        exponentials(b, g, kp, j, first)
                        if kp == 0 and j == 1 and has_next:
                            copy_rows(*ahead(b, g, 1), b * G + (g + 2))

            copy_rows(0, 0, 1)
            steps(act, step)
            empty_o(B - 1, G - 1)

        @block.vector
        def _(vector):
            def row_max(b, g, c):
                j, q = c // QT, c % QT
                vector.wait_ge(max_mm, b * (16 * G) + (16 * g + c + 1))
                vector.tensor_reduce(neg_max[:, g, q, j:j + 1], ps_m[:, c % 4, 0:keys(q)], AX.X, ALU.max,
                                     negate=True).then_inc(max_out[c % 4], 1)

            def split_maxima(b, g):
                n = b * G + g
                for i in range(4):
                    vector.wait_ge(max_out[i], n * 4 + 4)
                vector.tensor_copy(max_parts[:, g, :, 0], neg_max[:, g]).then_inc(max_hi, 1)
                vector.wait_ge(max_hi, n + 1)
                vector.tensor_tensor(max_parts[:, g, :, 1], neg_max[:, g], max_parts[:, g, :, 0],
                                     ALU.subtract).then_inc(max_lo, 1)

            def normalise(b, g):
                n = b * G + g
                vector.wait_ge(back_mm, n + 1)
                o = ps_x[:].rearrange("p (q j d) -> p q j d", q=QT, j=HG)
                vector.reciprocal(inv[:, 0], o[:, :, :, DH]).then_inc(inv_out, 1)
                vector.wait_ge(inv_out, n * (1 if causal else 2) + 1)
                scale = inv[:, 0]
                if not causal:
                    mask = t.head_mask[:, g * HG:(g + 1) * HG].rearrange("p (o h) -> p o h", o=1)
                    vector.tensor_tensor(inv[:, 1], inv[:, 0], mask.broadcast_to([P, QT, HG]),
                                         ALU.mult).then_inc(inv_out, 1)
                    vector.wait_ge(inv_out, n * 2 + 2)
                    scale = inv[:, 1]
                vector.wait_ge(attn_lo, max(n - 1, 0) if isinstance(n, int) else n - 1)
                out = o_norm[:, g % 2].rearrange("p q (j d) -> p q j d", j=HG)
                vector.tensor_tensor(out, o[:, :, :, 0:DH],
                                     scale.rearrange("p q (j o) -> p q j o", o=1).broadcast_to([P, QT, HG, DH]),
                                     ALU.mult).then_inc(norm_out, 1)

            def step(b, g, first=False, maxima=True, has_next=True):
                for c in range(16):
                    if maxima:
                        row_max(*ahead(b, g, 2), c)
                    if c == 12 and not first:
                        normalise(*ahead(b, g, -1))
                if maxima:
                    split_maxima(*ahead(b, g, 2))

            for g in range(2):
                for c in range(16):
                    row_max(0, g, c)
                split_maxima(0, g)
            steps(vector, step)
            normalise(B - 1, G - 1)


def attention_tensors(nc, ctx, t):
    sb = lambda n, s, d: ctx.enter_context(nc.sbuf_tensor(n, s, d))
    t.ident_bf = sb("ident_bf", [P, P], BF16)
    t.mask_kq, t.mask_qk = sb("mask_kq", [P, P], BF16), sb("mask_qk", [P, P], BF16)
    t.cos, t.sin = sb("rope_cos", [P, S], F32), sb("rope_sin", [P, S], F32)
    t.w_proj = sb("w_proj", [P, 8, 2, KD, D], F16)
    t.w_rot = sb("w_rot", [P, 2, 2, KD, D], F16)
    t.w_router = sb("w_router_parts", [P, 2, KD, E], F16)
    t.bq, t.bk, t.g1 = sb("bq", [P, KD], F32), sb("bk", [P, KD], F32), sb("g1", [P, KD], F32)
    t.bv2, t.bo = sb("bv2", [P, 2, D], F32), sb("bo", [P, D], F32)
    t.head_mask = sb("head_mask_row", [P, H], F32)
    t.g2 = sb("g2", [P, 1, D], F32)
    t.attn = sb("attn", [P, 2, NT, D], F16)
    t.qx = sb("qx", [P, G, HG, S], F16)
    t.kx = sb("kx", [P, G, HG, S], F16)
    t.v_in = sb("v_in", [P, G, QT, HG * DH], F32)
    t.x_parts = sb("x_parts", [P, 2, QT, 2 * D], F16)
    t.v_one = sb("v_one", [P, G, QT, HG, 32], F32)


def pipeline(engine, *stages):
    n = len(stages)

    def step(oldest, pair, parity):
        for ahead in range(n):
            if not isinstance(oldest, int) or 0 <= oldest + ahead < B:
                j = parity + ahead
                stages[n - 1 - ahead](oldest + ahead, j % 2, pair + j // 2)

    full = B - n + 1
    for oldest in range(1 - n, 0):
        step(oldest, oldest // 2, oldest % 2)
    with engine.Fori(0, full // 2) as pair:
        for parity in range(2):
            step(pair * 2 + parity, pair, parity)
    for oldest in range(full // 2 * 2, B):
        step(oldest, oldest // 2, oldest % 2)


def counted(engine, value):
    return value if isinstance(value, int) else engine.snap(engine.to_reg(value))


def before_last(b):
    return max(b - 1, 0) if isinstance(b, int) else b - 1


def project_out(nc, t, layer, x_res_dram, x_out_dram, part_dram):
    norm, route = layer == 0, layer == 1
    with ExitStack() as ctx:
        L = f"o{layer}_"
        sem = ctx.enter_context(stage_semaphores(nc, L))
        sb = lambda n, s, d: ctx.enter_context(nc.sbuf_tensor(L + n, s, d))
        ps = lambda n, s, d: ctx.enter_context(nc.psum_tensor(L + n, s, d))
        x_res = sb("x_res", [P, 2, QT, D], F32)
        aT = sb("aT", [P, 2, 2, KD, S], F16)
        x_new = sb("x_new", [P, 2, QT, D], F32)
        x_out = sb("x_out", [P, 2, QT, D], F32) if norm else x_new
        stats, mean_var = sb("stats", [P, 2, QT, 6], F32), sb("mean_var", [P, 2, QT, 2], F32)
        squares = sb("squares", [P, 2, QT, D], BF16)
        small = sb("small", [P, 2, 4, QT], F32)
        ms = sb("ms", [P, 2, QT], F32)
        constants = sb("constants", [P, 3, QT], F32)
        part = sb("part", [P, 2, QT, 2, D], F16)
        ps_aT = ps("ps_aT", [P, 2, KD, S], F16)
        ps_y = ps("ps_y", [P, 2, 2, D], F32)
        loaded, stored = [[sem(f"{n}{i}") for i in range(2)] for n in ("loaded", "stored")]
        aT_mm, aT_hi, aT_lo = map(sem, ("aT_mm", "aT_hi", "aT_lo"))
        y_mm, biased, summed, aggregated, var_out, rstd_out, x_done = map(sem, (
            "y_mm", "biased", "summed", "aggregated", "var_out", "rstd_out", "x_done"))
        squared, ms_out, rms_out, part_hi, part_lo, power, stat_out = map(sem, (
            "squared", "ms_out", "rms_out", "part_hi", "part_lo", "power", "stat_out"))
        if route:
            x_sum = sb("x_sum", [P, 2, QT, D], F32)
            normed = sb("normed", [P, 2, QT, D], F32)
            nT = sb("nT", [P, 2, KD, S], F16)
            ps_nT = ps("ps_nT", [P, 2, KD, S], F16)
            ps_l = ps("ps_l", [P, QT, E], F32)
            nT_mm, nT_hi, nT_lo, logits_mm, logits_out, added, normed_out = map(sem, (
                "nT_mm", "nT_hi", "nT_lo", "logits_mm", "logits_out", "added", "normed_out"))
        block = ctx.enter_context(nc.Block())
        tiles = lambda x: x.rearrange("(k p) n -> p k n", p=P)
        next_loaded = sem("next_loaded")
        PQ = QT if norm else 1
        idle = lambda b, s, k: None

        def wait_x(engine, b, q):
            if norm:
                engine.wait_ge(x_done, b * QT + (q + 1))
            else:
                engine.wait_ge(summed, b * 2 + (q // 2 + 1))

        @block.sync
        def _(sync):
            def load(b, s, k):
                sync.wait_ge(summed if norm else added, before_last(b) * (2 if norm else 1))
                sync.dma_start(x_res[:, s], tiles(x_res_dram)[:, ds(b * QT, QT), :]).then_inc(loaded[s], 16)

            def store(b, s, k):
                if norm and isinstance(b, int) and b == B - 1:
                    for i in range(2):
                        sync.wait_ge(stored[i], 32)
                        sync.dma_start(t.x_parts[:, i], tiles(part_dram)[:, i * QT:(i + 1) * QT, :]
                                       ).then_inc(next_loaded, 16)
                if norm:
                    sync.wait_ge(x_done, b * QT + QT)
                else:
                    sync.wait_ge(added, b + 1)
                sync.dma_start(tiles(x_out_dram)[:, ds(b * QT, QT), :],
                               (x_out if norm else x_sum)[:, s]).then_inc(stored[s], 16)
                sync.wait_ge(part_hi, b * PQ + PQ)
                sync.wait_ge(part_lo, b * PQ + PQ)
                sync.dma_start(tiles(part_dram)[:, ds(b * QT, QT), :],
                               part[:, s].rearrange("p q h n -> p q (h n)")).then_inc(stored[s], 16)

            pipeline(sync, load, idle, idle, idle, store)
            if norm:
                sync.wait_ge(next_loaded, 32)
            for s in range(2):
                sync.wait_ge(stored[s], 32 * (B // 2))

        @block.gpsimd
        def _(pool):
            def bias(b, s, k):
                if norm:
                    pool.wait_ge(loaded[s], k * 16 + 16)
                    pool.tensor_tensor(x_res[:, s], x_res[:, s], t.bo[:].rearrange("p (o n) -> p o n", o=1)
                                       .broadcast_to([P, QT, D]), ALU.add).then_inc(biased, 1)

            def inverse_root(b, s, src, eps, mid, out, first_done, done):
                pool.tensor_tensor(small[:, s, mid], src, constants[:, eps], ALU.add).then_inc(first_done, 1)
                pool.wait_ge(first_done, b + 1)
                pool.tensor_tensor(small[:, s, out], small[:, s, mid], constants[:, 0], ALU.pow).then_inc(done, 1)

            def deviation(b, s, k):
                if norm:
                    pool.wait_ge(aggregated, b * QT + QT)
                    inverse_root(b, s, mean_var[:, s, :, 1], 1, 0, 1, var_out, rstd_out)

            def root_mean_square(b, s, k):
                pool.wait_ge(squared, b * QT + QT)
                pool.wait_ge(part_lo, before_last(b) * PQ)
                inverse_root(b, s, ms[:, s], 2, 2, 3, ms_out, rms_out)

            def low_parts(b, s, k):
                if route:
                    pool.wait_ge(part_hi, b + 1)
                    pool.tensor_tensor(part[:, s, :, 1], normed[:, s], part[:, s, :, 0], ALU.subtract).then_inc(part_lo, 1)

            for i, value in enumerate((-0.5, LN_EPS, RMS_EPS)):
                pool.memset(constants[:, i], value).then_inc(power, 1)
            pool.wait_ge(power, 3)
            pipeline(pool, bias, deviation, root_mean_square, low_parts)

        @block.tensor
        def _(pe):
            def turn(b, s, k):
                pe.wait_ge(aT_hi, b)
                pe.wait_ge(aT_lo, b)
                for hl in range(2):
                    for kd in range(KD):
                        for q in range(QT):
                            a = t.attn[:, hl, ds(b * QT + q, 1), kd * P:(kd + 1) * P]
                            mm = pe.transpose(ps_aT[:, hl, kd, q * P:(q + 1) * P],
                                              a.rearrange("p o n -> p (o n)"), t.ident16[:])
                mm.then_inc(aT_mm, 1)

            def product(b, s, k):
                pe.wait_ge(aT_hi, b + 1)
                pe.wait_ge(aT_lo, b + 1)
                for u in range(2):
                    pe.wait_ge(summed, b * 2)
                    for j in range(2):
                        n, q = 0, 2 * u + j
                        for wh, ah in ((0, 0), (1, 0), (0, 1)):
                            for kd in range(KD):
                                mm = pe.matmul(ps_y[:, u, j], aT[:, s, ah, kd, q * P:(q + 1) * P],
                                               t.w_proj[:, 4 * layer + 3, wh, kd, :], start=n == 0, stop=n == 5)
                                n += 1
                    mm.then_inc(y_mm, 1)

            def logits(b, s, k):
                pe.wait_ge(part_hi, b + 1)
                pe.wait_ge(part_lo, b + 1)
                pe.wait_ge(nT_hi, b)
                pe.wait_ge(nT_lo, b)
                for hl in range(2):
                    for kd in range(KD):
                        for q in range(QT):
                            mm = pe.transpose(ps_nT[:, hl, kd, q * P:(q + 1) * P],
                                              part[:, s, q, hl, kd * P:(kd + 1) * P], t.ident16[:])
                mm.then_inc(nT_mm, 1)
                pe.wait_ge(nT_hi, b + 1)
                pe.wait_ge(nT_lo, b + 1)
                pe.wait_ge(logits_out, b)
                for q in range(QT):
                    n = 0
                    for wh, nh in ((0, 0), (1, 0), (0, 1)):
                        for kd in range(KD):
                            mm = pe.matmul(ps_l[:, q], nT[:, nh, kd, q * P:(q + 1) * P], t.w_router[:, wh, kd, :],
                                           start=n == 0, stop=n == 5)
                            n += 1
                mm.then_inc(logits_mm, 1)

            pipeline(pe, turn, product, *([idle, idle, logits] if route else []))

        @block.scalar
        def _(act):
            def turned_high(b, s, k):
                act.wait_ge(aT_mm, b + 1)
                act.activation(aT[:, s, 0], ps_aT[:, 0], ACT.Copy).then_inc(aT_hi, 1)

            def squared_sums(b, s, k):
                for q in range(QT):
                    wait_x(act, b, q)
                    act.activation(squares[:, s, q], x_out[:, s, q], ACT.Square, scale=D ** -0.5,
                                   accum_out=ms[:, s, q:q + 1]).then_inc(squared, 1)

            def high_parts(b, s, k):
                act.wait_ge(stored[s], k * 32)
                if route:
                    act.wait_ge(nT_mm, before_last(b))
                    act.wait_ge(normed_out, b * QT + QT)
                    act.activation(part[:, s, :, 0], normed[:, s], ACT.Copy).then_inc(part_hi, 1)
                else:
                    act.wait_ge(rms_out, b + 1)
                    for q in range(QT):
                        act.activation(part[:, s, q, 0], x_out[:, s, q], ACT.Copy,
                                       scale=small[:, s, 3, q:q + 1]).then_inc(part_hi, 1)

            def logits(b, s, k):
                act.wait_ge(nT_mm, b + 1)
                act.activation(nT[:, 0], ps_nT[:, 0], ACT.Copy).then_inc(nT_hi, 1)

            pipeline(act, turned_high, idle, squared_sums, high_parts, *([logits] if route else []))

        @block.vector
        def _(vector):
            def turned_low(b, s, k):
                vector.wait_ge(aT_mm, b + 1)
                vector.tensor_copy(aT[:, s, 1], ps_aT[:, 1]).then_inc(aT_lo, 1)

            def residual(b, s, k):
                if norm:
                    vector.wait_ge(biased, b + 1)
                    vector.wait_ge(x_done, before_last(b) * QT)
                else:
                    vector.wait_ge(loaded[s], k * 16 + 16)
                    vector.wait_ge(added, before_last(b))
                    vector.wait_ge(squared, before_last(b) * QT)
                    vector.wait_ge(normed_out, before_last(b) * QT)
                for u in range(2):
                    vector.wait_ge(y_mm, b * 2 + u + 1)
                    vector.tensor_tensor(x_new[:, s, 2 * u:2 * u + 2], ps_y[:, u], x_res[:, s, 2 * u:2 * u + 2],
                                         ALU.add).then_inc(summed, 1)
                if not norm:
                    return
                for q in range(QT):
                    vector.wait_ge(summed, b * 2 + q // 2 + 1)
                    vector.bn_stats(stats[:, s, q], x_new[:, s, q]).then_inc(stat_out, 1)
                n = counted(vector, b * QT + QT)
                vector.wait_ge(stat_out, 1)
                vector.wait_ge(stat_out, n)
                for q in range(QT):
                    vector.bn_aggr(mean_var[:, s, q], stats[:, s, q]).then_inc(aggregated, 1)

            def norm_or_sum(b, s, k):
                if route:
                    vector.wait_ge(summed, b * 2 + 2)
                    vector.wait_ge(stored[s], k * 32)
                    vector.tensor_tensor(x_sum[:, s], x_out[:, s], x_res[:, s], ALU.add).then_inc(added, 1)
                else:
                    vector.wait_ge(rstd_out, b + 1)
                    vector.wait_ge(stored[s], k * 32)
                    for q in range(QT):
                        vector.tensor_scalar(x_out[:, s, q], x_new[:, s, q], mean_var[:, s, q, 0:1],
                                             small[:, s, 1, q:q + 1], ALU.subtract, ALU.mult).then_inc(x_done, 1)

            def parts(b, s, k):
                if route:
                    vector.wait_ge(rms_out, b + 1)
                    vector.wait_ge(part_lo, before_last(b))
                    for q in range(QT):
                        vector.scalar_tensor_tensor(normed[:, s, q], x_out[:, s, q], small[:, s, 3, q:q + 1],
                                                    t.g2[:, 0], ALU.mult, ALU.mult).then_inc(normed_out, 1)
                else:
                    for q in range(QT):
                        vector.wait_ge(part_hi, b * QT + q + 1)
                        vector.scalar_tensor_tensor(part[:, s, q, 1], x_out[:, s, q], small[:, s, 3, q:q + 1],
                                                    part[:, s, q, 0], ALU.mult, ALU.subtract).then_inc(part_lo, 1)

            def logits(b, s, k):
                vector.wait_ge(nT_mm, b + 1)
                vector.tensor_copy(nT[:, 1], ps_nT[:, 1]).then_inc(nT_lo, 1)
                vector.wait_ge(logits_mm, b + 1)
                vector.tensor_copy(t.logits[:, ds(b * QT, QT), :], ps_l[:]).then_inc(logits_out, 1)

            pipeline(vector, turned_low, residual, norm_or_sum, parts, *([logits] if route else []))


def load_experts(sync, t, experts):
    for e in experts:
        for hl in range(2):
            if e > 0:
                sync.wait_ge(t.up_loaded[hl], 48 * e)
            w_gate, w_up = (t.w_dram[kind][hl][e].rearrange("(k p) f -> p k f", p=P) for kind in range(2))
            for at, src in ((0, w_up), (F, w_gate[:, :, F - FR:F]), (F + FR, w_gate[:, :, 0:F - FR])):
                sync.dma_start(t.w_up[:, e, hl, :, at:at + src.shape[2]], src).then_inc(t.up_loaded[hl], 16)
        if e > 0:
            sync.wait_ge(t.down_loaded, 64 * e)
        for hl in range(2):
            down = t.w_dram[2][hl][e]
            sync.dma_start(t.w_down[:, e, hl, 0:FT - 1],
                           down[0:(FT - 1) * P].rearrange("(k p) n -> p k n", p=P)).then_inc(t.down_loaded, 16)
            sync.dma_start(t.w_down[0:FR, e, hl, FT - 1], down[(FT - 1) * P:F]).then_inc(t.down_loaded, 16)


def route_tokens(nc, t):
    with ExitStack() as ctx:
        sem = ctx.enter_context(stage_semaphores(nc, "r_"))
        sb = lambda n, s, d: ctx.enter_context(nc.sbuf_tensor("r_" + n, s, d))
        ps = lambda n, s, d: ctx.enter_context(nc.psum_tensor("r_" + n, s, d))
        rank = sb("rank", [P, NT, E], F32)
        best = sb("best", [P, 2, NT], F32)
        hit = sb("hit", [P, NT, E], F32)
        pick = sb("pick", [P, NT], F32)
        chosen = sb("chosen", [P, 2, NT, E], F32)
        left = sb("left", [P, NT, E], F32)
        both = sb("both", [P, NT, E], F32)
        gap, e_gap, one_more = sb("gap", [P, NT], F32), sb("e_gap", [P, NT], F32), sb("one_more", [P, NT], F32)
        earlier, ones = sb("earlier", [P, P], F32), sb("ones", [P, P], F32)
        totals = sb("totals", [P, E, NT], F32)
        keep = sb("keep", [P, E, NT], F32)
        run = sb("run", [P, E, NT], F32)
        count_i, padded_i = sb("count_i", [P, E], I32), sb("padded_i", [P, E], I32)
        padded, ends, starts = sb("padded", [P, E], F32), sb("ends", [P, E], F32), sb("starts", [P, E], F32)
        before, row = sb("before", [P, E, NT], F32), sb("row", [P, NT, E], F32)
        mine = sb("mine", [P, NT, E], F32)
        pos, pos_i = sb("pos", [P, 2, NT], F32), sb("pos_i", [P, 2, NT], I32)
        slot_i = sb("slot_i", [P, HI], I32)
        own = sb("own", [P, HI], F32)
        tile_start = sb("tile_start", [P, MT, 1], F32)
        passed, expert = sb("passed", [P, MT, E], F32), sb("expert", [P, MT], F32)
        hi_i, lo_i = sb("hi_i", [P, 2 * NT], I32), sb("lo_i", [P, 2 * NT], I32)
        hi, lo = sb("hi", [P, 2 * NT, 1], BF16), sb("lo", [P, 2 * NT, 1], BF16)
        count_hi, count_lo = sb("count_hi", [P, 1, HI], BF16), sb("count_lo", [P, 1, P], BF16)
        hot_hi = sb("hot_hi", [P, 2 * NT, HI], BF16)
        hot_lo = sb("hot_lo", [P, 2 * NT, P], BF16)
        by_tile = sb("by_tile", [P, 2 * NT, HI], BF16)
        by_row = hot_hi
        tile_no, row_no = sb("tile_no", [P, 2 * NT, 1], F32), sb("row_no", [P, 1], F32)
        inverse = sb("inverse", [P, P], F32)
        ps_c = ps("ps_c", [P, 2, NT * E], F32)
        ps_i = ps("ps_i", [P, 2, P], F32)
        ps_t = ps("ps_t", [P, P], F32)
        made, did, exp_done, totalled, hot_done, by_row_done, inverse_mm, turned = map(sem, (
            "made", "did", "exp_done", "totalled", "hot_done", "by_row_done", "inverse_mm", "turned"))
        hot_hi_done, by_tile_done, padded_out = map(sem, ("hot_hi_done", "by_tile_done", "weights_padded"))
        ready_gap, ready_both, ready_inverse = sem("ready_gap"), sem("ready_both"), sem("ready_inverse")
        block = ctx.enter_context(nc.Block())
        flat = lambda x: x.rearrange("p a b -> p (a b)")
        wide = lambda x, n: x.rearrange("p (a o) -> p a o", o=1).broadcast_to([P, x.shape[1], n])

        @block.gpsimd
        def _(pool):
            iota = lambda out, pattern, base, mult: pool.iota(
                out, pattern, base=base, channel_multiplier=mult,
                allow_small_or_imprecise_dtypes=True).then_inc(made, 1)
            iota(rank[:], [[0, NT], [-1, E]], E, 0)
            iota(tile_start[:], [[SLOT, MT]], 0, 0)
            iota(count_hi[:], [[1, HI]], 0, 0)
            iota(count_lo[:], [[1, P]], 0, 0)
            iota(tile_no[:], [[1, 2 * NT]], 1, 0)
            iota(row_no[:], [[0, 1]], 0, 1)
            iota(own[:], [[P, HI]], P - SPARE, 1)
            pool.memset(ones[:], 1.0).then_inc(made, 1)
            pool.memset(keep[:], 1.0).then_inc(made, 1)
            pool.wait_ge(made, 9)
            pool.affine_select(out=earlier[:], in_=ones[:], pattern=[[1, P]], compare_op=ALU.is_gt, fill=0.0,
                               base=0, channel_multiplier=-1).then_inc(made, 1)
            pool.memset(keep[:, :, 0:1], 0.0).then_inc(made, 1)
            pool.wait_ge(made, 11)
            pool.wait_ge(hot_hi_done, 1)
            pool.tensor_tensor(by_tile[:], hot_hi[:], tile_no[:].broadcast_to([P, 2 * NT, HI]),
                               ALU.mult).then_inc(by_tile_done, 1)

        MADE = 11

        @block.sync
        def _(sync):
            load_experts(sync, t, range(E // 2))

        @block.scalar
        def _(act):
            act.wait_ge(ready_gap, 1)
            act.activation(e_gap[:], gap[:], ACT.Exp).then_inc(exp_done, 1)
            act.wait_ge(by_tile_done, 1)
            act.activation(flat(by_row[:]), flat(hot_hi[:]), ACT.Copy, scale=row_no[:, 0:1]).then_inc(by_row_done, 1)

        @block.tensor
        def _(pe):
            pe.wait_ge(made, MADE)
            pe.wait_ge(ready_both, 1)
            pe.matmul(ps_c[:, 0], earlier[:], flat(both[:]), start=True, stop=True)
            pe.matmul(ps_c[:, 1], ones[:], flat(both[:]), start=True, stop=True,
                      skip_group_check=True).then_inc(totalled, 1)
            pe.wait_ge(hot_done, 1)
            pe.wait_ge(by_tile_done, 1)
            for v, values in enumerate((by_tile, by_row)):
                if v == 1:
                    pe.wait_ge(by_row_done, 1)
                for n in range(2 * NT):
                    mm = pe.matmul(ps_i[0:HI, v], values[:, n, :], hot_lo[:, n, :], start=n == 0,
                                   stop=n == 2 * NT - 1, skip_group_check=True)
            mm.then_inc(inverse_mm, 1)
            pe.wait_ge(ready_inverse, 1)
            pe.transpose(ps_t[:, 0:HI], inverse[0:HI, :], t.ident32[0:HI, 0:HI]).then_inc(turned, 1)

        @block.vector
        def _(vector):
            done = [0]

            def chained(ins):
                done[0] += 1
                ins.then_inc(did, 1)
                vector.wait_ge(did, done[0])

            vector.memset(t.w_down[FR:P, :, :, FT - 1].rearrange("p e h n -> p (e h) n"), 0.0).then_inc(padded_out, 1)
            vector.wait_ge(made, MADE)
            vector.wait_ge(padded_out, 1)
            source = t.logits
            for c in range(2):
                chained(vector.tensor_reduce(best[:, c], source[:], AX.X, ALU.max))
                chained(vector.tensor_tensor(hit[:], source[:], wide(best[:, c], E), ALU.is_equal))
                chained(vector.tensor_tensor(hit[:], hit[:], rank[:], ALU.mult))
                chained(vector.tensor_reduce(pick[:], hit[:], AX.X, ALU.max))
                chained(vector.tensor_tensor(chosen[:, c], rank[:], wide(pick[:], E), ALU.is_equal))
                if c == 0:
                    chained(vector.scalar_tensor_tensor(flat(left[:]), flat(chosen[:, 0]), NEG, flat(source[:]),
                                                        ALU.mult, ALU.add))
                    source = left
            vector.tensor_tensor(gap[:], best[:, 1], best[:, 0], ALU.subtract).then_inc(ready_gap, 1)
            vector.tensor_tensor(both[:], chosen[:, 0], chosen[:, 1], ALU.add).then_inc(ready_both, 1)
            vector.wait_ge(exp_done, 1)
            chained(vector.tensor_scalar(one_more[:], e_gap[:], 1.0, None, ALU.add))
            chained(vector.reciprocal(t.weight[:, 0], one_more[:]))
            chained(vector.tensor_tensor(t.weight[:, 1], t.weight[:, 0], e_gap[:], ALU.mult))
            vector.wait_ge(totalled, 1)
            per_expert = ps_c[:, 1].rearrange("p (k e) -> p e k", e=E)
            chained(vector.tensor_copy(totals[:], per_expert))
            chained(vector.tensor_tensor_scan(flat(run[:]), flat(keep[:]), flat(totals[:]), 0.0, ALU.mult, ALU.add))
            chained(vector.tensor_scalar(count_i[:], run[:, :, NT - 1], float(SLOT - 1), None, ALU.add))
            shift = SLOT.bit_length() - 1
            chained(vector.tensor_scalar(padded_i[:], count_i[:], shift, shift, ALU.logical_shift_right,
                                         ALU.logical_shift_left))
            chained(vector.tensor_copy(padded[:], padded_i[:]))
            chained(vector.tensor_tensor_scan(ends[:], ones[:, 0:E], padded[:], 0.0, ALU.mult, ALU.add))
            chained(vector.tensor_tensor(starts[:], ends[:], padded[:], ALU.subtract))
            chained(vector.tensor_tensor(before[:], run[:], totals[:], ALU.subtract))
            chained(vector.tensor_tensor(before[:], before[:], wide(starts[:], NT), ALU.add))
            chained(vector.tensor_tensor(row[:], ps_c[:, 0].rearrange("p (k e) -> p k e", e=E),
                                         before[:].rearrange("p e k -> p k e"), ALU.add))
            for c in range(2):
                chained(vector.tensor_tensor(mine[:], row[:], chosen[:, c], ALU.mult))
                chained(vector.tensor_reduce(pos[:, c], mine[:], AX.X, ALU.add))
            chained(vector.tensor_copy(pos_i[:], pos[:]))
            flat_pos = pos_i[:].rearrange("p c k -> p (c k)")
            chained(vector.tensor_scalar(lo_i[:], flat_pos, P - 1, None, ALU.bitwise_and))
            chained(vector.tensor_scalar(hi_i[:], flat_pos, 7, None, ALU.logical_shift_right))
            chained(vector.tensor_copy(hi[:, :, 0], hi_i[:]))
            vector.tensor_tensor(hot_hi[:], hi[:].broadcast_to([P, 2 * NT, HI]),
                                 count_hi[:].broadcast_to([P, 2 * NT, HI]), ALU.is_equal).then_inc(hot_hi_done, 1)
            chained(vector.tensor_copy(lo[:, :, 0], lo_i[:]))
            vector.tensor_tensor(hot_lo[:], lo[:].broadcast_to([P, 2 * NT, P]),
                                 count_lo[:].broadcast_to([P, 2 * NT, P]), ALU.is_equal).then_inc(hot_done, 1)
            chained(vector.tensor_tensor(passed[:], ends[:].rearrange("p (o e) -> p o e", o=1)
                                         .broadcast_to([P, MT, E]), tile_start[:].broadcast_to([P, MT, E]), ALU.is_le))
            chained(vector.tensor_reduce(expert[:], passed[:], AX.X, ALU.add))
            chained(vector.tensor_scalar(t.tile_expert[:], expert[:], float(E - 1), None, ALU.min))
            vector.wait_ge(inverse_mm, 1)
            chained(vector.tensor_copy(inverse[0:HI, :], ps_i[0:HI, 1]))
            vector.scalar_tensor_tensor(inverse[0:HI, :], ps_i[0:HI, 0], float(P), inverse[0:HI, :],
                                        ALU.mult, ALU.add).then_inc(ready_inverse, 1)
            vector.wait_ge(turned, 1)
            chained(vector.scalar_tensor_tensor(own[:], ps_t[:, 0:HI], 1.0, own[:], ALU.is_lt, ALU.mult))
            chained(vector.scalar_tensor_tensor(t.slot_of_row[:], ps_t[:, 0:HI], float(SPARE - P), own[:],
                                                ALU.add, ALU.add))
            chained(vector.tensor_scalar(slot_i[:], ps_t[:, 0:HI], float(2 * T - P), None, ALU.add))
            chained(vector.tensor_scalar(t.token_of_row[:], slot_i[:], T - 1, None, ALU.bitwise_and))


def expert_tiles(nc, t):
    with ExitStack() as ctx:
        sem = ctx.enter_context(stage_semaphores(nc, "e_"))
        pair = lambda n: [sem(f"{n}{i}") for i in range(2)]
        sb = lambda n, s, d: ctx.enter_context(nc.sbuf_tensor("e_" + n, s, d))
        ps = lambda n, s, d: ctx.enter_context(nc.psum_tensor("e_" + n, s, d))
        w_up, w_down = t.w_up, t.w_down
        x = sb("x", [P, 2, 2, 2 * D], F16)
        take, put = sb("take", [P, 2, 2], I32), sb("put", [P, 2, 2], I32)
        xT = sb("xT", [P, 2, 2, KD, SLOT], F16)
        gate = sb("gate", [P, 2, 2, SLOT], F32)
        h32 = sb("h32", [P, 2, 2, SLOT], F32)
        h = sb("h", [P, 2, 2, FT, SLOT], F16)
        y = sb("y", [P, 2, 2, D], F32)
        ps_xT = ps("ps_xT", [P, 2, KD, SLOT], F16)
        ps_gu = ps("ps_gu", [P, 2, 2, 2, SLOT], F32)
        ps_y = ps("ps_y", [P, 2, 2, D], F32)
        cleared, h_cleared, h_loaded = sem("indices_cleared"), sem("h_cleared"), sem("h_loaded")
        gathered, taken, placed, stored, xT_mm, xT_out, y_mm, y_out = map(pair, (
            "gathered", "taken", "placed", "stored", "xT_mm", "xT_out", "y_mm", "y_out"))
        gu_mm, gate_out, h_out, h_hi, h_lo = map(pair, ("gu_mm", "gate_out", "h_out", "h_hi", "h_lo"))
        block = ctx.enter_context(nc.Block())
        FG = FT // 2
        column = lambda f, kind: f * P if kind else F + FR + f * P
        LAST = MT // 2 - 1

        @block.sync
        def _(sync):
            for s in range(2):
                sync.wait_ge(gathered[s], 32)
            load_experts(sync, t, range(E // 2, E))
            sync.dma_start(t.h[:], t.h_dram.rearrange("(k p) n -> p k n", p=P)).then_inc(h_loaded, 16)
            sync.wait_ge(h_loaded, 16)
            for hl in range(2):
                sync.wait_ge(t.up_loaded[hl], 48 * E)
            sync.wait_ge(t.down_loaded, 64 * E)

        @block.gpsimd
        def _(pool):
            pool.memset(take[:], 0).then_inc(cleared, 1)
            pool.memset(put[:], 0).then_inc(cleared, 1)

            def gather(r, s):
                used, copied = counted(pool, r * 32), counted(pool, r + 1)
                pool.wait_ge(cleared, 2)
                pool.wait_ge(gathered[s], used)
                pool.tensor_copy(take[:, s], t.token_of_row[:, ds(r * 4 + 2 * s, 2)]).then_inc(taken[s], 1)
                pool.wait_ge(cleared, 2)
                pool.wait_ge(taken[s], copied)
                pool.wait_ge(xT_mm[s], r)
                for half in range(2):
                    pool.indirect_dma_start(x[:, s, half], None, t.part_dram,
                                            bass.IndirectOffsetOnAxis(ap=take[:, s, half:half + 1], axis=0)
                                            ).then_inc(gathered[s], 16)

            def scatter(r, s):
                used, copied = counted(pool, r * 32), counted(pool, r + 1)
                pool.wait_ge(cleared, 2)
                pool.wait_ge(stored[s], used)
                pool.tensor_copy(put[:, s], t.slot_of_row[:, ds(r * 4 + 2 * s, 2)]).then_inc(placed[s], 1)
                pool.wait_ge(cleared, 2)
                pool.wait_ge(placed[s], copied)
                pool.wait_ge(y_out[s], copied)
                for half in range(2):
                    pool.indirect_dma_start(t.y_dram, bass.IndirectOffsetOnAxis(ap=put[:, s, half:half + 1], axis=0),
                                            y[:, s, half], None).then_inc(stored[s], 16)

            for s in range(2):
                gather(0, s)
            with pool.Fori(0, LAST) as r:
                for s in range(2):
                    gather(r + 1, s)
                    scatter(r, s)
            gather(LAST + 1, 0)
            for r, s in ((LAST, 0), (LAST, 1), (LAST + 1, 0)):
                scatter(r, s)
            for s in range(2):
                pool.wait_ge(stored[s], 32 * (LAST + 2 - s))

        @block.tensor
        def _(pe):
            def turn(r, s):
                pe.wait_ge(gathered[s], r * 32 + 32)
                pe.wait_ge(xT_out[1 - s], r + s)
                for hl in range(2):
                    for k in range(KD):
                        for half in range(2):
                            mm = pe.transpose(ps_xT[:, hl, k, half * P:(half + 1) * P],
                                              x[:, s, half, hl * D + k * P:hl * D + (k + 1) * P], t.ident16[:])
                mm.then_inc(xT_mm[s], 1)

            def group(r, s, e, i):
                c = s * FG + i
                bank, turns = c % 2, r * FG + c // 2
                pe.wait_ge(h_out[bank], turns)
                for f in (2 * i, 2 * i + 1):
                    for kind in ((1,) if f == FT - 1 else (0, 1)):
                        n = 0
                        for wh, xh in ((0, 0), (0, 1), (1, 0)):
                            for k in range(KD):
                                w = w_up[:, :, wh, k, column(f, kind):column(f, kind) + P]
                                mm = pe.matmul(ps_gu[:, bank, kind, f % 2],
                                               w[:, ds(e, 1)].rearrange("p o f -> p (o f)"),
                                               xT[:, s, xh, k, :], start=n == 0, stop=n == 5)
                                n += 1
                mm.then_inc(gu_mm[bank], 1)

            def expert_of(r, s):
                return pe.value_load(t.tile_expert[0:1, ds(r * 2 + s, 1)], min_val=0, max_val=E - 1)

            def down(r, s):
                e = expert_of(r, s)
                pe.wait_ge(t.down_loaded, e * 64 + 64)
                pe.wait_ge(y_out[s], r)
                for half in range(2):
                    c = 0
                    for f in range(FT):
                        if half == 0 and f % 2 == 0:
                            g = s * FG + f // 2
                            pe.wait_ge(h_hi[g % 2], r * FG + (g // 2 + 1))
                            pe.wait_ge(h_lo[g % 2], r * FG + (g // 2 + 1))
                        for hh, wh in ((0, 0), (0, 1), (1, 0)):
                            w = w_down[:, :, wh, f, :]
                            mm = pe.matmul(ps_y[:, s, half], h[:, s, hh, f, half * P:(half + 1) * P],
                                           w[:, ds(e, 1)].rearrange("p o f -> p (o f)"),
                                           start=c == 0, stop=c == 3 * FT - 1)
                            c += 1
                mm.then_inc(y_mm[s], 1)

            def tile(r, s, before, following):
                e = expert_of(r, s)
                for hl in range(2):
                    pe.wait_ge(t.up_loaded[hl], e * 48 + 48)
                pe.wait_ge(xT_out[s], r + 1)
                group(r, s, e, 0)
                if before is not None:
                    down(*before)
                group(r, s, e, 1)
                if following is not None:
                    turn(*following)
                group(r, s, e, 2)

            pe.wait_ge(h_cleared, 1)
            turn(0, 0)
            tile(0, 0, None, (0, 1))
            with pe.Fori(0, LAST) as r:
                tile(r, 1, (r, 0), (r + 1, 0))
                tile(r + 1, 0, (r, 1), (r + 1, 1))
            tile(LAST, 1, (LAST, 0), (LAST + 1, 0))
            tile(LAST + 1, 0, (LAST, 1), None)
            down(LAST + 1, 0)

        @block.scalar
        def _(act):
            def move_x(r, s):
                act.wait_ge(xT_mm[s], r + 1)
                act.activation(xT[:, s], ps_xT[:], ACT.Copy).then_inc(xT_out[s], 1)

            def tile(r, s, following):
                for i in range(FG):
                    c = s * FG + i
                    bank, turns = c % 2, r * FG + (c // 2 + 1)
                    act.wait_ge(gu_mm[bank], turns)
                    if i < FG - 1:
                        act.activation(gate[:, bank], ps_gu[:, bank, 0], ACT.Silu).then_inc(gate_out[bank], 1)
                        if i == 1 and following is not None:
                            move_x(*following)
                        act.wait_ge(h_out[bank], turns)
                        act.activation(h[:, s, 0, 2 * i:2 * i + 2], h32[:, bank], ACT.Copy).then_inc(h_hi[bank], 1)
                    else:
                        act.activation(gate[:, bank, 0], ps_gu[:, bank, 0, 0], ACT.Silu)
                        act.activation(gate[0:FR, bank, 1], ps_gu[FR:2 * FR, bank, 1, 1],
                                       ACT.Silu).then_inc(gate_out[bank], 1)
                        act.wait_ge(h_out[bank], turns)
                        act.activation(h[:, s, 0, 2 * i], h32[:, bank, 0], ACT.Copy)
                        act.activation(h[0:FR, s, 0, 2 * i + 1], h32[0:FR, bank, 1], ACT.Copy).then_inc(h_hi[bank], 1)

            move_x(0, 0)
            tile(0, 0, (0, 1))
            with act.Fori(0, LAST) as r:
                tile(r, 1, (r + 1, 0))
                tile(r + 1, 0, (r + 1, 1))
            tile(LAST, 1, (LAST + 1, 0))
            tile(LAST + 1, 0, None)

        @block.vector
        def _(vector):
            def empty_y(r, s):
                vector.wait_ge(y_mm[s], r + 1)
                vector.wait_ge(stored[s], r * 32)
                vector.tensor_copy(y[:, s], ps_y[:, s]).then_inc(y_out[s], 1)

            def tile(r, s, before):
                for i in range(FG):
                    c = s * FG + i
                    bank, turns = c % 2, r * FG + c // 2
                    parts = [(P, slice(0, 2))] if i < FG - 1 else [(P, slice(0, 1)), (FR, slice(1, 2))]
                    vector.wait_ge(gate_out[bank], turns + 1)
                    vector.wait_ge(h_hi[bank], turns)
                    for rows, m in parts:
                        op = vector.tensor_tensor(h32[0:rows, bank, m], gate[0:rows, bank, m],
                                                  ps_gu[0:rows, bank, 1, m], ALU.mult)
                    op.then_inc(h_out[bank], 1)
                    vector.wait_ge(h_hi[bank], turns + 1)
                    for rows, m in parts:
                        f = slice(2 * i + m.start, 2 * i + m.stop)
                        op = vector.tensor_tensor(h[0:rows, s, 1, f], h32[0:rows, bank, m], h[0:rows, s, 0, f],
                                                  ALU.subtract)
                    op.then_inc(h_lo[bank], 1)
                    if i == 0 and before is not None:
                        empty_y(*before)

            vector.memset(h[FR:P, :, :, FT - 1], 0.0).then_inc(h_cleared, 1)
            tile(0, 0, None)
            with vector.Fori(0, LAST) as r:
                tile(r, 1, (r, 0))
                tile(r + 1, 0, (r, 1))
            tile(LAST, 1, (LAST, 0))
            tile(LAST + 1, 0, (LAST, 1))
            empty_y(LAST + 1, 0)


def combine(nc, t, out):
    with ExitStack() as ctx:
        sem = ctx.enter_context(stage_semaphores(nc, "c_"))
        pair = lambda n: [sem(f"{n}{i}") for i in range(2)]
        sb = lambda n, s, d: ctx.enter_context(nc.sbuf_tensor("c_" + n, s, d))
        rows = sb("rows", [P, 2, 2, QT, D], F32)
        z = sb("z", [P, 2, QT, D], F32)
        res = sb("res", [P, 2, QT, D], F32)
        stats, mean_var = sb("stats", [P, 2, QT, 6], F32), sb("mean_var", [P, 2, QT, 2], F32)
        small = sb("small", [P, 2, 4, QT], F32)
        constants = sb("constants", [P, 3, QT], F32)
        loaded, stored = pair("loaded"), pair("stored")
        first, summed, stat_out, aggregated, power, mid_out, rstd_out, shift_out, done = map(sem, (
            "first", "summed", "stat_out", "aggregated", "power", "mid_out", "rstd_out", "shift_out", "done"))
        block = ctx.enter_context(nc.Block())
        tiles = lambda x: x.rearrange("(k p) n -> p k n", p=P)
        idle = lambda b, s, k: None

        @block.sync
        def _(sync):
            def load(b, s, k):
                sync.wait_ge(summed, before_last(b) * QT)
                for c in range(2):
                    sync.dma_start(rows[:, s, c], tiles(t.y_dram)[:, ds(b * QT + (HI + c * NT), QT), :]
                                   ).then_inc(loaded[s], 16)

            def store(b, s, k):
                sync.wait_ge(done, b * QT + QT)
                sync.dma_start(tiles(out)[:, ds(b * QT, QT), :], res[:, s]).then_inc(stored[s], 16)

            pipeline(sync, load, idle, idle, store)
            for s in range(2):
                sync.wait_ge(stored[s], 16 * (B // 2))

        @block.gpsimd
        def _(pool):
            for i, value in enumerate((-0.5, LN_EPS, -1.0)):
                pool.memset(constants[:, i], value).then_inc(power, 1)
            pool.wait_ge(power, 3)

            def deviation(b, s, k):
                pool.wait_ge(aggregated, b * QT + QT)
                pool.wait_ge(done, before_last(b) * QT)
                mean, var = mean_var[:, s, :, 0], mean_var[:, s, :, 1]
                pool.tensor_tensor(small[:, s, 0], var, constants[:, 1], ALU.add).then_inc(mid_out, 1)
                pool.tensor_tensor(small[:, s, 2], mean, constants[:, 2], ALU.mult).then_inc(mid_out, 1)
                pool.wait_ge(mid_out, b * 2 + 2)
                pool.tensor_tensor(small[:, s, 1], small[:, s, 0], constants[:, 0], ALU.pow).then_inc(rstd_out, 1)
                pool.wait_ge(rstd_out, b + 1)
                pool.tensor_tensor(small[:, s, 3], small[:, s, 2], small[:, s, 1], ALU.mult).then_inc(shift_out, 1)

            pipeline(pool, deviation, idle)

        @block.vector
        def _(vector):
            def weigh(b, s, k):
                vector.wait_ge(loaded[s], k * 32 + 32)
                vector.wait_ge(done, before_last(b) * QT)
                for c, ready in enumerate((first, summed)):
                    for q in range(QT):
                        w = t.weight[:, :, ds(b * QT + q, 1)]
                        if c == 1:
                            vector.wait_ge(first, b * QT + (q + 1))
                        h = t.h[:, ds(b * QT + q, 1), :].rearrange("p o n -> p (o n)")
                        vector.scalar_tensor_tensor(z[:, s, q] if c else rows[:, s, 0, q], rows[:, s, c, q],
                                                    w[:, c], rows[:, s, 0, q] if c else h,
                                                    ALU.mult, ALU.add).then_inc(ready, 1)
                for q in range(QT):
                    vector.wait_ge(summed, b * QT + (q + 1))
                    vector.bn_stats(stats[:, s, q], z[:, s, q]).then_inc(stat_out, 1)
                n = counted(vector, b * QT + QT)
                vector.wait_ge(stat_out, 1)
                vector.wait_ge(stat_out, n)
                for q in range(QT):
                    vector.bn_aggr(mean_var[:, s, q], stats[:, s, q]).then_inc(aggregated, 1)

            pipeline(vector, weigh, idle)

        @block.scalar
        def _(act):
            def normalise(b, s, k):
                act.wait_ge(rstd_out, b + 1)
                act.wait_ge(shift_out, b + 1)
                act.wait_ge(stored[s], k * 16)
                for q in range(QT):
                    act.activation(res[:, s, q], z[:, s, q], ACT.Identity, bias=small[:, s, 3, q:q + 1],
                                   scale=small[:, s, 1, q:q + 1]).then_inc(done, 1)

            pipeline(act, idle, normalise)


def feed_forward_kernel(nc, a, out):
    with ExitStack() as top:
        dram = lambda n, s, d: nc.dram_tensor(n, s, d).ap()
        sb = lambda n, s, d: top.enter_context(nc.sbuf_tensor(n, s, d))
        t = Tensors()
        t.qk_dram = [dram(f"qk_{hl}", [P, 4, T], F16) for hl in ("hi", "lo")]
        t.v_dram, x1_dram, t.h_dram = dram("v", [T, D], F32), dram("x1", [T, D], F32), dram("h", [T, D], F32)
        t.part_dram = dram("part", [T, 2 * D], F16)
        t.y_dram = dram("y", [SPARE + 2 * T, D], F32)
        t.w_dram = [[dram(f"w_{name}_{hl}", [E, *shape], F16) for hl in ("hi", "lo")]
                    for name, shape in (("gate", (D, F)), ("up", (D, F)), ("down", (F, D)))]
        t.ident32, t.ident16 = sb("ident32", [P, P], F32), sb("ident16", [P, P], F16)
        t.logits, t.weight = sb("logits", [P, NT, E], F32), sb("weight", [P, 2, NT], F32)
        t.token_of_row, t.slot_of_row = sb("token_of_row", [P, HI], I32), sb("slot_of_row", [P, HI], I32)
        t.tile_expert = sb("tile_expert", [P, MT], I32)
        with ExitStack() as ctx:
            attention_tensors(nc, ctx, t)
            row = lambda x: x.rearrange("(o n) -> o n", o=1).broadcast_to([P, x.shape[0]])
            setup(nc, t, [a["A_W" + k] for k in "qkvo"] + [a["F_w" + k] for k in "qkvo"], a["w_router"],
                  [(t.bq[:], a["bq"]), (t.g1[:], a["g1"]), (t.bk[:], a["bk"]), (t.g2[:, 0], row(a["g2"])),
                   (t.bv2[:, 0], row(a["bv"])), (t.bv2[:, 1], row(a["bv"])), (t.bo[:], row(a["bo"])),
                   (t.head_mask[:], row(a["head_mask"])), (t.cos[:], a["cos"]), (t.sin[:], a["sin"])])
            project_qkv(nc, t, 0, lambda b: a["xT"].rearrange("(k p) n -> p k n", p=P)[:, :, ds(b * S, S)])
            attend(nc, t, 0, (a["wg"], a["wu"], a["wd"]))
            project_out(nc, t, 0, a["x"], x1_dram, t.part_dram)
            project_qkv(nc, t, 1, lambda b: t.part_dram.rearrange("(k p) n -> p k n", p=P)[:, ds(b * QT, QT), :])
            attend(nc, t, 1)
            project_out(nc, t, 1, x1_dram, t.h_dram, t.part_dram)
        with ExitStack() as ctx:
            sem = ctx.enter_context(stage_semaphores(nc, "w_"))
            t.up_loaded, t.down_loaded = [sem(f"up_loaded{hl}") for hl in range(2)], sem("down_loaded")
            t.w_up = ctx.enter_context(nc.sbuf_tensor("w_up", [P, E, 2, KD, 2 * F], F16))
            t.w_down = ctx.enter_context(nc.sbuf_tensor("w_down", [P, E, 2, FT, D], F16))
            route_tokens(nc, t)
            t.h = ctx.enter_context(nc.sbuf_tensor("h_all", [P, NT, D], F32))
            expert_tiles(nc, t)
            combine(nc, t, out)


def kernel(**inputs):
    import concourse.bacc as bacc
    from concourse.bass_utils import run_bass_kernel_spmd

    given = {k: np.asarray(v) for k, v in inputs.items()}
    columns = lambda x: np.ascontiguousarray(x.reshape(KD, P).T)
    arrays = {"x": given["L0_attn_x"].reshape(T, D)}
    arrays["xT"] = np.ascontiguousarray(arrays["x"].T)
    for k in "qkvo":
        arrays["A_W" + k] = np.ascontiguousarray(given["L0_attn_W" + k].T)
        arrays["F_w" + k] = given["L0_ffn_w" + k]
    for k in ("bv", "bo", "head_mask"):
        arrays[k] = given["L0_attn_" + k]
    for k in ("w_router", "wg", "wu", "wd"):
        arrays[k] = given["L0_ffn_" + k]
    arrays["bq"], arrays["bk"] = columns(given["L0_attn_bq"]), columns(given["L0_attn_bk"])
    arrays["g1"], arrays["g2"] = columns(given["L0_ffn_g1"]), given["L0_ffn_g2"]
    inv_freq = 1.0 / 10000.0 ** (np.arange(0, DH, 2, dtype=np.float32) / DH)
    angle = np.einsum("i,j->ij", np.arange(S, dtype=np.float32), inv_freq)
    angle = np.tile(np.concatenate([angle, angle], axis=-1), (1, P // DH)).T
    arrays["cos"] = np.ascontiguousarray(np.cos(angle), np.float32)
    arrays["sin"] = np.ascontiguousarray(np.sin(angle), np.float32)
    nc = bacc.Bacc("TRN2", target_bir_lowering=False, num_devices=1)
    a = {n: nc.dram_tensor("in_" + n, v.shape, mybir.dt.from_np(v.dtype), kind="ExternalInput").ap()
         for n, v in arrays.items()}
    out = nc.dram_tensor("out", [T, D], F32, kind="ExternalOutput").ap()
    feed_forward_kernel(nc, a, out)
    r = run_bass_kernel_spmd(nc, [{"in_" + n: v for n, v in arrays.items()}], core_ids=[0])
    return np.asarray(r.results[0]["out"]).reshape(B, S, D)
```
